# Optimizing a Trainium2 kernel written in Bass

```python
import numpy as np
import jax
import jax.numpy as jnp

def _softmax(x, axis=-1):
    return jax.nn.softmax(x, axis=axis)

def _gelu(x):
    return jax.nn.gelu(x, approximate=True)

def _silu(x):
    return jax.nn.silu(x)

def _sigmoid(x):
    return jax.nn.sigmoid(x)

def _layernorm(x, axis=-1, eps=1e-05):
    m = jnp.mean(x, axis=axis, keepdims=True)
    v = jnp.var(x, axis=axis, keepdims=True)
    return (x - m) / jnp.sqrt(v + eps)

def _scatter_add(tgt, idx, src, axis=0):
    return tgt.at[idx].add(src)

def _segment_sum(src, seg, n):
    return jax.ops.segment_sum(src, seg, n)
kernel_name = 'mk_adaln_d2_jaxref_r8_62101a'

def setup_inputs(seed: int=0):
    np.random.seed(seed)
    _w = jnp.asarray

    def _L0_attn_setup():
        import jax, jax.numpy as jnp
        import numpy as np
        B, N, H = (1, 512, 256)
        NH, HD = (16, H // 16)
        WINDOW = 512
        EPS = 1e-06
        THETA = 10000.0
        NEG = -1e+30

        def rmsnorm(x, w):
            var = jnp.mean(jnp.square(x.astype(jnp.float32)), axis=-1, keepdims=True)
            return (x * jax.lax.rsqrt(var + EPS)).astype(w.dtype) * w

        def rotate_half(x):
            x1, x2 = (x[..., :x.shape[-1] // 2], x[..., x.shape[-1] // 2:])
            return jnp.concatenate((-x2, x1), axis=-1)
        key = jax.random.key(seed)
        k1, k2, k3 = jax.random.split(key, 3)
        x = jax.random.normal(k1, (B, N, H), dtype=jnp.float32)
        w_qkv = jax.random.normal(k2, (H, 3 * H), dtype=jnp.float32) * (1.0 / np.sqrt(H))
        w_out = jax.random.normal(k3, (H, H), dtype=jnp.float32) * (1.0 / np.sqrt(H))
        q_gamma = jnp.ones((HD,), dtype=jnp.float32)
        k_gamma = jnp.ones((HD,), dtype=jnp.float32)
        return {'x': x, 'w_qkv': w_qkv, 'w_out': w_out, 'q_gamma': q_gamma, 'k_gamma': k_gamma}
    _L0_attn_in = _L0_attn_setup()

    def _L0_ffn_setup():
        import jax, jax.numpy as jnp
        import numpy as np

        def _sparsify_2to4(h):
            B, S, I = h.shape
            g = h.reshape(B, S, I // 4, 4)
            a = jnp.abs(g)
            _, idx = jax.lax.top_k(a, 2)
            pos = jnp.arange(4)
            mask = (pos == idx[..., 0:1]) | (pos == idx[..., 1:2])
            return (g * mask.astype(g.dtype)).reshape(B, S, I)
        key = jax.random.key(seed)
        k1, k2, k3, k4 = jax.random.split(key, 4)
        B, S, H, I = (4, 256, 256, 1024)
        x = jax.random.normal(k1, (B, S, H), dtype=jnp.float32)
        w_gate = jax.random.normal(k2, (H, I), dtype=jnp.float32) / np.sqrt(H)
        w_up = jax.random.normal(k3, (H, I), dtype=jnp.float32) / np.sqrt(H)
        w_down = jax.random.normal(k4, (I, H), dtype=jnp.float32) / np.sqrt(I)
        return {'x': x, 'w_gate': w_gate, 'w_up': w_up, 'w_down': w_down}
    _L0_ffn_in = _L0_ffn_setup()
    _L0_c = _w((lambda *s: np.random.randn(*s).astype(np.float32) * 0.05)(2, 256))
    _L0_wmod = _w((lambda *s: np.random.randn(*s).astype(np.float32) * 0.05)(256, 6 * 256) * 256 ** (-0.5))

    def _L1_attn_setup():
        import jax, jax.numpy as jnp
        import numpy as np
        D_MODEL = 256
        EXPAND = 2
        INNER = EXPAND * D_MODEL
        HEADDIM = 64
        NHEADS = INNER // HEADDIM
        D_CONV = 4
        BATCH, SEQLEN = (2, 512)

        def _dw_causal_conv_silu(x, w, b):
            K = w.shape[1]
            L = x.shape[1]
            xp = jnp.pad(x, ((0, 0), (K - 1, 0), (0, 0)))
            y = b
            for k in range(K):
                y = y + w[:, k] * xp[:, k:k + L, :]
            return jax.nn.silu(y)

        def _diag_ssm_scan(a, u):

            def comb(c1, c2):
                a1, b1 = c1
                a2, b2 = c2
                return (a1 * a2, a2 * b1 + b2)
            _, s = jax.lax.associative_scan(comb, (a, u), axis=1)
            return s
        key = jax.random.key(seed)
        ks = jax.random.split(key, 12)
        f32 = jnp.float32
        return {'hidden_states': jax.random.normal(ks[0], (BATCH, SEQLEN, D_MODEL), f32), 'in_proj_w': jax.random.normal(ks[1], (INNER, D_MODEL), f32) * 0.02, 'gate_proj_w': jax.random.normal(ks[2], (INNER, D_MODEL), f32) * 0.02, 'out_proj_w': jax.random.normal(ks[3], (D_MODEL, INNER), f32) * 0.02, 'conv_weight': jax.random.normal(ks[4], (INNER, D_CONV), f32) * 0.02, 'conv_bias': jnp.zeros((INNER,), f32), 'dt_w': jax.random.normal(ks[5], (NHEADS, HEADDIM), f32) * 0.02, 'dt_b': jnp.zeros((NHEADS,), f32), 'A_log': jax.random.normal(ks[6], (NHEADS, HEADDIM), f32) * 0.1, 'B': jax.random.normal(ks[7], (NHEADS, HEADDIM), f32) * 0.02, 'C': jax.random.normal(ks[8], (NHEADS, HEADDIM), f32) * 0.02, 'D': jnp.ones((NHEADS, HEADDIM), f32)}
    _L1_attn_in = _L1_attn_setup()

    def _L1_ffn_setup():
        import jax, jax.numpy as jnp
        import numpy as np
        B, S, D, H = (4, 256, 256, 1024)

        def fwht(x):
            orig_shape = x.shape
            n = orig_shape[-1]
            x = x.reshape(-1, n)
            h = 1
            while h < n:
                xb = x.reshape(-1, n // (2 * h), 2, h)
                a = xb[:, :, 0, :]
                b = xb[:, :, 1, :]
                x = jnp.stack([a + b, a - b], axis=2).reshape(-1, n)
                h *= 2
            scale = jnp.asarray(1.0 / np.sqrt(n), dtype=x.dtype)
            return (x * scale).reshape(orig_shape)
        key = jax.random.key(seed)
        kx, k1, k2, k3 = jax.random.split(key, 4)
        x = jax.random.normal(kx, (B, S, D), dtype=jnp.float32)
        W1 = jax.random.normal(k1, (H, D), dtype=jnp.float32) * (1.0 / np.sqrt(D))
        W2 = jax.random.normal(k2, (D, H), dtype=jnp.float32) * (1.0 / np.sqrt(H))
        W3 = jax.random.normal(k3, (H, D), dtype=jnp.float32) * (1.0 / np.sqrt(D))
        return {'x': x, 'W1': W1, 'W2': W2, 'W3': W3}
    _L1_ffn_in = _L1_ffn_setup()
    _L1_c = _w((lambda *s: np.random.randn(*s).astype(np.float32) * 0.05)(2, 256))
    _L1_wmod = _w((lambda *s: np.random.randn(*s).astype(np.float32) * 0.05)(256, 6 * 256) * 256 ** (-0.5))
    _d = {'L0_attn_x': _L0_attn_in['x'], 'L0_attn_w_qkv': _L0_attn_in['w_qkv'], 'L0_attn_w_out': _L0_attn_in['w_out'], 'L0_attn_q_gamma': _L0_attn_in['q_gamma'], 'L0_attn_k_gamma': _L0_attn_in['k_gamma'], 'L0_ffn_w_gate': _L0_ffn_in['w_gate'], 'L0_ffn_w_up': _L0_ffn_in['w_up'], 'L0_ffn_w_down': _L0_ffn_in['w_down'], 'L0_c': _L0_c, 'L0_wmod': _L0_wmod, 'L1_attn_in_proj_w': _L1_attn_in['in_proj_w'], 'L1_attn_gate_proj_w': _L1_attn_in['gate_proj_w'], 'L1_attn_out_proj_w': _L1_attn_in['out_proj_w'], 'L1_attn_conv_weight': _L1_attn_in['conv_weight'], 'L1_attn_conv_bias': _L1_attn_in['conv_bias'], 'L1_attn_dt_w': _L1_attn_in['dt_w'], 'L1_attn_dt_b': _L1_attn_in['dt_b'], 'L1_attn_A_log': _L1_attn_in['A_log'], 'L1_attn_B': _L1_attn_in['B'], 'L1_attn_C': _L1_attn_in['C'], 'L1_attn_D': _L1_attn_in['D'], 'L1_ffn_W1': _L1_ffn_in['W1'], 'L1_ffn_W2': _L1_ffn_in['W2'], 'L1_ffn_W3': _L1_ffn_in['W3'], 'L1_c': _L1_c, 'L1_wmod': _L1_wmod}
    _x0 = _d['L0_attn_x']
    _d['L0_attn_x'] = jax.random.normal(jax.random.fold_in(jax.random.key(seed), 1), (2, 512, 256), dtype=_x0.dtype)
    del _x0
    return _d

def reference(L0_attn_x, L0_attn_w_qkv, L0_attn_w_out, L0_attn_q_gamma, L0_attn_k_gamma, L0_ffn_w_gate, L0_ffn_w_up, L0_ffn_w_down, L0_c, L0_wmod, L1_attn_in_proj_w, L1_attn_gate_proj_w, L1_attn_out_proj_w, L1_attn_conv_weight, L1_attn_conv_bias, L1_attn_dt_w, L1_attn_dt_b, L1_attn_A_log, L1_attn_B, L1_attn_C, L1_attn_D, L1_ffn_W1, L1_ffn_W2, L1_ffn_W3, L1_c, L1_wmod):

    def _L0_attn_ref(x, w_qkv, w_out, q_gamma, k_gamma):
        import jax, jax.numpy as jnp
        import numpy as np
        B, N, H = (1, 512, 256)
        NH, HD = (16, H // 16)
        WINDOW = 512
        EPS = 1e-06
        THETA = 10000.0
        NEG = -1e+30

        def rmsnorm(x, w):
            var = jnp.mean(jnp.square(x.astype(jnp.float32)), axis=-1, keepdims=True)
            return (x * jax.lax.rsqrt(var + EPS)).astype(w.dtype) * w

        def rotate_half(x):
            x1, x2 = (x[..., :x.shape[-1] // 2], x[..., x.shape[-1] // 2:])
            return jnp.concatenate((-x2, x1), axis=-1)
        b, n, _ = x.shape
        qkv = jnp.einsum('bnh,hm->bnm', x, w_qkv)
        q, k, v = jnp.split(qkv, 3, axis=-1)
        q = q.reshape(b, n, NH, HD).transpose(0, 2, 1, 3)
        k = k.reshape(b, n, NH, HD).transpose(0, 2, 1, 3)
        v = v.reshape(b, n, NH, HD).transpose(0, 2, 1, 3)
        q = rmsnorm(q, q_gamma)
        k = rmsnorm(k, k_gamma)
        inv_freq = 1.0 / THETA ** (jnp.arange(0, HD, 2, dtype=jnp.float32) / HD)
        t = jnp.arange(n, dtype=jnp.float32)
        freqs = t[:, None] * inv_freq[None, :]
        emb = jnp.concatenate((freqs, freqs), axis=-1)
        cos = jnp.cos(emb)[None, None, :, :]
        sin = jnp.sin(emb)[None, None, :, :]
        q = q * cos + rotate_half(q) * sin
        k = k * cos + rotate_half(k) * sin
        kv_len = k.shape[-2]
        q_idx = jnp.arange(n)[:, None] + (kv_len - n)
        k_idx = jnp.arange(kv_len)[None, :]
        mask = (q_idx >= k_idx) & (q_idx - k_idx <= WINDOW)
        scores = jnp.einsum('bhqd,bhkd->bhqk', q, k) / np.sqrt(HD)
        scores = jnp.where(mask[None, None, :, :], scores, NEG)
        attn = jax.nn.softmax(scores, axis=-1)
        out = jnp.einsum('bhqk,bhkd->bhqd', attn, v)
        out = out.transpose(0, 2, 1, 3).reshape(b, n, H)
        return jnp.einsum('bnh,hm->bnm', out, w_out)

    def _L0_ffn_ref(x, w_gate, w_up, w_down):
        import jax, jax.numpy as jnp
        import numpy as np

        def _sparsify_2to4(h):
            B, S, I = h.shape
            g = h.reshape(B, S, I // 4, 4)
            a = jnp.abs(g)
            _, idx = jax.lax.top_k(a, 2)
            pos = jnp.arange(4)
            mask = (pos == idx[..., 0:1]) | (pos == idx[..., 1:2])
            return (g * mask.astype(g.dtype)).reshape(B, S, I)
        h = jax.nn.silu(jnp.einsum('bsh,hi->bsi', x, w_gate)) * jnp.einsum('bsh,hi->bsi', x, w_up)
        h_sparse = _sparsify_2to4(h)
        return jnp.einsum('bsi,ih->bsh', h_sparse, w_down)

    def _L1_attn_ref(hidden_states, in_proj_w, gate_proj_w, out_proj_w, conv_weight, conv_bias, dt_w, dt_b, A_log, B, C, D):
        import jax, jax.numpy as jnp
        import numpy as np
        D_MODEL = 256
        EXPAND = 2
        INNER = EXPAND * D_MODEL
        HEADDIM = 64
        NHEADS = INNER // HEADDIM
        D_CONV = 4
        BATCH, SEQLEN = (2, 512)

        def _dw_causal_conv_silu(x, w, b):
            K = w.shape[1]
            L = x.shape[1]
            xp = jnp.pad(x, ((0, 0), (K - 1, 0), (0, 0)))
            y = b
            for k in range(K):
                y = y + w[:, k] * xp[:, k:k + L, :]
            return jax.nn.silu(y)

        def _diag_ssm_scan(a, u):

            def comb(c1, c2):
                a1, b1 = c1
                a2, b2 = c2
                return (a1 * a2, a2 * b1 + b2)
            _, s = jax.lax.associative_scan(comb, (a, u), axis=1)
            return s
        batch, seqlen, _ = hidden_states.shape
        projected = jnp.einsum('bld,cd->blc', hidden_states, in_proj_w)
        conv_out = _dw_causal_conv_silu(projected, conv_weight, conv_bias)
        gate = jax.nn.sigmoid(jnp.einsum('bld,cd->blc', hidden_states, gate_proj_w))
        X = conv_out.reshape(batch, seqlen, NHEADS, HEADDIM)
        dt = jax.nn.softplus(jnp.einsum('blhp,hp->blh', X, dt_w) + dt_b)
        A = -jnp.exp(A_log)
        a = jnp.exp(dt[..., None] * A)
        u = dt[..., None] * B * X
        s = _diag_ssm_scan(a, u)
        y = C * s + D * X
        combined = y.reshape(batch, seqlen, INNER) * gate
        return jnp.einsum('blc,dc->bld', combined, out_proj_w)

    def _L1_ffn_ref(x, W1, W2, W3):
        import jax, jax.numpy as jnp
        import numpy as np
        B, S, D, H = (4, 256, 256, 1024)

        def fwht(x):
            orig_shape = x.shape
            n = orig_shape[-1]
            x = x.reshape(-1, n)
            h = 1
            while h < n:
                xb = x.reshape(-1, n // (2 * h), 2, h)
                a = xb[:, :, 0, :]
                b = xb[:, :, 1, :]
                x = jnp.stack([a + b, a - b], axis=2).reshape(-1, n)
                h *= 2
            scale = jnp.asarray(1.0 / np.sqrt(n), dtype=x.dtype)
            return (x * scale).reshape(orig_shape)
        up_gate = jnp.einsum('bsd,hd->bsh', x, W1)
        up_lin = jnp.einsum('bsd,hd->bsh', x, W3)
        hidden = jax.nn.silu(up_gate) * up_lin
        hidden = fwht(hidden)
        out = jnp.einsum('bsh,dh->bsd', hidden, W2)
        return out
    x = L0_attn_x
    mod = (_silu(L0_c) @ L0_wmod).reshape(L0_c.shape[0], 6, 1, -1)
    sa, ca, ga, sb, cb, gb = (mod[:, 0], mod[:, 1], mod[:, 2], mod[:, 3], mod[:, 4], mod[:, 5])
    ga = (2 * (ga >= 0) - 1) * jnp.maximum(jnp.abs(ga), 0.25)
    gb = (2 * (gb >= 0) - 1) * jnp.maximum(jnp.abs(gb), 0.25)
    h = _layernorm(x, axis=-1) * (1 + ca) + sa
    x = x + ga * _L0_attn_ref(h, L0_attn_w_qkv, L0_attn_w_out, L0_attn_q_gamma, L0_attn_k_gamma)
    h = _layernorm(x, axis=-1) * (1 + cb) + sb
    x = x + gb * _L0_ffn_ref(h, L0_ffn_w_gate, L0_ffn_w_up, L0_ffn_w_down)
    mod = (_silu(L1_c) @ L1_wmod).reshape(L1_c.shape[0], 6, 1, -1)
    sa, ca, ga, sb, cb, gb = (mod[:, 0], mod[:, 1], mod[:, 2], mod[:, 3], mod[:, 4], mod[:, 5])
    ga = (2 * (ga >= 0) - 1) * jnp.maximum(jnp.abs(ga), 0.25)
    gb = (2 * (gb >= 0) - 1) * jnp.maximum(jnp.abs(gb), 0.25)
    h = _layernorm(x, axis=-1) * (1 + ca) + sa
    x = x + ga * _L1_attn_ref(h, L1_attn_in_proj_w, L1_attn_gate_proj_w, L1_attn_out_proj_w, L1_attn_conv_weight, L1_attn_conv_bias, L1_attn_dt_w, L1_attn_dt_b, L1_attn_A_log, L1_attn_B, L1_attn_C, L1_attn_D)
    h = _layernorm(x, axis=-1) * (1 + cb) + sb
    x = x + gb * _L1_ffn_ref(h, L1_ffn_W1, L1_ffn_W2, L1_ffn_W3)
    return x

_drawn_inputs = setup_inputs


def setup_inputs(seed=0):
    import zlib

    import numpy as np

    out = dict(_drawn_inputs(seed))
    spreads = {'L0_attn_q_gamma': (1.0, 0.6),
     'L0_attn_k_gamma': (1.0, 0.6),
     'L1_attn_conv_bias': (0.0, 0.8),
     'L1_attn_dt_b': (0.0, 2.0),
     'L1_attn_D': (1.0, 0.6)}
    factors = {'L1_attn_in_proj_w': 8.0,
     'L1_attn_gate_proj_w': 8.0,
     'L1_attn_out_proj_w': 8.0,
     'L1_attn_conv_weight': 8.0,
     'L1_attn_dt_w': 61.002,
     'L1_attn_A_log': 59.428,
     'L1_attn_B': 8.0,
     'L1_attn_C': 23.961,
     'L1_ffn_W1': 6.378,
     'L1_ffn_W2': 5.926,
     'L1_ffn_W3': 6.154}
    for name, (base, spread) in spreads.items():
        noise = np.random.default_rng([zlib.crc32(name.encode()), seed]).standard_normal(out[name].shape)
        drawn = base * np.exp(spread * noise) if base else spread * noise
        out[name] = jnp.asarray(drawn.astype(out[name].dtype))
    for name, factor in factors.items():
        out[name] = (out[name] * factor).astype(out[name].dtype)
    return out
```

```python
from contextlib import ExitStack

import numpy as np

import concourse.bass as bass
from concourse import mybir

F32 = mybir.dt.float32
R32 = mybir.dt.float32r
BF16 = mybir.dt.bfloat16
ALU = mybir.AluOpType
ACT = mybir.ActivationFunctionType
AX = mybir.AxisListType

P = 128
NB, SEQ, D = 2, 512, 256
TT = SEQ // P
DC = D // P
NH, HD = 16, 16
HALF = HD // 2
HID = 1024
FC = HID // P
GB = FC // 4
INNER = 512
KC = INNER // P
SH, SHD = 8, 64
TAPS = 4
SLOT = 64
SHIFT = 3 * HD
HPG = 4
NG = NB * NH // HPG
GPB = NH // HPG
RING = 7
LN_EPS, RMS_EPS = 1e-5, 1e-6
LOWEST = -3.0e38
NEG = -1.0e30

C_ID = 0
C_HAD = C_ID + P
C_SEL = C_HAD + P
C_MASK = C_SEL + KC * P
C_COS = C_MASK + SEQ
C_SIN = C_COS + TT * HD
C_END = C_SIN + TT * HD
S_CONV, S_BIAS, S_ALOG, S_B, S_C, S_D, S_END = 0, 4, 5, 6, 7, 8, 9


def attention_steps(g):
    steps = []
    if g >= 0:
        steps.append(("maxT", g))
    maxes = [("mx", g + 1, h, t) for h in range(HPG) for t in range(TT)] if g + 1 < NG else []
    if g + 1 < NG:
        steps.append(("T", g + 1))
    if g < 0:
        return steps + maxes
    if g >= 1:
        steps.append(("oN", g - 1))
    steps += maxes[:4]
    maxes = maxes[4:]
    scores = [("st", g, s, i) for s, n in ((0, 4), (1, 4), (2, 2)) for i in range(n)]
    for i, sc in enumerate(scores):
        steps.append(sc)
        if i == 5:
            steps.append(("pv", g, 0))
        if i == 9:
            steps.append(("pv", g, 1))
        take = (len(maxes) + (9 - i)) // (10 - i)
        steps += maxes[:take]
        maxes = maxes[take:]
    steps.append(("pv", g, 2))
    return steps


def plan():
    s = [("ln", 0, 0), ("mod", 0), ("qkv", 0, 0), ("qkv", 0, 1), ("qkv", 0, 2), ("qkv", 0, 3), ("mod", 1), ("ln", 0, 1)]
    for g in range(-1, NG):
        s += attention_steps(g)
        if g == 2:
            s += [("qkv", 1, t) for t in range(TT)]
        if g == GPB:
            s += [("aT", 0), ("y", 0, 0)]
    s += [("oN", NG - 1), ("aT", 1), ("ln", 1, 0)]
    s += [("gu", 1, 0, f) for f in range(FC)]
    s += [("y", 0, 1), ("ln", 1, 1)]
    s += [("gu", 1, 1, f) for f in range(FC)]
    s += [("y", 1, 0), ("ln", 2, 0)]
    s += [("proj", 0), ("y", 1, 1), ("ln", 2, 1), ("dt", 0), ("proj", 1), ("spread", 0), ("dt", 1), ("had",), ("y", 2, 0)]
    s += [("ln", 3, 0), ("spread", 1)]
    s += [("gu", 3, 0, f) for f in range(FC)]
    s += [("y", 2, 1), ("ln", 3, 1)]
    s += [("gu", 3, 1, f) for f in range(FC)]
    s += [("y", 3, 0), ("y", 3, 1)]
    return s


def products(stage):
    k = stage[0]
    if k == "ln":
        return [("ln", stage[1], stage[2], c) for c in range(DC)]
    if k == "mod":
        return [("modT", stage[1])] + [("modG", stage[1], b) for b in range(NB)]
    if k == "qkv":
        return [("qk",) + stage[1:], ("v",) + stage[1:]]
    if k == "T":
        return [(n, stage[1], j) for j in range(2) for n in ("qT", "kT")]
    if k in ("mx", "st", "maxT", "oN", "dt"):
        return [stage]
    if k == "pv":
        return []
    if k == "aT":
        return [("aT", stage[1], c) for c in range(DC)]
    if k == "y":
        return [stage + (i,) for i in range(TT // 2)]
    if k == "gu":
        return [("gate",) + stage[1:], ("up",) + stage[1:]]
    if k == "proj":
        return [(n, stage[1], c) for c in range(KC) for n in ("pj", "gt")]
    if k == "spread":
        return [("spread", stage[1], c) for c in range(KC)]
    if k == "had":
        return [("had", i) for i in range(FC // 2)]
    raise ValueError(stage)


def adaln_blocks(nc, x, wqkv, wout, gammas, wgu0, wdn0, wmod, cT, wproj, woutp, chan, dtw, dtb, wgu1, w2t, consts, out):
    stages = plan()
    place = {}
    for s in stages:
        for u in products(s):
            place[u] = (len(place) % RING, len(place) // RING)

    with ExitStack() as ctx:
        cursor = [(nc.sbuf_base + 31) // 32 * 32]

        def at(name, shape, dt=F32):
            n = int(np.prod(shape[1:])) * (2 if dt == BF16 else 4)
            t = nc.alloc_sbuf_tensor_at(name, shape, dt, offset=cursor[0])
            cursor[0] += (n + 31) // 32 * 32
            return t

        cst = at("cst", [P, C_END])
        sel = at("sel", [P, KC, P], R32)
        rope_c = at("rope_c", [P, TT, 2, HD])
        rope_s = at("rope_s", [P, TT, 2, HD])
        gam = at("gam", [P, 2, HD])
        ch = at("ch", [P, KC, S_END])
        neg_a = at("neg_a", [P, KC])
        dtw_s = at("dtw_s", [P, KC, SH])
        dtb_s = at("dtb_s", [SH, 1])
        c_s = at("c_s", [P, 2, DC, NB])
        silu_c = at("silu_c", [P, 2, DC, NB])
        modT = at("modT", [P, 2, 4, DC, NB])
        gates = at("gates", [P, 2, 2, NB, D])
        mhalf = at("mhalf", [P, 2 * NH])
        stats = at("stats", [P, TT, 6])
        mv = at("mv", [P, TT, 2])
        ln_ve = at("ln_ve", [P, TT])
        ln_rs = at("ln_rs", [P, TT])
        qk_ss = at("qk_ss", [P, 2 * NH])
        qk_ve = at("qk_ve", [P, 2, 2 * NH])
        qk_rs = at("qk_rs", [P, 2, 2 * NH])
        X = at("X", [P, NB * TT, D])
        h_hi = at("h_hi", [P, NB, DC, SEQ], R32)
        h_lo = at("h_lo", [P, NB, DC, SEQ], R32)
        wout_s = at("wout_s", [P, DC, D])
        wq_hi = at("wq_hi", [P, DC, 3 * D], R32)
        wq_lo = at("wq_lo", [P, DC, 3 * D], R32)
        w2b_at = cursor[0] - 2 * DC * 3 * D * 4
        stage = at("stage", [P, 2, 2, 2, DC, P])
        gua_at = cursor[0]
        gua_hi = at("gua_hi", [P, FC // 2, 2, DC, P], R32)
        gua_lo = at("gua_lo", [P, FC // 2, 2, DC, P], R32)
        xn = at("xn", [P, TT, D])
        hf = at("hf", [P, DC, SEQ])
        area = cursor[0]

        qkp = at("qkp", [P, TT, 2, NH, SLOT], R32)
        QT = at("QT", [P, 2, 2, SEQ], R32)
        KT = at("KT", [P, 2, 2, 2, SEQ], R32)
        vp = at("vp", [P, NB, TT, NH, 32])
        sqt = at("sqt", [P, 2, 2, NH, HD])
        qn = at("qn", [P, 2, 2, NH, HD])
        rr = at("rr", [P, 2, 2, NH, HD])
        early = cursor[0]
        PTa = at("PTa", [P, HPG, SEQ])
        PTb = at("PTb", [P, HPG, SEQ])
        PTc = at("PTc", [P, HPG, SEQ // 2])
        oT = at("oT", [P, SEQ])
        junk = at("junk", [P, 3, SEQ], BF16)
        mx = at("mx", [P, 2, TT, HPG])
        negm = at("negm", [HPG, SEQ], R32)
        rc = at("rc", [P, TT, HPG])
        att = at("att", [P, TT, D])
        aT = at("aT", [P, DC, SEQ])
        cursor[0] = early
        wmod_s = at("wmod_s", [P, 2, DC, 6 * D])
        g_abs = at("g_abs", [P, 2, D])
        g_neg = at("g_neg", [P, 2, D])
        g_sgn = at("g_sgn", [P, 2, D])
        silu_cb = at("silu_cb", [P, 2, DC, NB, P])
        cursor[0] = gua_at
        wq_raw = at("wq_raw", [P, DC, 3 * D])

        cursor[0] = area
        gub_hi = at("gub_hi", [P, FC // 2, 2, DC, P], R32)
        gub_lo = at("gub_lo", [P, FC // 2, 2, DC, P], R32)
        pj_hi = at("pj_hi", [P, KC, 2, DC, P], R32)
        pj_lo = at("pj_lo", [P, KC, 2, DC, P], R32)
        wdn_s = at("wdn_s", [P, FC, D])
        woutp_s = at("woutp_s", [P, KC, D])
        w2a = at("w2a", [P, FC, D])
        hidden_at = cursor[0]
        H = at("H", [P, NB, FC, SEQ])
        sg = at("sg", [P, 2, SEQ])
        ab = at("ab", [P, 4, SEQ])
        pair_hi = at("pair_hi", [P, 2, SEQ])
        pair_lo = at("pair_lo", [P, 2, SEQ])
        odd_wins = at("odd_wins", [P, 2, SEQ], BF16)
        both = at("both", [P, 2, SEQ], BF16)
        lean = at("lean", [P, SEQ], BF16)
        d_sub = at("d_sub", [P, 2, SEQ], BF16)
        d_add = at("d_add", [P, 2, SEQ], BF16)
        yt = at("yt", [P, 2, D])
        w2b = nc.alloc_sbuf_tensor_at("w2b", [P, FC, D], F32, offset=w2b_at)
        xc = [nc.alloc_sbuf_tensor_at(f"xc{b}", [P, KC, SEQ], F32, offset=hidden_at + b * FC * SEQ * 4) for b in range(NB)]
        gt = [nc.alloc_sbuf_tensor_at(f"gt{b}", [P, KC, SEQ], F32, offset=hidden_at + b * FC * SEQ * 4 + KC * SEQ * 4) for b in range(NB)]
        cursor[0] = hidden_at + NB * FC * SEQ * 4
        acc = at("acc", [P, 2, SEQ])
        decay = at("decay", [P, 2, SEQ])
        drive = at("drive", [P, SEQ])
        state = at("state", [P, SEQ])
        skip = at("skip", [P, 2, SEQ])
        yv = at("yv", [P, 2, SEQ])
        dts = at("dts", [P, SEQ], R32)
        sp_z = at("sp_z", [SH, SEQ])
        sp_a = at("sp_a", [SH, SEQ])
        sp_e = at("sp_e", [SH, SEQ])
        sp_l = at("sp_l", [SH, SEQ])
        sp_u = at("sp_u", [SH, SEQ])
        sp_c = at("sp_c", [SH, SEQ])

        ident = cst[:, C_ID:C_ID + P]
        had = cst[:, C_HAD:C_HAD + P]
        mask = cst[:, C_MASK:C_MASK + SEQ]
        cosv = cst[:, C_COS:C_SIN].rearrange("p (t d) -> p t d", t=TT)
        sinv = cst[:, C_SIN:C_END].rearrange("p (t d) -> p t d", t=TT)
        PT = [PTa, PTb, PTc]

        bank = [ctx.enter_context(nc.psum_tensor(f"bank{i}", [P, SEQ], F32)) for i in range(RING)]
        pv_bank = ctx.enter_context(nc.psum_tensor("pv_bank", [P, SEQ], F32))

        def sem(name):
            return ctx.enter_context(nc.semaphore(name))

        bank_full = [sem(f"bank_full{i}") for i in range(RING)]
        bank_free = [sem(f"bank_free{i}") for i in range(RING)]
        x_in = [sem(f"x_in{b}") for b in range(NB)]
        wq_in, cst_in, wout_in = sem("wq_in"), sem("cst_in"), sem("wout_in")
        wmod_in = [sem("wmod_in0"), sem("wmod_in1")]
        c_in, gam_in, chan_in = sem("c_in"), sem("gam_in"), sem("chan_in")
        stage_in = [sem("stage_in0"), sem("stage_in1")]
        wdn_in, woutp_in, w2_in = sem("wdn_in"), sem("woutp_in"), sem("w2_in")
        shift_in = [sem("shift_in0"), sem("shift_in1")]
        out_done = sem("out_done")
        pool_consts, pool_chain, dve_chain, act_chain = sem("pool_consts"), sem("pool_chain"), sem("dve_chain"), sem("act_chain")
        silu_c_done, silu_cb_done, mod_done = sem("silu_c_done"), sem("silu_cb_done"), sem("mod_done")
        wq_split_hi, wq_split = sem("wq_split_hi"), sem("wq_split")
        stage_split = sem("stage_split")
        ln_var, ln_rstd, xn_done, h_done = sem("ln_var"), sem("ln_rstd"), sem("xn_done"), sem("h_done")
        sq_done, rms_var, rms_rstd, cos_done, roped, qk_high, qk_split = (
            sem(n) for n in ("sq_done", "rms_var", "rms_rstd", "cos_done", "roped", "qk_high", "qk_split"))
        qT_out, kT_out_dve, kT_out_act = sem("qT_out"), sem("kT_out_dve"), sem("kT_out_act")
        causal_done, pv_done, pv_free = (
            sem(n) for n in ("causal_done", "pv_done", "pv_free"))
        abs_done, abs_used, sparse_done, x_done = sem("abs_done"), sem("abs_used"), sem("sparse_done"), sem("x_done")
        conv_begun, xc_done = sem("conv_begun"), sem("xc_done")
        sp_e_done, sp_l_done, dts_done = sem("sp_e_done"), sem("sp_l_done"), sem("dts_done")
        decay_done, skip_done, y_done, comb_done = (
            sem("decay_done"), sem("skip_done"), sem("y_done"), sem("comb_done"))
        w2_mixed = sem("w2_mixed")
        sel_done, rope_done = sem("sel_done"), sem("rope_done")

        def ps(u):
            return bank[place[u][0]]

        def claim(eng, u):
            if place[u][1]:
                eng.wait_ge(bank_free[place[u][0]], place[u][1])

        def filled(eng, u):
            eng.wait_ge(bank_full[place[u][0]], place[u][1] + 1)

        def read(eng, u):
            eng.wait_ge(bank_free[place[u][0]], place[u][1] + 1)

        def h_used(eng, n, b):
            filled(eng, (("v", b, TT - 1), ("up", 1, b, FC - 1), ("gt", b, KC - 1))[n])

        def fill(ins, u):
            ins.then_inc(bank_full[place[u][0]], 1)

        def free(ins, u):
            ins.then_inc(bank_free[place[u][0]], 1)

        block = ctx.enter_context(nc.Block())
        NCONST = 6

        @block.sync
        def _(sp):
            xv = x.rearrange("(b t p) d -> b p t d", b=NB, p=P)
            ov = out.rearrange("(b t p) d -> b p t d", b=NB, p=P)
            sp.dma_start(X[:, 0:TT, :], xv[0]).then_inc(x_in[0], 16)
            sp.dma_start(c_s[:], cT).then_inc(c_in, 16)
            sp.dma_start(cst[:], consts).then_inc(cst_in, 16)
            sp.dma_start(wmod_s[:, 0], wmod[:, 0]).then_inc(wmod_in[0], 16)
            sp.dma_start(wq_raw[:], wqkv).then_inc(wq_in, 16)
            sp.dma_start(gam[:], gammas).then_inc(gam_in, 16)
            sp.dma_start(wmod_s[:, 1], wmod[:, 1]).then_inc(wmod_in[1], 16)
            sp.dma_start(X[:, TT:2 * TT, :], xv[1]).then_inc(x_in[1], 16)
            sp.dma_start(ch[:], chan).then_inc(chan_in, 16)
            sp.dma_start(dtw_s[:], dtw).then_inc(chan_in, 16)
            sp.dma_start(dtb_s[:], dtb).then_inc(chan_in, 16)
            sp.dma_start(wout_s[:], wout).then_inc(wout_in, 16)

            def stage_load(i):
                src = wgu0[:, 2 * i:2 * i + 2] if i < 4 else wproj[:, 2 * (i - 4):2 * (i - 4) + 2] if i < 6 else wgu1[:, 2 * (i - 6):2 * (i - 6) + 2]
                if i >= 2:
                    sp.wait_ge(stage_split, i - 1)
                sp.dma_start(stage[:, i % 2], src).then_inc(stage_in[i % 2], 16)

            for i in range(4):
                stage_load(i)
            for g in range(NG):
                read(sp, ("maxT", g))
                for h in range(HPG):
                    row = SHIFT + SLOT * (h % 2)
                    sp.dma_start(QT[row:row + 1, g % 2, h // 2, :].bitcast(F32), negm[h:h + 1, :].bitcast(F32)).then_inc(shift_in[g % 2], 16)
            stage_load(4)
            stage_load(5)
            filled(sp, ("st", NG - 1, 2, 1))
            sp.dma_start(wdn_s[:], wdn0).then_inc(wdn_in, 16)
            sp.wait_ge(x_done, 4)
            sp.dma_start(woutp_s[:], woutp).then_inc(woutp_in, 16)
            sp.dma_start(w2a[:], w2t).then_inc(w2_in, 16)
            for i in range(6, 10):
                stage_load(i)
            for b in range(NB):
                for i in range(TT // 2):
                    sp.wait_ge(x_done, 2 * (2 * 3 + b) + i + 1)
                    sp.dma_start(ov[b][:, 2 * i:2 * i + 2, :], X[:, TT * b + 2 * i:TT * b + 2 * i + 2, :]).then_inc(out_done, 16)
            sp.wait_ge(out_done, 16 * TT)

        @block.gpsimd
        def _(pool):
            g = nc.gpsimd
            chain = [0]

            def link(ins):
                chain[0] += 1
                ins.then_inc(pool_chain, 1)
                pool.wait_ge(pool_chain, chain[0])

            def ln_pow(i):
                pool.wait_ge(ln_var, i + 1)
                g.tensor_tensor(ln_rs[:], ln_ve[:], mhalf[:, 0:TT], ALU.pow).then_inc(ln_rstd, 1)

            def rms_pow(n):
                pool.wait_ge(rms_var, n + 1)
                g.tensor_tensor(qk_rs[:, n % 2], qk_ve[:, n % 2], mhalf[:], ALU.pow).then_inc(rms_rstd, 1)

            def rope(n):
                t, s = n % TT, n % 2
                read(pool, ("qk", n // TT, t))
                if n == 0:
                    pool.wait_ge(rope_done, 1)
                for lo, hi in ((0, HALF), (HALF, 0)):
                    tab = rope_s[:, t, :, lo:lo + HALF].unsqueeze(2).broadcast_to([P, 2, NH, HALF])
                    last = g.tensor_tensor(sqt[:, s, :, :, lo:lo + HALF], qn[:, s, :, :, hi:hi + HALF], tab, ALU.mult)
                link(last)
                pool.wait_ge(cos_done, n + 1)
                g.tensor_tensor(rr[:, s], rr[:, s], sqt[:, s], ALU.add).then_inc(roped, 1)

            def split_stage(i):
                half = stage[:, i % 2]
                if i < 4 or i >= 6:
                    j = i % 4 if i < 4 else i - 6
                    hi_t, lo_t = (gua_hi, gua_lo) if j < 2 else (gub_hi, gub_lo)
                    j = j % 2
                else:
                    hi_t, lo_t, j = pj_hi, pj_lo, i - 4
                pool.wait_ge(stage_in[i % 2], 16 * (i // 2 + 1))
                link(g.tensor_copy(hi_t[:, 2 * j:2 * j + 2], half))
                g.tensor_tensor(lo_t[:, 2 * j:2 * j + 2], half, hi_t[:, 2 * j:2 * j + 2].bitcast(F32), ALU.subtract).then_inc(stage_split, 1)

            def causal(gr, s, i):
                read(pool, ("st", gr, s, i))
                if s == 0:
                    v = PTa[:, i, 0:P].unsqueeze(1)
                elif s == 1:
                    v = PTb[:, i, :].rearrange("p (c k) -> p c k", k=P)[:, 0:4:3, :]
                else:
                    v = PTc[:, 2 * i:2 * i + 2, 0:P]
                g.affine_select(out=v, in_=v, compare_op=ALU.is_ge, fill=0.0, base=0,
                                pattern=[[0, v.shape[1]], [1, P]], channel_multiplier=-1).then_inc(causal_done, 1)

            def comb(b, k):
                n = KC * b + k
                pool.wait_ge(y_done, n + 1)
                read(pool, ("gt", b, k))
                g.tensor_tensor(gt[b][:, k], yv[:, k % 2], gt[b][:, k], ALU.mult).then_inc(comb_done, 1)

            g.memset(mhalf[:], -0.5).then_inc(pool_consts, 1)
            g.memset(vp[:, :, :, :, HD:32], 0.0).then_inc(pool_consts, 1)
            g.memset(qkp[:, :, :, :, SHIFT:SLOT].bitcast(F32), 0.0).then_inc(pool_consts, 1)
            g.memset(KT[:].bitcast(F32), 0.0).then_inc(pool_consts, 1)
            pool.wait_ge(pool_consts, 4)
            g.memset(vp[:, :, :, :, HD:HD + 1], 1.0).then_inc(pool_consts, 1)
            g.memset(qkp[:, :, 1, :, SHIFT:SHIFT + 1].bitcast(F32), 1.0).then_inc(pool_consts, 1)
            ln_pow(0)
            for n in range(TT + 1):
                if n < TT:
                    rms_pow(n)
                if n >= 1:
                    rope(n - 1)
            ln_pow(1)
            pool.wait_ge(wq_split, 1)
            split_stage(0)
            split_stage(1)
            for gr in range(NG):
                for s, n in ((0, 4), (1, 4), (2, 2)):
                    for i in range(n):
                        causal(gr, s, i)
                if gr == 2:
                    for n in range(TT, 2 * TT + 1):
                        if n < 2 * TT:
                            rms_pow(n)
                        if n > TT:
                            rope(n - 1)
                if gr == NG - 2:
                    for j in range(2):
                        filled(pool, ("kT", NG - 1, j))
                    split_stage(2)
                    split_stage(3)
            ln_pow(2)
            split_stage(4)
            split_stage(5)
            ln_pow(3)
            ln_pow(4)
            ln_pow(5)
            pool.wait_ge(w2_in, 16)
            src, dst = w2a, w2b
            for r in range(3):
                s = 1 << r
                a = src[:].rearrange("p (m two s) d -> p m two (s d)", two=2, s=s)
                z = dst[:].rearrange("p (m two s) d -> p m two (s d)", two=2, s=s)
                g.tensor_tensor(z[:, :, 0], a[:, :, 0], a[:, :, 1], ALU.add)
                last = g.tensor_tensor(z[:, :, 1], a[:, :, 0], a[:, :, 1], ALU.subtract)
                if r < 2:
                    link(last)
                else:
                    last.then_inc(w2_mixed, 1)
                src, dst = dst, src
            for k in range(KC):
                comb(0, k)
            h_used(pool, 1, 1)
            split_stage(6)
            ln_pow(6)
            split_stage(7)
            for k in range(KC):
                comb(1, k)
            split_stage(8)
            split_stage(9)
            ln_pow(7)

        @block.scalar
        def _(act):
            a = nc.scalar
            chain = [0]

            def link(ins):
                chain[0] += 1
                ins.then_inc(act_chain, 1)
                act.wait_ge(act_chain, chain[0])

            def ln(n, b):
                i, l, k = 2 * n + b, n // 2, 2 * (n % 2)
                if n == 0 and b == 0:
                    act.wait_ge(mod_done, 1)
                if n == 2 and b == 0:
                    act.wait_ge(mod_done, 2)
                if i:
                    act.wait_ge(h_done, i)
                if n:
                    h_used(act, n - 1, b)
                for c in range(DC):
                    u = ("ln", n, b, c)
                    filled(act, u)
                    sh, sc = modT[:, l, k, c, b:b + 1], modT[:, l, k + 1, c, b:b + 1]
                    a.activation(hf[:, c], ps(u)[:], ACT.Identity, bias=sh, scale=sc)
                    free(a.activation(h_hi[:, b, c], ps(u)[:], ACT.Identity, bias=sh, scale=sc), u)

            def qkv_in(n):
                b, t = n // TT, n % TT
                u, v = ("qk", b, t), ("v", b, t)
                filled(act, u)
                if n >= 2:
                    act.wait_ge(roped, n - 1)
                a.activation(sqt[:, n % 2].rearrange("p a h d -> p (a h d)"), ps(u)[:], ACT.Square).then_inc(sq_done, 1)
                filled(act, v)
                if n == 0:
                    act.wait_ge(pool_consts, NCONST)
                free(a.copy(vp[:, b, t, :, 0:HD], ps(v)[:, 0:D].rearrange("p (h d) -> p h d", d=HD)), v)

            def qk_hi(n):
                t = n % TT
                act.wait_ge(roped, n + 1)
                if n == TT:
                    for j in range(2):
                        filled(act, ("kT", GPB - 1, j))
                a.copy(qkp[:, t, :, :, 0:HD], rr[:, n % 2])
                a.copy(qkp[:, t, 0, :, 2 * HD:3 * HD], rr[:, n % 2, 0])
                a.copy(qkp[:, t, 1, :, HD:2 * HD], rr[:, n % 2, 1]).then_inc(qk_high, 1)

            def heads_out(gr):
                if gr >= 2:
                    act.wait_ge(pv_done, 3 * (gr - 1))
                for j in range(2):
                    u = ("qT", gr, j)
                    filled(act, u)
                    free(a.copy(QT[:, gr % 2, j], ps(u)[:]), u)
                u = ("kT", gr, 1)
                filled(act, u)
                a.copy(KT[0:SLOT, gr % 2, 1, 0], ps(u)[0:SLOT])
                free(a.copy(KT[SLOT:P, gr % 2, 1, 1], ps(u)[SLOT:P]), u)

            def exps(gr):
                for s, n in ((0, 4), (1, 4), (2, 2)):
                    if gr:
                        act.wait_ge(pv_done, 3 * (gr - 1) + s + 1)
                    for i in range(n):
                        u = ("st", gr, s, i)
                        filled(act, u)
                        if s < 2:
                            dst, src = PT[s][:, i], ps(u)[:]
                        else:
                            dst, src = PTc[:, 2 * i:2 * i + 2], ps(u)[:].rearrange("p (h q) -> p h q", h=2)
                        free(a.activation(dst, src, ACT.Exp), u)

            def aT_out(b):
                if b:
                    filled(act, ("y", 0, b - 1, 1))
                for c in range(DC):
                    u = ("aT", b, c)
                    filled(act, u)
                    free(a.copy(aT[:, c], ps(u)[:]), u)

            def gu(n, b, f):
                u = ("gate", n, b, f)
                filled(act, u)
                prev = f - 2 + FC * b
                if prev >= 0:
                    read(act, ("up", n, prev // FC, prev % FC))
                free(a.activation(sg[:, f % 2], ps(u)[:], ACT.Silu), u)

            def absolute(b, gb):
                n = GB * b + gb
                read(act, ("up", 1, b, 4 * gb + 3))
                if n:
                    act.wait_ge(abs_used, n)
                a.activation(ab[:], H[:, b, 4 * gb:4 * gb + 4], ACT.Abs).then_inc(abs_done, 1)

            def proj(b):
                if b == 0:
                    act.wait_ge(chan_in, 48)
                filled(act, ("y", 1, b, 1))
                for k in range(KC):
                    n = KC * b + k
                    u = ("pj", b, k)
                    filled(act, u)
                    if n >= 2:
                        act.wait_ge(xc_done, n - 1)
                    a.activation(acc[:, k % 2], ps(u)[:], ACT.Identity, bias=ch[:, k, S_BIAS:S_BIAS + 1],
                                 scale=ch[:, k, S_CONV + TAPS - 1:S_CONV + TAPS]).then_inc(conv_begun, 1)
                    if k:
                        conv_out(b, k - 1)
                conv_out(b, KC - 1)
                for k in range(KC):
                    u = ("gt", b, k)
                    filled(act, u)
                    free(a.activation(gt[b][:, k], ps(u)[:], ACT.Sigmoid), u)

            def conv_out(b, k):
                read(act, ("pj", b, k))
                a.activation(xc[b][:, k], acc[:, k % 2], ACT.Silu).then_inc(xc_done, 1)

            def softplus(b):
                u = ("dt", b)
                filled(act, u)
                if b:
                    act.wait_ge(dts_done, b)
                a.activation(sp_z[:], ps(u)[0:SH], ACT.Identity, bias=dtb_s[:, 0:1])
                last = a.activation(sp_a[:], ps(u)[0:SH], ACT.Abs, bias=dtb_s[:, 0:1])
                free(last, u)
                read(act, u)
                a.activation(sp_e[:], sp_a[:], ACT.Exp, scale=-1.0).then_inc(sp_e_done, 1)
                act.wait_ge(sp_e_done, b + 1)
                a.activation(sp_l[:], sp_e[:], ACT.Ln, bias=1.0).then_inc(sp_l_done, 1)

            def spread(b):
                if b == 0:
                    link(a.activation(neg_a[:], ch[:, :, S_ALOG], ACT.Exp))
                    link(a.mul(neg_a[:], neg_a[:], -1.0))
                for k in range(KC):
                    n = KC * b + k
                    u = ("spread", b, k)
                    filled(act, u)
                    if n >= 2:
                        act.wait_ge(y_done, n - 1)
                    a.activation(decay[:, k % 2], ps(u)[:], ACT.Exp, scale=neg_a[:, k:k + 1]).then_inc(decay_done, 1)
                    a.activation(skip[:, k % 2], xc[b][:, k], ACT.Copy, scale=ch[:, k, S_D:S_D + 1]).then_inc(skip_done, 1)

            act.wait_ge(c_in, 16)
            a.activation(silu_c[:], c_s[:], ACT.Silu).then_inc(silu_c_done, 1)
            act.wait_ge(wq_in, 16)
            a.copy(wq_hi[:], wq_raw[:]).then_inc(wq_split_hi, 1)
            ln(0, 0)
            for n in range(TT + 2):
                if n < TT:
                    qkv_in(n)
                if n >= 2:
                    qk_hi(n - 2)
            ln(0, 1)
            heads_out(0)
            for gr in range(NG):
                if gr + 1 < NG:
                    heads_out(gr + 1)
                exps(gr)
                if gr == 2:
                    for n in range(TT, 2 * TT + 2):
                        if n < 2 * TT:
                            qkv_in(n)
                        if n >= TT + 2:
                            qk_hi(n - 2)
                if gr == GPB:
                    aT_out(0)
            aT_out(1)
            ln(1, 0)
            for b in range(NB):
                for f in range(FC):
                    gu(1, b, f)
                    if f % 4 == 1 and (b or f > 1):
                        n = GB * b + f // 4 - 1
                        absolute(n // GB, n % GB)
                    if b == 0 and f == FC - 1:
                        ln(1, 1)
            absolute(1, 1)
            ln(2, 0)
            proj(0)
            ln(2, 1)
            softplus(0)
            proj(1)
            spread(0)
            softplus(1)
            for i in range(FC // 2):
                u = ("had", i)
                filled(act, u)
                free(a.mul(w2a[:, 2 * i:2 * i + 2], ps(u)[:].rearrange("p (c d) -> p c d", c=2), 1.0 / HID ** 0.5), u)
            ln(3, 0)
            spread(1)
            for b in range(NB):
                for f in range(FC):
                    gu(3, b, f)
                if b == 0:
                    ln(3, 1)

        @block.vector
        def _(dve):
            v = nc.vector
            chain = [0]

            def link(ins):
                chain[0] += 1
                ins.then_inc(dve_chain, 1)
                dve.wait_ge(dve_chain, chain[0])

            def ln_stats(n, b):
                i = 2 * n + b
                if n == 0:
                    dve.wait_ge(x_in[b], 16)
                if i:
                    dve.wait_ge(xn_done, i)
                for t in range(TT):
                    last = v.bn_stats(stats[:, t], X[:, TT * b + t])
                link(last)
                for t in range(TT):
                    last = v.bn_aggr(mv[:, t], stats[:, t])
                link(last)
                v.tensor_scalar(ln_ve[:], mv[:, :, 1], LN_EPS, None, ALU.add).then_inc(ln_var, 1)
                if i:
                    filled(dve, ("ln", (i - 1) // 2, (i - 1) % 2, DC - 1))
                dve.wait_ge(ln_rstd, i + 1)
                for t in range(TT):
                    last = v.tensor_scalar(xn[:, t], X[:, TT * b + t], mv[:, t, 0:1], ln_rs[:, t:t + 1], ALU.subtract, ALU.mult)
                last.then_inc(xn_done, 1)

            def ln_lo(n, b):
                i = 2 * n + b
                read(dve, ("ln", n, b, DC - 1))
                v.tensor_tensor(h_lo[:, b], hf[:], h_hi[:, b].bitcast(F32), ALU.subtract).then_inc(h_done, 1)

            def mod_out(l):
                u = ("modT", l)
                filled(dve, u)
                if l:
                    dve.wait_ge(mod_done, l)
                m = ps(u)[:, 0:16].rearrange("p (k c b) -> p k c b", k=4, c=DC)
                v.tensor_copy(modT[:, l, 0:4:2], m[:, 0:4:2])
                free(v.tensor_scalar(modT[:, l, 1:4:2], m[:, 1:4:2], 1.0, None, ALU.add), u)
                for b in range(NB):
                    u = ("modG", l, b)
                    filled(dve, u)
                    gv = ps(u)[:].rearrange("p (k d) -> p k d", k=2)
                    v.tensor_scalar(g_abs[:], gv, 0.25, None, ALU.max)
                    v.tensor_scalar(g_neg[:], gv, -1.0, 0.25, ALU.mult, ALU.max)
                    free(v.tensor_scalar(g_sgn[:], gv, 0.0, 2.0, ALU.is_ge, ALU.mult), u)
                    read(dve, u)
                    link(v.tensor_tensor(g_abs[:], g_abs[:], g_neg[:], ALU.max))
                    last = v.scalar_tensor_tensor(gates[:, l, :, b], g_sgn[:], -1.0, g_abs[:], ALU.add, ALU.mult)
                    if b == 0:
                        link(last)
                last.then_inc(mod_done, 1)

            def rope_tables():
                dve.wait_ge(gam_in, 16)
                dve.wait_ge(cst_in, 16)
                for w in range(2):
                    s = HD ** -0.5 if w == 0 else 1.0
                    gm = gam[:, w].unsqueeze(1)
                    v.scalar_tensor_tensor(rope_c[:, :, w], cosv, s, gm.broadcast_to([P, TT, HD]), ALU.mult, ALU.mult)
                    for o, g0, sign in ((0, HALF, -1.0), (HALF, 0, 1.0)):
                        gs = gam[:, w, g0:g0 + HALF].unsqueeze(1).broadcast_to([P, TT, HALF])
                        last = v.scalar_tensor_tensor(rope_s[:, :, w, o:o + HALF], sinv[:, :, o:o + HALF], s * sign, gs, ALU.mult, ALU.mult)
                last.then_inc(rope_done, 1)

            def rms_stats(n):
                dve.wait_ge(sq_done, n + 1)
                if n:
                    dve.wait_ge(rms_var, n)
                link(v.tensor_reduce(qk_ss[:], sqt[:, n % 2].rearrange("p a h d -> p (a h) d"), AX.X, ALU.add))
                v.tensor_scalar(qk_ve[:, n % 2], qk_ss[:], 1.0 / HD, RMS_EPS, ALU.mult, ALU.add).then_inc(rms_var, 1)

            def rms_rope(n):
                b, t, s = n // TT, n % TT, n % 2
                u = ("qk", b, t)
                dve.wait_ge(rms_rstd, n + 1)
                if n >= 2:
                    dve.wait_ge(qk_split, n - 1)
                rs = qk_rs[:, s].unsqueeze(2).broadcast_to([P, 2 * NH, HD])
                free(v.tensor_tensor(qn[:, s].rearrange("p a h d -> p (a h) d"), ps(u)[:].rearrange("p (h d) -> p h d", d=HD),
                                rs, ALU.mult), u)
                read(dve, u)
                if n == 0:
                    dve.wait_ge(rope_done, 1)
                tab = rope_c[:, t].unsqueeze(2).broadcast_to([P, 2, NH, HD])
                v.tensor_tensor(rr[:, s], qn[:, s], tab, ALU.mult).then_inc(cos_done, 1)

            def qk_lo(n):
                t, s = n % TT, n % 2
                dve.wait_ge(qk_high, n + 1)
                v.tensor_tensor(qkp[:, t, 0, :, HD:2 * HD], rr[:, s, 0], qkp[:, t, 0, :, 0:HD].bitcast(F32), ALU.subtract)
                v.tensor_tensor(qkp[:, t, 1, :, 2 * HD:3 * HD], rr[:, s, 1], qkp[:, t, 1, :, 0:HD].bitcast(F32),
                                ALU.subtract).then_inc(qk_split, 1)

            def heads_out(gr):
                if gr == 0:
                    dve.wait_ge(pool_consts, NCONST)
                if gr >= 2:
                    dve.wait_ge(pv_done, 3 * (gr - 1))
                u = ("kT", gr, 0)
                filled(dve, u)
                v.tensor_copy(KT[0:SLOT, gr % 2, 0, 0], ps(u)[0:SLOT])
                free(v.tensor_copy(KT[SLOT:P, gr % 2, 0, 1], ps(u)[SLOT:P]), u)

            def maxima(gr, hs):
                for h in hs:
                    for t in range(TT):
                        u = ("mx", gr, h, t)
                        n = P * (t + 1)
                        filled(dve, u)
                        m = TT * h + t + TT * HPG * gr
                        if m >= 3:
                            read(dve, ("mx", (m - 3) // (TT * HPG), (m - 3) // TT % HPG, (m - 3) % TT))
                        free(v.tensor_tensor_reduce(out=junk[:, m % 3, 0:n], in0=ps(u)[:, 0:n], in1=mask[:, SEQ - n:SEQ], scale=1.0,
                                                    scalar=LOWEST, op0=ALU.add, op1=ALU.max,
                                                    accum_out=mx[:, gr % 2, t, h:h + 1]), u)

            def negate(gr):
                u = ("maxT", gr)
                filled(dve, u)
                if gr:
                    dve.wait_ge(shift_in[(gr - 1) % 2], 16 * HPG * ((gr - 1) // 2 + 1))
                free(v.tensor_scalar(negm[:], ps(u)[0:HPG], -1.0, None, ALU.mult), u)

            def pv_out(gr):
                dve.wait_ge(pv_done, 3 * gr + 3)
                if gr:
                    filled(dve, ("oN", gr - 1))
                v.tensor_copy(oT[:], pv_bank[:]).then_inc(pv_free, 1)

            def normalise(gr):
                u = ("oN", gr)
                gb = gr % GPB
                filled(dve, u)
                if gr == GPB:
                    filled(dve, ("aT", 0, DC - 1))
                if gr:
                    read(dve, ("oN", gr - 1))
                m = ps(u)[:].rearrange("p (t h e) -> p t h e", t=TT, h=HPG)
                link(v.reciprocal(rc[:], m[:, :, :, HD]))
                dst = att[:, :, gb * HPG * HD:(gb + 1) * HPG * HD].rearrange("p t (h d) -> p t h d", d=HD)
                free(v.tensor_tensor(dst, m[:, :, :, 0:HD], rc[:].unsqueeze(3).broadcast_to([P, TT, HPG, HD]), ALU.mult), u)

            def residual(n, b):
                l, k = n // 2, n % 2
                for i in range(TT // 2):
                    u = ("y", n, b, i)
                    filled(dve, u)
                    if 2 * (2 * n + b) + i:
                        dve.wait_ge(x_done, 2 * (2 * n + b) + i)
                    gt_b = gates[:, l, k, b].unsqueeze(1).broadcast_to([P, 2, D])
                    free(v.tensor_tensor(yt[:], ps(u)[:].rearrange("p (t d) -> p t d", t=2), gt_b, ALU.mult), u)
                    read(dve, u)
                    xs = X[:, TT * b + 2 * i:TT * b + 2 * i + 2]
                    v.tensor_tensor(xs, xs, yt[:], ALU.add).then_inc(x_done, 1)
                dve.wait_ge(x_done, 2 * (2 * n + b) + 2)

            def hidden(n, b, f):
                u = ("up", n, b, f)
                filled(dve, u)
                read(dve, ("gate", n, b, f))
                free(v.tensor_tensor(H[:, b, f], ps(u)[:], sg[:, f % 2], ALU.mult), u)

            def sparsify(b, gb, part):
                n = GB * b + gb
                if part == 0:
                    dve.wait_ge(abs_done, n + 1)
                    ev, od = ab[:, 0:4:2], ab[:, 1:4:2]
                    v.tensor_tensor(pair_hi[:], ev, od, ALU.max)
                    v.tensor_tensor(pair_lo[:], ev, od, ALU.min)
                if part == 1:
                    ev, od = ab[:, 0:4:2], ab[:, 1:4:2]
                    v.tensor_tensor(odd_wins[:], od, ev, ALU.is_gt).then_inc(abs_used, 1)
                    dve.wait_ge(abs_used, n + 1)
                    v.tensor_tensor(both[:, 0], pair_lo[:, 0], pair_hi[:, 1], ALU.is_ge)
                    link(v.tensor_tensor(both[:, 1], pair_lo[:, 1], pair_hi[:, 0], ALU.is_gt))
                if part == 2:
                    if n:
                        dve.wait_ge(sparse_done, n)
                    link(v.tensor_tensor(lean[:], both[:, 0], both[:, 1], ALU.subtract))
                    ln2 = lean[:].unsqueeze(1).broadcast_to([P, 2, SEQ])
                    v.tensor_tensor(d_sub[:], ln2, odd_wins[:], ALU.subtract)
                    link(v.tensor_tensor(d_add[:], ln2, odd_wins[:], ALU.add))
                if part == 3:
                    for j, (d, thr, op) in enumerate(((d_sub[:, 0], 0.0, ALU.is_ge), (d_add[:, 0], 1.0, ALU.is_ge),
                                                      (d_add[:, 1], 0.0, ALU.is_le), (d_sub[:, 1], -1.0, ALU.is_le))):
                        hj = H[:, b, 4 * gb + j]
                        last = v.scalar_tensor_tensor(hj, d, thr, hj, op, ALU.mult)
                    last.then_inc(sparse_done, 1)

            def conv(b):
                dve.wait_ge(chan_in, 48)
                for k in range(KC):
                    n = KC * b + k
                    u = ("pj", b, k)
                    dve.wait_ge(conv_begun, n + 1)
                    for j in range(TAPS - 2, -1, -1):
                        s = TAPS - 1 - j
                        last = v.scalar_tensor_tensor(acc[:, k % 2, s:SEQ], ps(u)[:, 0:SEQ - s], ch[:, k, S_CONV + j:S_CONV + j + 1],
                                                      acc[:, k % 2, s:SEQ], ALU.mult, ALU.add)
                        if j:
                            link(last)
                        else:
                            free(last, u)

            def softplus(b):
                dve.wait_ge(sp_e_done, b + 1)
                if b:
                    dve.wait_ge(dts_done, b)
                    filled(dve, ("spread", b - 1, KC - 1))
                link(v.tensor_scalar(sp_u[:], sp_e[:], 1.0, -1.0, ALU.add, ALU.add))
                link(v.tensor_tensor(sp_c[:], sp_e[:], sp_u[:], ALU.subtract))
                dve.wait_ge(sp_l_done, b + 1)
                link(v.tensor_tensor(sp_u[:], sp_l[:], sp_c[:], ALU.add))
                link(v.scalar_tensor_tensor(sp_c[:], sp_z[:], 0.0, sp_u[:], ALU.max, ALU.add))
                link(v.tensor_copy(dts[0:SH], sp_c[:]))
                v.tensor_tensor(dts[32:32 + SH], sp_c[:], dts[0:SH].bitcast(F32), ALU.subtract).then_inc(dts_done, 1)

            def mix(b):
                for k in range(KC):
                    n = KC * b + k
                    u = ("spread", b, k)
                    filled(dve, u)
                    dve.wait_ge(decay_done, n + 1)
                    free(v.scalar_tensor_tensor(drive[:], ps(u)[:], ch[:, k, S_B:S_B + 1], xc[b][:, k], ALU.mult, ALU.mult), u)
                    read(dve, u)
                    if n:
                        dve.wait_ge(y_done, n)
                    link(v.tensor_tensor_scan(state[:], decay[:, k % 2], drive[:], 0.0, ALU.mult, ALU.add))
                    dve.wait_ge(skip_done, n + 1)
                    if n >= 2:
                        dve.wait_ge(comb_done, n - 1)
                    v.scalar_tensor_tensor(yv[:, k % 2], state[:], ch[:, k, S_C:S_C + 1], skip[:, k % 2], ALU.mult, ALU.add).then_inc(y_done, 1)

            ln_stats(0, 0)
            dve.wait_ge(silu_c_done, 1)
            v.tensor_copy(silu_cb[:].rearrange("p l c b m -> p (l c b) m"),
                          silu_c[:].rearrange("p l c b -> p (l c b)").unsqueeze(2).broadcast_to([P, 2 * DC * NB, P])).then_inc(silu_cb_done, 1)
            dve.wait_ge(wq_split_hi, 1)
            v.tensor_tensor(wq_lo[:], wq_raw[:], wq_hi[:].bitcast(F32), ALU.subtract).then_inc(wq_split, 1)
            mod_out(0)
            ln_lo(0, 0)
            rope_tables()
            v.tensor_copy(sel[:], cst[:, C_SEL:C_MASK].rearrange("p (k m) -> p k m", k=KC)).then_inc(sel_done, 1)
            rms_stats(0)
            for n in range(1, TT + 3):
                if n < TT:
                    rms_stats(n)
                if n >= 3:
                    qk_lo(n - 3)
                if n <= TT:
                    rms_rope(n - 1)
            ln_stats(0, 1)
            mod_out(1)
            ln_lo(0, 1)
            heads_out(0)
            maxima(0, range(HPG))
            for gr in range(NG):
                negate(gr)
                if gr + 1 < NG:
                    heads_out(gr + 1)
                if gr:
                    normalise(gr - 1)
                if gr + 1 < NG:
                    maxima(gr + 1, range(HPG))
                pv_out(gr)
                if gr == 2:
                    rms_stats(TT)
                    for n in range(TT + 1, 2 * TT + 3):
                        if n < 2 * TT:
                            rms_stats(n)
                        if n >= TT + 3:
                            qk_lo(n - 3)
                        if n <= 2 * TT:
                            rms_rope(n - 1)
                if gr == GPB:
                    residual(0, 0)
            normalise(NG - 1)
            ln_stats(1, 0)
            ln_lo(1, 0)
            todo = []
            for b in range(NB):
                for f in range(FC):
                    hidden(1, b, f)
                    if todo:
                        sparsify(*todo.pop(0))
                    if f % 4 == 3:
                        todo += [(b, f // 4, part) for part in range(4)]
                if b == 0:
                    residual(0, 1)
                    ln_stats(1, 1)
                    ln_lo(1, 1)
            for td in todo:
                sparsify(*td)
            residual(1, 0)
            ln_stats(2, 0)
            ln_lo(2, 0)
            v.memset(dts[:].bitcast(F32), 0.0)
            conv(0)
            residual(1, 1)
            ln_stats(2, 1)
            ln_lo(2, 1)
            softplus(0)
            conv(1)
            dve.wait_ge(chan_in, 48)
            mix(0)
            softplus(1)
            residual(2, 0)
            ln_stats(3, 0)
            ln_lo(3, 0)
            mix(1)
            for b in range(NB):
                for f in range(FC):
                    hidden(3, b, f)
                if b == 0:
                    residual(2, 1)
                    ln_stats(3, 1)
                    ln_lo(3, 1)
            residual(3, 0)
            residual(3, 1)

        @block.tensor
        def _(pe):
            mm, tr = nc.tensor.matmul, nc.tensor.transpose

            def mm3(dst, a_hi, a_lo, b_hi, b_lo, first, last):
                mm(dst, a_hi, b_hi, start=first, stop=False)
                mm(dst, a_hi, b_lo, start=False, stop=False)
                return mm(dst, a_lo, b_hi, start=False, stop=last)

            def ln(n, b):
                pe.wait_ge(xn_done, 2 * n + b + 1)
                if n == 0 and b == 0:
                    pe.wait_ge(cst_in, 16)
                for c in range(DC):
                    u = ("ln", n, b, c)
                    claim(pe, u)
                    for t in range(TT):
                        last = tr(ps(u)[:, P * t:P * t + P], xn[:, t, P * c:P * c + P], ident)
                    fill(last, u)

            def mod(l):
                pe.wait_ge(wmod_in[l], 16)
                pe.wait_ge(silu_cb_done, 1)
                u = ("modT", l)
                claim(pe, u)
                for ki, kind in enumerate((0, 1, 3, 4)):
                    for c in range(DC):
                        o = 2 * (DC * ki + c)
                        for kc in range(DC):
                            last = mm(ps(u)[:, o:o + NB], wmod_s[:, l, kc, D * kind + P * c:D * kind + P * c + P],
                                      silu_c[:, l, kc], start=kc == 0, stop=kc == DC - 1)
                fill(last, u)
                for b in range(NB):
                    u = ("modG", l, b)
                    claim(pe, u)
                    for ki, kind in enumerate((2, 5)):
                        for kc in range(DC):
                            last = mm(ps(u)[:, D * ki:D * ki + D], silu_cb[:, l, kc, b], wmod_s[:, l, kc, D * kind:D * kind + D],
                                      start=kc == 0, stop=kc == DC - 1)
                    fill(last, u)

            def qkv(b, t):
                if t == 0:
                    pe.wait_ge(h_done, b + 1)
                    pe.wait_ge(wq_split, 1)
                for u, o, n in ((("qk", b, t), 0, 2 * D), (("v", b, t), 2 * D, D)):
                    claim(pe, u)
                    for c in range(DC):
                        ts = slice(P * t, P * t + P)
                        last = mm3(ps(u)[:, 0:n], h_hi[:, b, c, ts], h_lo[:, b, c, ts],
                                   wq_hi[:, c, o:o + n], wq_lo[:, c, o:o + n], c == 0, c == DC - 1)
                    fill(last, u)

            def heads(gr):
                b, g4 = gr // GPB, gr % GPB
                pe.wait_ge(qk_split, TT * (b + 1))
                if gr == 0:
                    pe.wait_ge(pool_consts, NCONST)
                for j in range(2):
                    for w, nm in enumerate(("qT", "kT")):
                        u = (nm, gr, j)
                        claim(pe, u)
                        for t in range(TT):
                            h0 = HPG * g4 + 2 * j
                            last = tr(ps(u)[:, P * t:P * t + P], qkp[:, t, w, h0:h0 + 2, :].rearrange("p h e -> p (h e)").bitcast(F32), ident)
                        fill(last, u)

            def score_max(gr, h, t):
                u = ("mx", gr, h, t)
                claim(pe, u)
                s = gr % 2
                if h == 0 and t == 0:
                    read(pe, ("qT", gr, 1))
                    read(pe, ("kT", gr, 0))
                    read(pe, ("kT", gr, 1))
                fill(mm(ps(u)[:, 0:P * (t + 1)], QT[:, s, h // 2, P * t:P * t + P], KT[:, s, h // 2, h % 2, 0:P * (t + 1)],
                        start=True, stop=True), u)

            def max_T(gr):
                u = ("maxT", gr)
                read(pe, ("mx", gr, HPG - 1, TT - 1))
                claim(pe, u)
                for t in range(TT):
                    last = tr(ps(u)[0:HPG, P * t:P * t + P], mx[:, gr % 2, t], ident)
                fill(last, u)

            def scores(gr, s, i):
                u = ("st", gr, s, i)
                w = gr % 2
                claim(pe, u)
                if s == 0 and i == 0:
                    pe.wait_ge(shift_in[w], 16 * HPG * (gr // 2 + 1))
                parts = (((i, 0, 0),), ((i, 1, 0), (i, 3, 384)), ((2 * i, 2, 0), (2 * i + 1, 2, 256)))[s]
                for h, c, o in parts:
                    n = SEQ - P * c
                    last = mm(ps(u)[:, o:o + n], KT[:, w, h // 2, h % 2, P * c:P * c + P], QT[:, w, h // 2, P * c:SEQ],
                              start=True, stop=True)
                fill(last, u)

            def probs_v(gr, s):
                b = gr // GPB
                pe.wait_ge(causal_done, 10 * gr + (4, 8, 10)[s])
                if s == 0 and gr:
                    pe.wait_ge(pv_free, gr)
                for c in ((0,), (1, 3), (2,))[s]:
                    o = 384 if c == 3 else 0
                    n = SEQ - P * c
                    for h in range(HPG):
                        last = mm(pv_bank[32 * h:32 * h + 32, P * c:SEQ], vp[:, b, c, HPG * (gr % GPB) + h, :],
                                  PT[s][:, h, o:o + n], start=c == 0, stop=c == 2, tile_position=(0, 32 * h))
                last.then_inc(pv_done, 1)

            def out_T(gr):
                u = ("oN", gr)
                pe.wait_ge(pv_free, gr + 1)
                claim(pe, u)
                for t in range(TT):
                    last = tr(ps(u)[:, P * t:P * t + P], oT[:, P * t:P * t + P], ident)
                fill(last, u)

            def att_T(b):
                read(pe, ("oN", GPB * b + GPB - 1))
                for c in range(DC):
                    u = ("aT", b, c)
                    claim(pe, u)
                    for t in range(TT):
                        last = tr(ps(u)[:, P * t:P * t + P], att[:, t, P * c:P * c + P], ident)
                    fill(last, u)

            def down(n, b):
                if n == 0:
                    pe.wait_ge(wout_in, 16)
                    read(pe, ("aT", b, DC - 1))
                    srcs = [(aT[:, c], wout_s[:, c]) for c in range(DC)]
                elif n == 1:
                    pe.wait_ge(wdn_in, 16)
                    pe.wait_ge(sparse_done, GB * (b + 1))
                    srcs = [(H[:, b, f], wdn_s[:, f]) for f in range(FC)]
                elif n == 2:
                    pe.wait_ge(woutp_in, 16)
                    pe.wait_ge(comb_done, KC * (b + 1))
                    srcs = [(gt[b][:, k], woutp_s[:, k]) for k in range(KC)]
                else:
                    read(pe, ("had", FC // 2 - 1))
                    read(pe, ("up", 3, b, FC - 1))
                    srcs = [(H[:, b, f], w2a[:, f]) for f in range(FC)]
                for i in range(TT // 2):
                    u = ("y", n, b, i)
                    claim(pe, u)
                    for tt in range(2):
                        t = 2 * i + tt
                        for j, (act_t, w) in enumerate(srcs):
                            last = mm(ps(u)[:, D * tt:D * tt + D], act_t[:, P * t:P * t + P], w, start=j == 0, stop=j == len(srcs) - 1)
                    fill(last, u)

            def gate_up(n, b, f):
                if f == 0:
                    pe.wait_ge(h_done, 2 * n + b + 1)
                if f % 2 == 0 and b == 0:
                    pe.wait_ge(stage_split, (1 if n == 1 else 7) + f // 2)
                hi, lo = (gua_hi, gua_lo) if f < 4 else (gub_hi, gub_lo)
                for w, nm in enumerate(("gate", "up")):
                    u = (nm, n, b, f)
                    claim(pe, u)
                    for c in range(DC):
                        last = mm3(ps(u)[:], hi[:, f % 4, w, c], lo[:, f % 4, w, c], h_hi[:, b, c], h_lo[:, b, c], c == 0, c == DC - 1)
                    fill(last, u)

            def proj(b):
                pe.wait_ge(h_done, 4 + b + 1)
                pe.wait_ge(stage_split, 6)
                for k in range(KC):
                    for w, nm in enumerate(("pj", "gt")):
                        u = (nm, b, k)
                        claim(pe, u)
                        for c in range(DC):
                            last = mm3(ps(u)[:], pj_hi[:, k, w, c], pj_lo[:, k, w, c], h_hi[:, b, c], h_lo[:, b, c], c == 0, c == DC - 1)
                        fill(last, u)

            def dt(b):
                u = ("dt", b)
                claim(pe, u)
                pe.wait_ge(chan_in, 48)
                pe.wait_ge(xc_done, KC * (b + 1))
                for k in range(KC):
                    last = mm(ps(u)[0:SH], dtw_s[:, k], xc[b][:, k], start=k == 0, stop=k == KC - 1)
                fill(last, u)

            def spread(b):
                pe.wait_ge(dts_done, b + 1)
                pe.wait_ge(sel_done, 1)
                for k in range(KC):
                    u = ("spread", b, k)
                    claim(pe, u)
                    fill(mm(ps(u)[:], sel[:, k], dts[:], start=True, stop=True), u)

            def hadamard():
                pe.wait_ge(w2_mixed, 1)
                for i in range(FC // 2):
                    u = ("had", i)
                    claim(pe, u)
                    for c in range(2):
                        last = mm(ps(u)[:, D * c:D * c + D], had, w2b[:, 2 * i + c], start=True, stop=True)
                    fill(last, u)

            run = {"ln": ln, "mod": mod, "qkv": qkv, "T": heads, "mx": score_max, "maxT": max_T, "st": scores, "pv": probs_v,
                   "oN": out_T, "aT": att_T, "y": down, "gu": gate_up, "proj": proj, "dt": dt, "spread": spread, "had": hadamard}
            for s in stages:
                run[s[0]](*s[1:])


def shape_constants():
    c = np.zeros((P, C_END), np.float32)
    c[:, C_ID:C_HAD] = np.eye(P, dtype=np.float32)
    i = np.arange(P)
    par = np.array([[bin(a & b).count("1") & 1 for b in i] for a in i])
    c[:, C_HAD:C_SEL] = 1 - 2 * par
    for k in range(KC):
        for m in range(P):
            h = (P * k + m) // SHD
            c[h, C_SEL + P * k + m] = 1
            c[32 + h, C_SEL + P * k + m] = 1
    tri = np.where(i[None, :] > i[:, None], NEG, 0.0)
    c[:, C_COS - P:C_COS] = tri
    inv = (1.0 / 10000.0 ** (np.arange(0, HD, 2, dtype=np.float32) / HD)).astype(np.float32)
    fr = np.arange(SEQ, dtype=np.float32)[:, None] * inv[None, :]
    emb = np.concatenate([fr, fr], -1)
    for o, f in ((C_COS, np.cos), (C_SIN, np.sin)):
        c[:, o:o + TT * HD] = f(emb).reshape(TT, P, HD).transpose(1, 0, 2).reshape(P, TT * HD)
    return c


def kernel(**inputs):
    import concourse.bacc as _bacc
    from concourse.bass_utils import run_bass_kernel_spmd as _run

    w = {k: np.asarray(v) for k, v in inputs.items()}

    def rows(a):
        return a.reshape(-1, P, a.shape[-1]).transpose(1, 0, 2)

    def pair_up(a, b):
        both = np.stack([a, b]).reshape(2, DC, P, -1, P)
        return both.transpose(2, 3, 0, 1, 4)

    order = np.arange(HID).reshape(GB, P, 4).transpose(0, 2, 1).reshape(-1)
    chan = np.concatenate([w["L1_attn_conv_weight"]] + [w["L1_attn_" + n].reshape(INNER, 1)
                          for n in ("conv_bias", "A_log", "B", "C", "D")], axis=1)
    dtw = np.zeros((INNER, SH), np.float32)
    for h in range(SH):
        dtw[SHD * h:SHD * (h + 1), h] = w["L1_attn_dt_w"][h]
    arrays = {
        "x": w["L0_attn_x"].reshape(NB * SEQ, D),
        "wqkv": rows(w["L0_attn_w_qkv"]),
        "wout": rows(w["L0_attn_w_out"]),
        "gammas": np.tile(np.stack([w["L0_attn_q_gamma"], w["L0_attn_k_gamma"]])[None], (P, 1, 1)),
        "wgu0": pair_up(w["L0_ffn_w_gate"][:, order], w["L0_ffn_w_up"][:, order]),
        "wdn0": rows(w["L0_ffn_w_down"][order]),
        "wmod": np.stack([rows(w["L0_wmod"]), rows(w["L1_wmod"])], axis=1),
        "cT": np.stack([rows(w["L0_c"].T), rows(w["L1_c"].T)], axis=1),
        "wproj": pair_up(w["L1_attn_in_proj_w"].T, w["L1_attn_gate_proj_w"].T),
        "woutp": rows(w["L1_attn_out_proj_w"].T),
        "chan": rows(chan),
        "dtw": rows(dtw),
        "dtb": w["L1_attn_dt_b"].reshape(SH, 1),
        "wgu1": pair_up(w["L1_ffn_W1"].T, w["L1_ffn_W3"].T),
        "w2t": rows(w["L1_ffn_W2"].T),
        "consts": shape_constants(),
    }
    arrays = {f"in_{k}": np.ascontiguousarray(v) for k, v in arrays.items()}
    nc = _bacc.Bacc("TRN2", target_bir_lowering=False, num_devices=1)
    args = [nc.dram_tensor(k, v.shape, mybir.dt.from_np(v.dtype), kind="ExternalInput").ap() for k, v in arrays.items()]
    out = nc.dram_tensor("out_0", (NB * SEQ, D), F32, kind="ExternalOutput").ap()
    adaln_blocks(nc, *args, out)
    r = _run(nc, [arrays], core_ids=[0])
    return r.results[0]["out_0"].reshape(NB, SEQ, D)
```

```python
from contextlib import ExitStack

import numpy as np

import concourse.bass as bass
from concourse import mybir

F32 = mybir.dt.float32
R32 = mybir.dt.float32r
I32 = mybir.dt.int32
BF16 = mybir.dt.bfloat16
ALU = mybir.AluOpType
ACT = mybir.ActivationFunctionType
AX = mybir.AxisListType

P = 128
NB, SEQ, D = 2, 512, 256
TT = SEQ // P
DC = D // P
NH, HD = 16, 16
HALF = HD // 2
HID = 1024
FC = HID // P
GB = FC // 4
INNER = 512
KC = INNER // P
SH, SHD = 8, 64
TAPS = 4
SLOT = 64
SHIFT = 3 * HD
HPG = 4
NG = NB * NH // HPG
GPB = NH // HPG
RING = 7
LN_EPS, RMS_EPS = 1e-5, 1e-6
RSQRT_GUESS = float(0x5F3759DF)
LOWEST = -3.0e38
NEG = -1.0e30

C_ID = 0
C_HAD = C_ID + P
C_MASK = C_HAD + P
C_COS = C_MASK + SEQ
C_SIN = C_COS + TT * HD
C_END = C_SIN + TT * HD
S_CONV, S_BIAS, S_ALOG, S_B, S_C, S_D, S_END = 0, 4, 5, 6, 7, 8, 9


def attention_steps(g):
    nxt = [("mx", g + 1, h, t) for h in range(HPG) for t in range(TT)] if g + 1 < NG else []
    steps = nxt[:4] + ([("oN", g - 1)] if g else [])
    nxt = nxt[4:]
    between = {3: [("qkv", 1, 0)], 7: [("qkv", 1, 1)]} if g == 0 else {3: [("qkv", 1, 2)], 7: [("qkv", 1, 3)]} if g == 1 else \
        {1: [("aT", 0)]} if g == GPB else {7: [("ln", 1, 0)]} if g == GPB + 1 else {}
    scores = [("st", g, s, i) for s, n in ((0, 4), (1, 4), (2, 2)) for i in range(n)]
    for i, sc in enumerate(scores):
        take = 2 if i in (2, 5) else 1
        steps += [sc] + nxt[:take] + between.get(i, [])
        nxt = nxt[take:]
        if i == 7:
            steps.append(("pv", g, 0))
    if g + 2 < NG:
        steps.append(("T", g + 2))
    if g + 1 < NG:
        steps.append(("maxT", g + 1))
    return steps + [("pv", g, 1), ("pv", g, 2)] + ([("y", 0, 0)] if g == GPB else [])


def plan():
    def gu(n, b, lo, hi):
        return [("gu", n, b, f) for f in range(lo, hi)]

    s = [("ln", 0, 0), ("modT", 0)] + [("qkv", 0, t) for t in range(TT)] + [("modT", 1), ("ln", 0, 1), ("gT", 0), ("T", 0), ("gT", 1)]
    s += [("mx", 0, h, t) for h in range(HPG) for t in range(TT)] + [("maxT", 0), ("T", 1)]
    for g in range(NG):
        s += attention_steps(g)
    s += gu(1, 0, 0, 2) + [("oN", NG - 1)] + gu(1, 0, 2, 3) + [("aT", 1)] + gu(1, 0, 3, 4) + [("y", 0, 1)]
    s += gu(1, 0, 4, 7) + [("ln", 1, 1)] + gu(1, 0, 7, 8)
    s += gu(1, 1, 0, 5) + [("y", 1, 0)] + gu(1, 1, 5, 8)
    s += [("ln", 2, 0), ("proj", 0), ("y", 1, 1), ("had",), ("dt", 0), ("ln", 2, 1), ("proj", 1), ("spread", 0), ("dt", 1)]
    s += [("y", 2, 0), ("spread", 1), ("ln", 3, 0)]
    s += gu(3, 0, 0, 4) + [("y", 2, 1)] + gu(3, 0, 4, 7) + [("ln", 3, 1)] + gu(3, 0, 7, 8)
    s += gu(3, 1, 0, 5) + [("y", 3, 0)] + gu(3, 1, 5, 8) + [("y", 3, 1)]
    return s


def products(stage):
    k = stage[0]
    if k == "ln":
        return [("ln", stage[1], stage[2], c) for c in range(DC)]
    if k == "gT":
        return [("gT", stage[1], w) for w in range(2)]
    if k == "qkv":
        return [("qk",) + stage[1:], ("v",) + stage[1:]]
    if k == "T":
        return [(n, stage[1], j) for j in range(2) for n in ("qT", "kT")]
    if k in ("modT", "mx", "st", "maxT", "oN", "dt"):
        return [stage]
    if k == "pv":
        return []
    if k == "aT":
        return [("aT", stage[1], c) for c in range(DC)]
    if k == "y":
        return [stage + (i,) for i in range(TT // 2)]
    if k == "gu":
        return [("gate",) + stage[1:], ("up",) + stage[1:]]
    if k == "proj":
        return [(n, stage[1], c) for c in range(KC) for n in ("pj", "gt")]
    if k == "spread":
        return [("spread", stage[1], c) for c in range(KC)]
    if k == "had":
        return [("had", i) for i in range(FC // 2)]
    raise ValueError(stage)


def adaln_blocks(nc, x, wqkv, wout, gammas, wgu0, wdn0, wmod, cT, wproj, woutp, chan, dtw, dtb, wgu1, w2t, consts, spread_sel, out):
    stages = plan()
    place = {}
    for s in stages:
        for u in products(s):
            place[u] = (len(place) % RING, len(place) // RING)

    with ExitStack() as ctx:
        cursor = [(nc.sbuf_base + 31) // 32 * 32]

        def at(name, shape, dt=F32):
            n = int(np.prod(shape[1:])) * (2 if dt == BF16 else 4)
            t = nc.alloc_sbuf_tensor_at(name, shape, dt, offset=cursor[0])
            cursor[0] += (n + 31) // 32 * 32
            return t

        cst = at("cst", [P, C_END])
        sel = at("sel", [P, KC, P], R32)
        rope_c = at("rope_c", [P, TT, 2, HD])
        rope_s = at("rope_s", [P, TT, 2, HD])
        gam = at("gam", [P, 2, HD])
        ch = at("ch", [P, KC, S_END])
        neg_a = at("neg_a", [P, KC])
        dtw_s = at("dtw_s", [P, KC, SH])
        dtb_s = at("dtb_s", [SH, 1])
        c_s = at("c_s", [P, 2, DC, NB])
        silu_c = at("silu_c", [P, 2, DC, NB])
        modT = at("modT", [P, 2, 4, DC, NB])
        gates = at("gates", [P, 2, 2, NB, D])
        stats = at("stats", [P, TT, 6])
        mv = at("mv", [P, TT, 2])
        ln_ve = at("ln_ve", [P, TT])
        ln_rs = at("ln_rs", [P, TT])
        nt = at("nt", [P, TT * 2 * NH])
        qk_ss = at("qk_ss", [P, TT, 2 * NH])
        qk_rs = at("qk_rs", [P, TT, 2 * NH])
        gateT = at("gateT", [P, 2, 2, DC, NB])
        g_tmp = at("g_tmp", [P, 3, 2, DC, NB])
        X = at("X", [P, NB * TT, D])
        h_hi = at("h_hi", [P, NB, DC, SEQ], R32)
        h_lo = at("h_lo", [P, NB, DC, SEQ], R32)
        wout_s = at("wout_s", [P, DC, D])
        wq_hi = at("wq_hi", [P, DC, 3 * D], R32)
        wq_lo = at("wq_lo", [P, DC, 3 * D], R32)
        w2b_at = cursor[0] - 2 * DC * 3 * D * 4
        stage_at = cursor[0]
        stage = at("stage", [P, 2, 2, 2, DC, P])
        gua_hi = at("gua_hi", [P, FC // 2, 2, DC, P], R32)
        gua_lo = at("gua_lo", [P, FC // 2, 2, DC, P], R32)
        xn = at("xn", [P, TT, D])
        hf = at("hf", [P, DC, SEQ])
        yt = at("yt", [P, 2, D])
        area = cursor[0]

        qkp = at("qkp", [P, TT, 2, NH, SLOT], R32)
        QT = at("QT", [P, 2, 2, SEQ], R32)
        KT = at("KT", [P, 2, 2, 2, SEQ], R32)
        vp = at("vp", [P, NB, TT, NH, 32])
        rot = at("rot", [P, 2, NH, HD])
        early = cursor[0]
        PTa = at("PTa", [P, HPG, SEQ])
        PTb = at("PTb", [P, HPG, SEQ])
        PTc = at("PTc", [P, HPG, SEQ // 2])
        oT = at("oT", [P, SEQ])
        junk = at("junk", [P, 3, SEQ], BF16)
        mx = at("mx", [P, 2, TT, HPG])
        negm = at("negm", [HPG, SEQ], R32)
        rc = at("rc", [P, TT, HPG])
        att_at = cursor[0]
        att = at("att", [P, TT, D])
        aT_at = cursor[0]
        aT = at("aT", [P, DC, SEQ])
        wmod_s = nc.alloc_sbuf_tensor_at("wmod_s", [P, 2, DC, 6 * D], F32, offset=early)
        g_cols = nc.alloc_sbuf_tensor_at("g_cols", [P, 2, DC, NB, P], F32, offset=att_at)
        sel_raw = nc.alloc_sbuf_tensor_at("sel_raw", [P, KC, P], F32, offset=aT_at)
        wq_raw = nc.alloc_sbuf_tensor_at("wq_raw", [P, DC, 3 * D], F32, offset=stage_at)
        cursor[0] = stage_at
        sq = at("sq", [P, TT, 2, NH, HD])
        qn = at("qn", [P, TT, 2, NH, HD])
        rr = at("rr", [P, TT, 2, NH, HD])

        cursor[0] = area
        gub_hi = at("gub_hi", [P, FC // 2, 2, DC, P], R32)
        gub_lo = at("gub_lo", [P, FC // 2, 2, DC, P], R32)
        pj_hi = at("pj_hi", [P, KC, 2, DC, P], R32)
        pj_lo = at("pj_lo", [P, KC, 2, DC, P], R32)
        wdn_s = at("wdn_s", [P, FC, D])
        woutp_s = at("woutp_s", [P, KC, D])
        w2a = at("w2a", [P, FC, D])
        hidden_at = cursor[0]
        H = at("H", [P, NB, FC, SEQ])
        sg = at("sg", [P, 2, SEQ])
        ab = at("ab", [P, 4, SEQ])
        pair_hi = at("pair_hi", [P, 2, SEQ])
        pair_lo = at("pair_lo", [P, 2, SEQ])
        odd_wins = at("odd_wins", [P, 2, SEQ], BF16)
        both = at("both", [P, 2, SEQ], BF16)
        lean = at("lean", [P, SEQ], BF16)
        d_sub = at("d_sub", [P, 2, SEQ], BF16)
        d_add = at("d_add", [P, 2, SEQ], BF16)
        w2b = nc.alloc_sbuf_tensor_at("w2b", [P, FC, D], F32, offset=w2b_at)
        xc = [nc.alloc_sbuf_tensor_at(f"xc{b}", [P, KC, SEQ], F32, offset=hidden_at + b * FC * SEQ * 4) for b in range(NB)]
        gt = [nc.alloc_sbuf_tensor_at(f"gt{b}", [P, KC, SEQ], F32, offset=hidden_at + b * FC * SEQ * 4 + KC * SEQ * 4) for b in range(NB)]
        cursor[0] = hidden_at + NB * FC * SEQ * 4
        acc = at("acc", [P, 2, SEQ])
        decay = at("decay", [P, 2, SEQ])
        drive = at("drive", [P, SEQ])
        state = at("state", [P, SEQ])
        skip = at("skip", [P, 2, SEQ])
        yv = at("yv", [P, 2, SEQ])
        dts = at("dts", [P, SEQ], R32)
        sp_z = at("sp_z", [SH, SEQ])
        sp_a = at("sp_a", [SH, SEQ])
        sp_e = at("sp_e", [SH, SEQ])
        sp_l = at("sp_l", [SH, SEQ])
        sp_u = at("sp_u", [SH, SEQ])
        sp_c = at("sp_c", [SH, SEQ])

        ident = cst[:, C_ID:C_ID + P]
        had = cst[:, C_HAD:C_HAD + P]
        mask = cst[:, C_MASK:C_MASK + SEQ]
        cosv = cst[:, C_COS:C_SIN].rearrange("p (t d) -> p t d", t=TT)
        sinv = cst[:, C_SIN:C_END].rearrange("p (t d) -> p t d", t=TT)
        PT = [PTa, PTb, PTc]

        bank = [ctx.enter_context(nc.psum_tensor(f"bank{i}", [P, SEQ], F32)) for i in range(RING)]
        pv_bank = ctx.enter_context(nc.psum_tensor("pv_bank", [P, SEQ], F32))

        def sem(name):
            return ctx.enter_context(nc.semaphore(name))

        bank_full = [sem(f"bank_full{i}") for i in range(RING)]
        bank_free = [sem(f"bank_free{i}") for i in range(RING)]
        x_in = [sem(f"x_in{b}") for b in range(NB)]
        wq_in, cst_in, wout_in = sem("wq_in"), sem("cst_in"), sem("wout_in")
        wmod_in = [sem("wmod_in0"), sem("wmod_in1")]
        c_in, gam_in, chan_in, sel_in = sem("c_in"), sem("gam_in"), sem("chan_in"), sem("sel_in")
        stage_in = [sem("stage_in0"), sem("stage_in1")]
        wdn_in, woutp_in, w2_in = sem("wdn_in"), sem("woutp_in"), sem("w2_in")
        shift_in = [sem("shift_in0"), sem("shift_in1")]
        out_done = sem("out_done")
        pool_consts, pool_chain, dve_chain, act_chain = sem("pool_consts"), sem("pool_chain"), sem("dve_chain"), sem("act_chain")
        silu_c_done, gateT_done, g_cols_done = sem("silu_c_done"), sem("gateT_done"), sem("g_cols_done")
        wq_split_hi, wq_split = sem("wq_split_hi"), sem("wq_split")
        stage_split = sem("stage_split")
        xn_done, h_done = sem("xn_done"), sem("h_done")
        sq_done, cos_done, roped, scaled, qk_high, qk_split = (
            sem(n) for n in ("sq_done", "cos_done", "roped", "scaled", "qk_high", "qk_split"))
        causal_done, pv_done, pv_free = (
            sem(n) for n in ("causal_done", "pv_done", "pv_free"))
        abs_done, abs_used, sparse_done, x_done = sem("abs_done"), sem("abs_used"), sem("sparse_done"), sem("x_done")
        conv_begun, xc_done = sem("conv_begun"), sem("xc_done")
        sp_e_done, sp_l_done, dts_done = sem("sp_e_done"), sem("sp_l_done"), sem("dts_done")
        decay_done, skip_done, y_done, comb_done = (
            sem("decay_done"), sem("skip_done"), sem("y_done"), sem("comb_done"))
        w2_mixed = sem("w2_mixed")
        sel_done, rope_done = sem("sel_done"), sem("rope_done")

        def ps(u):
            return bank[place[u][0]]

        def claim(eng, u):
            if place[u][1]:
                eng.wait_ge(bank_free[place[u][0]], place[u][1])

        def filled(eng, u):
            eng.wait_ge(bank_full[place[u][0]], place[u][1] + 1)

        def read(eng, u):
            eng.wait_ge(bank_free[place[u][0]], place[u][1] + 1)

        def h_used(eng, n, b):
            filled(eng, (("v", b, TT - 1), ("up", 1, b, FC - 1), ("gt", b, KC - 1))[n])

        def fill(ins, u):
            ins.then_inc(bank_full[place[u][0]], 1)

        def free(ins, u):
            ins.then_inc(bank_free[place[u][0]], 1)

        block = ctx.enter_context(nc.Block())
        NCONST = 5

        @block.sync
        def _(sp):
            xv = x.rearrange("(b t p) d -> b p t d", b=NB, p=P)
            ov = out.rearrange("(b t p) d -> b p t d", b=NB, p=P)
            sp.dma_start(X[:, 0:TT, :], xv[0]).then_inc(x_in[0], 16)
            sp.dma_start(c_s[:], cT).then_inc(c_in, 16)
            sp.dma_start(cst[:], consts).then_inc(cst_in, 16)
            sp.dma_start(wmod_s[:, 0], wmod[:, 0]).then_inc(wmod_in[0], 16)
            sp.dma_start(wq_raw[:], wqkv).then_inc(wq_in, 16)
            sp.dma_start(gam[:], gammas).then_inc(gam_in, 16)
            sp.dma_start(wmod_s[:, 1], wmod[:, 1]).then_inc(wmod_in[1], 16)
            sp.dma_start(X[:, TT:2 * TT, :], xv[1]).then_inc(x_in[1], 16)
            sp.dma_start(ch[:], chan).then_inc(chan_in, 16)
            sp.dma_start(dtw_s[:], dtw).then_inc(chan_in, 16)
            sp.dma_start(dtb_s[:], dtb).then_inc(chan_in, 16)
            sp.dma_start(sel_raw[:], spread_sel).then_inc(sel_in, 16)
            sp.dma_start(wout_s[:], wout).then_inc(wout_in, 16)

            def stage_load(i):
                src = wgu0[:, 2 * i:2 * i + 2] if i < 4 else wproj[:, 2 * (i - 4):2 * (i - 4) + 2] if i < 6 else wgu1[:, 2 * (i - 6):2 * (i - 6) + 2]
                if i >= 2:
                    sp.wait_ge(stage_split, i - 1)
                sp.dma_start(stage[:, i % 2], src).then_inc(stage_in[i % 2], 16)

            for g in range(NG):
                read(sp, ("maxT", g))
                for h in range(HPG):
                    row = SHIFT + SLOT * (h % 2)
                    sp.dma_start(QT[row:row + 1, g % 2, h // 2, :].bitcast(F32), negm[h:h + 1, :].bitcast(F32)).then_inc(shift_in[g % 2], 16)
                if g == GPB:
                    sp.wait_ge(qk_split, NB * TT)
                    stage_load(0)
                    stage_load(1)
                if g == GPB + 2:
                    stage_load(2)
                    stage_load(3)
            stage_load(4)
            stage_load(5)
            filled(sp, ("st", NG - 1, 2, 1))
            sp.dma_start(wdn_s[:], wdn0).then_inc(wdn_in, 16)
            sp.wait_ge(x_done, 4)
            sp.dma_start(woutp_s[:], woutp).then_inc(woutp_in, 16)
            sp.dma_start(w2a[:], w2t).then_inc(w2_in, 16)
            for i in range(6, 10):
                stage_load(i)
            for b in range(NB):
                for i in range(TT // 2):
                    sp.wait_ge(x_done, 2 * (2 * 3 + b) + i + 1)
                    sp.dma_start(ov[b][:, 2 * i:2 * i + 2, :], X[:, TT * b + 2 * i:TT * b + 2 * i + 2, :]).then_inc(out_done, 16)
            sp.wait_ge(out_done, 16 * TT)

        @block.gpsimd
        def _(pool):
            g = nc.gpsimd
            chain = [0]

            def link(ins):
                chain[0] += 1
                ins.then_inc(pool_chain, 1)
                pool.wait_ge(pool_chain, chain[0])

            def rope(n):
                t = n % TT
                read(pool, ("qk", n // TT, t))
                if n == 0:
                    pool.wait_ge(rope_done, 1)
                else:
                    pool.wait_ge(roped, n)
                for lo, hi in ((0, HALF), (HALF, 0)):
                    tab = rope_s[:, t, :, lo:lo + HALF].unsqueeze(2).broadcast_to([P, 2, NH, HALF])
                    last = g.tensor_tensor(rot[:, :, :, lo:lo + HALF], qn[:, t, :, :, hi:hi + HALF], tab, ALU.mult)
                link(last)
                pool.wait_ge(cos_done, n + 1)
                g.tensor_tensor(rr[:, t], rr[:, t], rot[:], ALU.add).then_inc(roped, 1)

            def gate_columns(l):
                pool.wait_ge(gateT_done, l + 1)
                if l:
                    filled(pool, ("gT", l - 1, 1))
                g.tensor_copy(g_cols[:],
                              gateT[:, l].unsqueeze(4).broadcast_to([P, 2, DC, NB, P])).then_inc(g_cols_done, 1)

            def split_stage(i):
                half = stage[:, i % 2]
                if i < 4 or i >= 6:
                    j = i % 4 if i < 4 else i - 6
                    hi_t, lo_t = (gua_hi, gua_lo) if j < 2 else (gub_hi, gub_lo)
                    j = j % 2
                else:
                    hi_t, lo_t, j = pj_hi, pj_lo, i - 4
                pool.wait_ge(stage_in[i % 2], 16 * (i // 2 + 1))
                link(g.tensor_copy(hi_t[:, 2 * j:2 * j + 2], half))
                g.tensor_tensor(lo_t[:, 2 * j:2 * j + 2], half, hi_t[:, 2 * j:2 * j + 2].bitcast(F32), ALU.subtract).then_inc(stage_split, 1)

            def causal(gr, s, i):
                read(pool, ("st", gr, s, i))
                if s == 0:
                    v = PTa[:, i, 0:P].unsqueeze(1)
                elif s == 1:
                    v = PTb[:, i, :].rearrange("p (c k) -> p c k", k=P)[:, 0:4:3, :]
                else:
                    v = PTc[:, 2 * i:2 * i + 2, 0:P]
                g.affine_select(out=v, in_=v, compare_op=ALU.is_ge, fill=0.0, base=0,
                                pattern=[[0, v.shape[1]], [1, P]], channel_multiplier=-1).then_inc(causal_done, 1)

            def comb(b, k):
                n = KC * b + k
                pool.wait_ge(y_done, n + 1)
                read(pool, ("gt", b, k))
                g.tensor_tensor(gt[b][:, k], yv[:, k % 2], gt[b][:, k], ALU.mult).then_inc(comb_done, 1)

            g.memset(vp[:, :, :, :, HD:32], 0.0).then_inc(pool_consts, 1)
            g.memset(qkp[:, :, :, :, SHIFT:SLOT].bitcast(F32), 0.0).then_inc(pool_consts, 1)
            g.memset(KT[:].bitcast(F32), 0.0).then_inc(pool_consts, 1)
            pool.wait_ge(pool_consts, 3)
            g.memset(vp[:, :, :, :, HD:HD + 1], 1.0).then_inc(pool_consts, 1)
            g.memset(qkp[:, :, 1, :, SHIFT:SHIFT + 1].bitcast(F32), 1.0).then_inc(pool_consts, 1)
            for n in range(TT):
                rope(n)
            gate_columns(0)
            gate_columns(1)
            for gr in range(NG):
                for s, n in ((0, 4), (1, 4), (2, 2)):
                    for i in range(n):
                        causal(gr, s, i)
                    if (gr, s) in ((0, 2), (1, 0), (1, 1), (1, 2)):
                        rope(TT + gr + s if gr else TT)
                if gr == GPB + 1:
                    split_stage(0)
                    split_stage(1)
                if gr == GPB + 2:
                    for j in range(2):
                        filled(pool, ("kT", NG - 1, j))
                    split_stage(2)
                    split_stage(3)
            split_stage(4)
            split_stage(5)
            pool.wait_ge(w2_in, 16)
            src, dst = w2a, w2b
            for r in range(3):
                s = 1 << r
                a = src[:].rearrange("p (m two s) d -> p m two (s d)", two=2, s=s)
                z = dst[:].rearrange("p (m two s) d -> p m two (s d)", two=2, s=s)
                g.tensor_tensor(z[:, :, 0], a[:, :, 0], a[:, :, 1], ALU.add)
                last = g.tensor_tensor(z[:, :, 1], a[:, :, 0], a[:, :, 1], ALU.subtract)
                if r < 2:
                    link(last)
                else:
                    last.then_inc(w2_mixed, 1)
                src, dst = dst, src
            filled(pool, ("up", 1, 1, FC // 2 - 1))
            split_stage(6)
            split_stage(7)
            for k in range(KC):
                comb(0, k)
            h_used(pool, 1, 1)
            split_stage(8)
            split_stage(9)
            for k in range(KC):
                comb(1, k)

        @block.scalar
        def _(act):
            a = nc.scalar
            chain = [0]

            def link(ins):
                chain[0] += 1
                ins.then_inc(act_chain, 1)
                act.wait_ge(act_chain, chain[0])

            def ln(n, b):
                i, l, k = 2 * n + b, n // 2, 2 * (n % 2)
                read(act, ("modT", l))
                if i:
                    act.wait_ge(h_done, i)
                if n:
                    h_used(act, n - 1, b)
                for c in range(DC):
                    u = ("ln", n, b, c)
                    filled(act, u)
                    sh, sc = modT[:, l, k, c, b:b + 1], modT[:, l, k + 1, c, b:b + 1]
                    a.activation(hf[:, c], ps(u)[:], ACT.Identity, bias=sh, scale=sc)
                    free(a.activation(h_hi[:, b, c], ps(u)[:], ACT.Identity, bias=sh, scale=sc), u)

            def qkv_in(n):
                b, t = n // TT, n % TT
                u, v = ("qk", b, t), ("v", b, t)
                filled(act, u)
                if b:
                    act.wait_ge(roped, n - TT + 1)
                a.activation(sq[:, t].rearrange("p a h d -> p (a h d)"), ps(u)[:], ACT.Square).then_inc(sq_done, 1)
                free(a.copy(qn[:, t].rearrange("p a h d -> p (a h d)"), ps(u)[:]), u)
                filled(act, v)
                if n == 0:
                    act.wait_ge(pool_consts, NCONST)
                free(a.copy(vp[:, b, t, :, 0:HD], ps(v)[:, 0:D].rearrange("p (h d) -> p h d", d=HD)), v)

            def qk_hi(n):
                t = n % TT
                act.wait_ge(scaled, n + 1)
                if n == TT:
                    filled(act, ("kT", GPB - 1, 1))
                a.copy(qkp[:, t, :, :, 0:HD], rr[:, t])
                a.copy(qkp[:, t, 0, :, 2 * HD:3 * HD], rr[:, t, 0])
                a.copy(qkp[:, t, 1, :, HD:2 * HD], rr[:, t, 1]).then_inc(qk_high, 1)

            def gates_out(l):
                for w in range(2):
                    u = ("gT", l, w)
                    filled(act, u)
                    free(a.copy(gates[:, l, w].rearrange("p b d -> p (b d)"), ps(u)[:]), u)

            def heads_out(gr):
                if gr >= 2:
                    filled(act, ("st", gr - 2, 2, 1))
                for j in range(2):
                    u, w = ("qT", gr, j), ("kT", gr, j)
                    filled(act, u)
                    free(a.copy(QT[:, gr % 2, j], ps(u)[:]), u)
                    filled(act, w)
                    a.copy(KT[0:SLOT, gr % 2, j, 0], ps(w)[0:SLOT])
                    free(a.copy(KT[SLOT:P, gr % 2, j, 1], ps(w)[SLOT:P]), w)

            def exps(gr, s):
                if gr:
                    act.wait_ge(pv_done, 3 * (gr - 1) + s + 1)
                for i in range((4, 4, 2)[s]):
                    u = ("st", gr, s, i)
                    filled(act, u)
                    if s < 2:
                        dst, src = PT[s][:, i], ps(u)[:]
                    else:
                        dst, src = PTc[:, 2 * i:2 * i + 2], ps(u)[:].rearrange("p (h q) -> p h q", h=2)
                    free(a.activation(dst, src, ACT.Exp), u)

            def aT_out(b):
                if b:
                    filled(act, ("y", 0, b - 1, 1))
                for c in range(DC):
                    u = ("aT", b, c)
                    filled(act, u)
                    free(a.copy(aT[:, c], ps(u)[:]), u)

            def gu(n, b, f):
                u = ("gate", n, b, f)
                filled(act, u)
                prev = f - 2 + FC * b
                if prev >= 0:
                    read(act, ("up", n, prev // FC, prev % FC))
                free(a.activation(sg[:, f % 2], ps(u)[:], ACT.Silu), u)

            def absolute(b, gb):
                n = GB * b + gb
                read(act, ("up", 1, b, 4 * gb + 3))
                if n:
                    act.wait_ge(abs_used, n)
                a.activation(ab[:], H[:, b, 4 * gb:4 * gb + 4], ACT.Abs).then_inc(abs_done, 1)

            def proj(b):
                if b == 0:
                    act.wait_ge(chan_in, 48)
                filled(act, ("y", 1, b, 1))
                for k in range(KC):
                    n = KC * b + k
                    u = ("pj", b, k)
                    filled(act, u)
                    if n >= 2:
                        act.wait_ge(xc_done, n - 1)
                    a.activation(acc[:, k % 2], ps(u)[:], ACT.Identity, bias=ch[:, k, S_BIAS:S_BIAS + 1],
                                 scale=ch[:, k, S_CONV + TAPS - 1:S_CONV + TAPS]).then_inc(conv_begun, 1)
                    if k:
                        conv_out(b, k - 1)
                conv_out(b, KC - 1)
                for k in range(KC):
                    u = ("gt", b, k)
                    filled(act, u)
                    free(a.activation(gt[b][:, k], ps(u)[:], ACT.Sigmoid), u)

            def conv_out(b, k):
                read(act, ("pj", b, k))
                a.activation(xc[b][:, k], acc[:, k % 2], ACT.Silu).then_inc(xc_done, 1)

            def softplus(b):
                u = ("dt", b)
                filled(act, u)
                if b:
                    act.wait_ge(dts_done, b)
                a.activation(sp_z[:], ps(u)[0:SH], ACT.Identity, bias=dtb_s[:, 0:1])
                last = a.activation(sp_a[:], ps(u)[0:SH], ACT.Abs, bias=dtb_s[:, 0:1])
                free(last, u)
                read(act, u)
                a.activation(sp_e[:], sp_a[:], ACT.Exp, scale=-1.0).then_inc(sp_e_done, 1)
                act.wait_ge(sp_e_done, b + 1)
                a.activation(sp_l[:], sp_e[:], ACT.Ln, bias=1.0).then_inc(sp_l_done, 1)

            def spread(b):
                if b == 0:
                    link(a.activation(neg_a[:], ch[:, :, S_ALOG], ACT.Exp))
                    link(a.mul(neg_a[:], neg_a[:], -1.0))
                for k in range(KC):
                    n = KC * b + k
                    u = ("spread", b, k)
                    filled(act, u)
                    if n >= 2:
                        act.wait_ge(y_done, n - 1)
                    a.activation(decay[:, k % 2], ps(u)[:], ACT.Exp, scale=neg_a[:, k:k + 1]).then_inc(decay_done, 1)
                    a.activation(skip[:, k % 2], xc[b][:, k], ACT.Copy, scale=ch[:, k, S_D:S_D + 1]).then_inc(skip_done, 1)

            act.wait_ge(c_in, 16)
            a.activation(silu_c[:], c_s[:], ACT.Silu).then_inc(silu_c_done, 1)
            act.wait_ge(wq_in, 16)
            a.copy(wq_hi[:], wq_raw[:]).then_inc(wq_split_hi, 1)
            ln(0, 0)
            for n in range(TT):
                qkv_in(n)
            qk_hi(0)
            qk_hi(1)
            ln(0, 1)
            qk_hi(2)
            qk_hi(3)
            gates_out(0)
            heads_out(0)
            gates_out(1)
            heads_out(1)
            for gr in range(NG):
                for s in range(3):
                    exps(gr, s)
                    if gr < 2 and s < 2:
                        qkv_in(TT + 2 * gr + s)
                    if gr == 2 and s < 2:
                        qk_hi(TT + 2 * s)
                        qk_hi(TT + 2 * s + 1)
                    if gr == GPB and s == 0:
                        aT_out(0)
                    if gr == GPB + 1 and s == 1:
                        ln(1, 0)
                if gr + 2 < NG:
                    heads_out(gr + 2)
            for b in range(NB):
                for f in range(FC):
                    gu(1, b, f)
                    if b == 0 and f == 2:
                        aT_out(1)
                    if f % 4 == 1 and (b or f > 1):
                        n = GB * b + f // 4 - 1
                        absolute(n // GB, n % GB)
                    if b == 0 and f == 6:
                        ln(1, 1)
            absolute(1, 1)
            ln(2, 0)
            proj(0)
            for i in range(FC // 2):
                u = ("had", i)
                filled(act, u)
                free(a.mul(w2a[:, 2 * i:2 * i + 2], ps(u)[:].rearrange("p (c d) -> p c d", c=2), 1.0 / HID ** 0.5), u)
            softplus(0)
            ln(2, 1)
            proj(1)
            spread(0)
            softplus(1)
            spread(1)
            ln(3, 0)
            for b in range(NB):
                for f in range(FC):
                    gu(3, b, f)
                    if b == 0 and f == 6:
                        ln(3, 1)

        @block.vector
        def _(dve):
            v = nc.vector
            chain = [0]

            def link(ins):
                chain[0] += 1
                ins.then_inc(dve_chain, 1)
                dve.wait_ge(dve_chain, chain[0])

            def rsqrt(y, x, t):
                link(v.tensor_scalar(y.bitcast(I32), x.bitcast(I32), -0.5, RSQRT_GUESS, ALU.mult, ALU.add))
                for _ in range(3):
                    link(v.tensor_tensor(t, y, y, ALU.mult))
                    link(v.scalar_tensor_tensor(t, t, -0.5, x, ALU.mult, ALU.mult))
                    link(v.scalar_tensor_tensor(y, t, 1.5, y, ALU.add, ALU.mult))

            def ln_stats(n, b):
                i = 2 * n + b
                if n == 0:
                    dve.wait_ge(x_in[b], 16)
                if i:
                    dve.wait_ge(xn_done, i)
                for t in range(TT):
                    last = v.bn_stats(stats[:, t], X[:, TT * b + t])
                link(last)
                for t in range(TT):
                    last = v.bn_aggr(mv[:, t], stats[:, t])
                link(last)
                link(v.tensor_scalar(ln_ve[:], mv[:, :, 1], LN_EPS, None, ALU.add))
                rsqrt(ln_rs[:], ln_ve[:], nt[:, 0:TT])
                if i:
                    filled(dve, ("ln", (i - 1) // 2, (i - 1) % 2, DC - 1))
                for t in range(TT):
                    last = v.tensor_scalar(xn[:, t], X[:, TT * b + t], mv[:, t, 0:1], ln_rs[:, t:t + 1], ALU.subtract, ALU.mult)
                last.then_inc(xn_done, 1)

            def ln_lo(n, b):
                i = 2 * n + b
                read(dve, ("ln", n, b, DC - 1))
                v.tensor_tensor(h_lo[:, b], hf[:], h_hi[:, b].bitcast(F32), ALU.subtract).then_inc(h_done, 1)

            def mod_out(l):
                u = ("modT", l)
                filled(dve, u)
                m = ps(u)[:, 0:24].rearrange("p (k c b) -> p k c b", k=6, c=DC)
                v.tensor_copy(modT[:, l, 0:4:2], m[:, 0:6:3])
                v.tensor_scalar(modT[:, l, 1:4:2], m[:, 1:6:3], 1.0, None, ALU.add)
                gv = m[:, 2:6:3]
                v.tensor_scalar(g_tmp[:, 0], gv, 0.25, None, ALU.max)
                v.tensor_scalar(g_tmp[:, 1], gv, -1.0, 0.25, ALU.mult, ALU.max)
                free(v.tensor_scalar(g_tmp[:, 2], gv, 0.0, 2.0, ALU.is_ge, ALU.mult), u)
                read(dve, u)
                link(v.tensor_tensor(g_tmp[:, 0], g_tmp[:, 0], g_tmp[:, 1], ALU.max))
                v.scalar_tensor_tensor(gateT[:, l], g_tmp[:, 2], -1.0, g_tmp[:, 0], ALU.add, ALU.mult).then_inc(gateT_done, 1)
                dve.wait_ge(gateT_done, l + 1)

            def rope_tables():
                dve.wait_ge(gam_in, 16)
                dve.wait_ge(cst_in, 16)
                for w in range(2):
                    s = HD ** -0.5 if w == 0 else 1.0
                    gm = gam[:, w].unsqueeze(1)
                    v.scalar_tensor_tensor(rope_c[:, :, w], cosv, s, gm.broadcast_to([P, TT, HD]), ALU.mult, ALU.mult)
                    for o, g0, sign in ((0, HALF, -1.0), (HALF, 0, 1.0)):
                        gs = gam[:, w, g0:g0 + HALF].unsqueeze(1).broadcast_to([P, TT, HALF])
                        last = v.scalar_tensor_tensor(rope_s[:, :, w, o:o + HALF], sinv[:, :, o:o + HALF], s * sign, gs, ALU.mult, ALU.mult)
                last.then_inc(rope_done, 1)

            def rms_cos(n):
                b, t = n // TT, n % TT
                dve.wait_ge(sq_done, n + 1)
                link(v.tensor_reduce(qk_ss[:, t], sq[:, t].rearrange("p a h d -> p (a h) d"), AX.X, ALU.add))
                read(dve, ("qk", b, t))
                if n == 0:
                    dve.wait_ge(rope_done, 1)
                tab = rope_c[:, t].unsqueeze(2).broadcast_to([P, 2, NH, HD])
                if b:
                    dve.wait_ge(qk_split, n - TT + 1)
                v.tensor_tensor(rr[:, t], qn[:, t], tab, ALU.mult).then_inc(cos_done, 1)

            def rms_scale(b, lo, hi):
                x = qk_ss[:, lo:hi].rearrange("p t h -> p (t h)")
                y = qk_rs[:, lo:hi].rearrange("p t h -> p (t h)")
                link(v.tensor_scalar(x, x, 1.0 / HD, RMS_EPS, ALU.mult, ALU.add))
                rsqrt(y, x, nt[:, 0:(hi - lo) * 2 * NH])
                for t in range(lo, hi):
                    dve.wait_ge(roped, TT * b + t + 1)
                    q = rr[:, t].rearrange("p a h d -> p (a h) d")
                    v.tensor_tensor(q, q, qk_rs[:, t].unsqueeze(2).broadcast_to([P, 2 * NH, HD]), ALU.mult).then_inc(scaled, 1)

            def qk_lo(n):
                t = n % TT
                dve.wait_ge(qk_high, n + 1)
                v.tensor_tensor(qkp[:, t, 0, :, HD:2 * HD], rr[:, t, 0], qkp[:, t, 0, :, 0:HD].bitcast(F32), ALU.subtract)
                v.tensor_tensor(qkp[:, t, 1, :, 2 * HD:3 * HD], rr[:, t, 1], qkp[:, t, 1, :, 0:HD].bitcast(F32),
                                ALU.subtract).then_inc(qk_split, 1)

            def maxima(gr, lo=0, hi=HPG * TT):
                for h in range(HPG):
                    for t in range(TT):
                        if not lo <= TT * h + t < hi:
                            continue
                        u = ("mx", gr, h, t)
                        n = P * (t + 1)
                        filled(dve, u)
                        m = TT * h + t + TT * HPG * gr
                        if m >= 3:
                            read(dve, ("mx", (m - 3) // (TT * HPG), (m - 3) // TT % HPG, (m - 3) % TT))
                        free(v.tensor_tensor_reduce(out=junk[:, m % 3, 0:n], in0=ps(u)[:, 0:n], in1=mask[:, SEQ - n:SEQ], scale=1.0,
                                                    scalar=LOWEST, op0=ALU.add, op1=ALU.max,
                                                    accum_out=mx[:, gr % 2, t, h:h + 1]), u)

            def negate(gr):
                u = ("maxT", gr)
                filled(dve, u)
                if gr:
                    dve.wait_ge(shift_in[(gr - 1) % 2], 16 * HPG * ((gr - 1) // 2 + 1))
                free(v.tensor_scalar(negm[:], ps(u)[0:HPG], -1.0, None, ALU.mult), u)

            def pv_out(gr):
                dve.wait_ge(pv_done, 3 * gr + 3)
                if gr:
                    filled(dve, ("oN", gr - 1))
                v.tensor_copy(oT[:], pv_bank[:]).then_inc(pv_free, 1)

            def normalise(gr):
                u = ("oN", gr)
                gb = gr % GPB
                filled(dve, u)
                if gr == 0:
                    filled(dve, ("gT", 1, 1))
                if gr == GPB:
                    filled(dve, ("aT", 0, DC - 1))
                if gr:
                    read(dve, ("oN", gr - 1))
                m = ps(u)[:].rearrange("p (t h e) -> p t h e", t=TT, h=HPG)
                link(v.reciprocal(rc[:], m[:, :, :, HD]))
                dst = att[:, :, gb * HPG * HD:(gb + 1) * HPG * HD].rearrange("p t (h d) -> p t h d", d=HD)
                free(v.tensor_tensor(dst, m[:, :, :, 0:HD], rc[:].unsqueeze(3).broadcast_to([P, TT, HPG, HD]), ALU.mult), u)

            def residual(n, b):
                l, k = n // 2, n % 2
                for i in range(TT // 2):
                    u = ("y", n, b, i)
                    filled(dve, u)
                    if 2 * (2 * n + b) + i:
                        dve.wait_ge(x_done, 2 * (2 * n + b) + i)
                    gt_b = gates[:, l, k, b].unsqueeze(1).broadcast_to([P, 2, D])
                    free(v.tensor_tensor(yt[:], ps(u)[:].rearrange("p (t d) -> p t d", t=2), gt_b, ALU.mult), u)
                    read(dve, u)
                    xs = X[:, TT * b + 2 * i:TT * b + 2 * i + 2]
                    v.tensor_tensor(xs, xs, yt[:], ALU.add).then_inc(x_done, 1)
                dve.wait_ge(x_done, 2 * (2 * n + b) + 2)

            def hidden(n, b, f):
                u = ("up", n, b, f)
                filled(dve, u)
                read(dve, ("gate", n, b, f))
                free(v.tensor_tensor(H[:, b, f], ps(u)[:], sg[:, f % 2], ALU.mult), u)

            def sparsify(b, gb, part):
                n = GB * b + gb
                if part == 0:
                    dve.wait_ge(abs_done, n + 1)
                    ev, od = ab[:, 0:4:2], ab[:, 1:4:2]
                    v.tensor_tensor(pair_hi[:], ev, od, ALU.max)
                    v.tensor_tensor(pair_lo[:], ev, od, ALU.min)
                if part == 1:
                    ev, od = ab[:, 0:4:2], ab[:, 1:4:2]
                    v.tensor_tensor(odd_wins[:], od, ev, ALU.is_gt).then_inc(abs_used, 1)
                    dve.wait_ge(abs_used, n + 1)
                    v.tensor_tensor(both[:, 0], pair_lo[:, 0], pair_hi[:, 1], ALU.is_ge)
                    link(v.tensor_tensor(both[:, 1], pair_lo[:, 1], pair_hi[:, 0], ALU.is_gt))
                if part == 2:
                    if n:
                        dve.wait_ge(sparse_done, n)
                    link(v.tensor_tensor(lean[:], both[:, 0], both[:, 1], ALU.subtract))
                    ln2 = lean[:].unsqueeze(1).broadcast_to([P, 2, SEQ])
                    v.tensor_tensor(d_sub[:], ln2, odd_wins[:], ALU.subtract)
                    link(v.tensor_tensor(d_add[:], ln2, odd_wins[:], ALU.add))
                if part == 3:
                    for j, (d, thr, op) in enumerate(((d_sub[:, 0], 0.0, ALU.is_ge), (d_add[:, 0], 1.0, ALU.is_ge),
                                                      (d_add[:, 1], 0.0, ALU.is_le), (d_sub[:, 1], -1.0, ALU.is_le))):
                        hj = H[:, b, 4 * gb + j]
                        last = v.scalar_tensor_tensor(hj, d, thr, hj, op, ALU.mult)
                    last.then_inc(sparse_done, 1)

            def conv(b):
                dve.wait_ge(chan_in, 48)
                for k in range(KC):
                    n = KC * b + k
                    u = ("pj", b, k)
                    dve.wait_ge(conv_begun, n + 1)
                    for j in range(TAPS - 2, -1, -1):
                        s = TAPS - 1 - j
                        last = v.scalar_tensor_tensor(acc[:, k % 2, s:SEQ], ps(u)[:, 0:SEQ - s], ch[:, k, S_CONV + j:S_CONV + j + 1],
                                                      acc[:, k % 2, s:SEQ], ALU.mult, ALU.add)
                        if j:
                            link(last)
                        else:
                            free(last, u)

            def softplus(b):
                dve.wait_ge(sp_e_done, b + 1)
                if b:
                    dve.wait_ge(dts_done, b)
                    filled(dve, ("spread", b - 1, KC - 1))
                link(v.tensor_scalar(sp_u[:], sp_e[:], 1.0, -1.0, ALU.add, ALU.add))
                link(v.tensor_tensor(sp_c[:], sp_e[:], sp_u[:], ALU.subtract))
                dve.wait_ge(sp_l_done, b + 1)
                link(v.tensor_tensor(sp_u[:], sp_l[:], sp_c[:], ALU.add))
                link(v.scalar_tensor_tensor(sp_c[:], sp_z[:], 0.0, sp_u[:], ALU.max, ALU.add))
                link(v.tensor_copy(dts[0:SH], sp_c[:]))
                v.tensor_tensor(dts[32:32 + SH], sp_c[:], dts[0:SH].bitcast(F32), ALU.subtract).then_inc(dts_done, 1)

            def mix(b):
                for k in range(KC):
                    n = KC * b + k
                    u = ("spread", b, k)
                    filled(dve, u)
                    dve.wait_ge(decay_done, n + 1)
                    free(v.scalar_tensor_tensor(drive[:], ps(u)[:], ch[:, k, S_B:S_B + 1], xc[b][:, k], ALU.mult, ALU.mult), u)
                    read(dve, u)
                    if n:
                        dve.wait_ge(y_done, n)
                    link(v.tensor_tensor_scan(state[:], decay[:, k % 2], drive[:], 0.0, ALU.mult, ALU.add))
                    dve.wait_ge(skip_done, n + 1)
                    if n >= 2:
                        dve.wait_ge(comb_done, n - 1)
                    v.scalar_tensor_tensor(yv[:, k % 2], state[:], ch[:, k, S_C:S_C + 1], skip[:, k % 2], ALU.mult, ALU.add).then_inc(y_done, 1)

            ln_stats(0, 0)
            dve.wait_ge(wq_split_hi, 1)
            v.tensor_tensor(wq_lo[:], wq_raw[:], wq_hi[:].bitcast(F32), ALU.subtract).then_inc(wq_split, 1)
            mod_out(0)
            ln_lo(0, 0)
            rope_tables()
            ln_stats(0, 1)
            rms_cos(0)
            rms_cos(1)
            rms_scale(0, 0, 2)
            rms_cos(2)
            rms_cos(3)
            qk_lo(0)
            qk_lo(1)
            rms_scale(0, 2, 4)
            mod_out(1)
            qk_lo(2)
            ln_lo(0, 1)
            qk_lo(3)
            dve.wait_ge(sel_in, 16)
            v.tensor_copy(sel[:], sel_raw[:]).then_inc(sel_done, 1)
            maxima(0)
            negate(0)
            for gr in range(NG):
                if gr + 1 < NG:
                    maxima(gr + 1, 0, 4)
                if gr:
                    normalise(gr - 1)
                if gr == GPB + 1:
                    ln_stats(1, 0)
                if gr + 1 < NG:
                    if gr == 2:
                        rms_scale(1, 0, TT)
                    maxima(gr + 1, 4, 8)
                    if gr == 1:
                        rms_cos(TT + 2)
                    if gr == 2:
                        qk_lo(TT)
                        qk_lo(TT + 1)
                    maxima(gr + 1, 8, 11)
                    if gr == 0:
                        rms_cos(TT)
                        rms_cos(TT + 1)
                    if gr == 1:
                        rms_cos(TT + 3)
                    if gr == 2:
                        qk_lo(TT + 2)
                        qk_lo(TT + 3)
                    if gr == GPB + 1:
                        ln_lo(1, 0)
                    maxima(gr + 1, 11, 16)
                    negate(gr + 1)
                    pv_out(gr)
                    if gr == GPB:
                        residual(0, 0)
            pv_out(NG - 1)
            todo = []
            for b in range(NB):
                for f in range(FC):
                    hidden(1, b, f)
                    if todo:
                        sparsify(*todo.pop(0))
                    if f % 4 == 3:
                        todo += [(b, f // 4, part) for part in range(4)]
                    if b == 0 and f == 1:
                        normalise(NG - 1)
                    if b == 0 and f == 3:
                        residual(0, 1)
                        ln_stats(1, 1)
                    if b == 0 and f == 6:
                        ln_lo(1, 1)
                    if b == 1 and f == 4:
                        residual(1, 0)
                        ln_stats(2, 0)
            for td in todo:
                sparsify(*td)
            ln_lo(2, 0)
            v.memset(dts[:].bitcast(F32), 0.0)
            conv(0)
            residual(1, 1)
            ln_stats(2, 1)
            softplus(0)
            ln_lo(2, 1)
            conv(1)
            mix(0)
            softplus(1)
            residual(2, 0)
            ln_stats(3, 0)
            mix(1)
            ln_lo(3, 0)
            for b in range(NB):
                for f in range(FC):
                    hidden(3, b, f)
                    if b == 0 and f == 3:
                        residual(2, 1)
                        ln_stats(3, 1)
                    if b == 0 and f == 6:
                        ln_lo(3, 1)
                    if b == 1 and f == 4:
                        residual(3, 0)
            residual(3, 1)

        @block.tensor
        def _(pe):
            mm, tr = nc.tensor.matmul, nc.tensor.transpose

            def mm3(dst, a_hi, a_lo, b_hi, b_lo, first, last):
                mm(dst, a_hi, b_hi, start=first, stop=False)
                mm(dst, a_hi, b_lo, start=False, stop=False)
                return mm(dst, a_lo, b_hi, start=False, stop=last)

            def ln(n, b):
                pe.wait_ge(xn_done, 2 * n + b + 1)
                if n == 0 and b == 0:
                    pe.wait_ge(cst_in, 16)
                for c in range(DC):
                    u = ("ln", n, b, c)
                    claim(pe, u)
                    for t in range(TT):
                        last = tr(ps(u)[:, P * t:P * t + P], xn[:, t, P * c:P * c + P], ident)
                    fill(last, u)

            def mod_T(l):
                pe.wait_ge(wmod_in[l], 16)
                pe.wait_ge(silu_c_done, 1)
                u = ("modT", l)
                claim(pe, u)
                for kind in range(6):
                    for c in range(DC):
                        o = 2 * (DC * kind + c)
                        for kc in range(DC):
                            last = mm(ps(u)[:, o:o + NB], wmod_s[:, l, kc, D * kind + P * c:D * kind + P * c + P],
                                      silu_c[:, l, kc], start=kc == 0, stop=kc == DC - 1)
                fill(last, u)

            def gates_T(l):
                pe.wait_ge(g_cols_done, l + 1)
                for w in range(2):
                    u = ("gT", l, w)
                    claim(pe, u)
                    for b in range(NB):
                        for c in range(DC):
                            o = D * b + P * c
                            last = tr(ps(u)[:, o:o + P], g_cols[:, w, c, b], ident)
                    fill(last, u)

            def qkv(b, t):
                if t == 0:
                    pe.wait_ge(h_done, b + 1)
                    pe.wait_ge(wq_split, 1)
                for u, o, n in ((("qk", b, t), 0, 2 * D), (("v", b, t), 2 * D, D)):
                    claim(pe, u)
                    for c in range(DC):
                        ts = slice(P * t, P * t + P)
                        last = mm3(ps(u)[:, 0:n], h_hi[:, b, c, ts], h_lo[:, b, c, ts],
                                   wq_hi[:, c, o:o + n], wq_lo[:, c, o:o + n], c == 0, c == DC - 1)
                    fill(last, u)

            def heads(gr):
                b, g4 = gr // GPB, gr % GPB
                pe.wait_ge(qk_split, TT * (b + 1))
                if gr == 0:
                    pe.wait_ge(pool_consts, NCONST)
                for j in range(2):
                    for w, nm in enumerate(("qT", "kT")):
                        u = (nm, gr, j)
                        claim(pe, u)
                        for t in range(TT):
                            h0 = HPG * g4 + 2 * j
                            last = tr(ps(u)[:, P * t:P * t + P], qkp[:, t, w, h0:h0 + 2, :].rearrange("p h e -> p (h e)").bitcast(F32), ident)
                        fill(last, u)

            def score_max(gr, h, t):
                u = ("mx", gr, h, t)
                claim(pe, u)
                s = gr % 2
                if h % 2 == 0 and t == 0:
                    read(pe, ("qT", gr, h // 2))
                    read(pe, ("kT", gr, h // 2))
                fill(mm(ps(u)[:, 0:P * (t + 1)], QT[:, s, h // 2, P * t:P * t + P], KT[:, s, h // 2, h % 2, 0:P * (t + 1)],
                        start=True, stop=True), u)

            def max_T(gr):
                u = ("maxT", gr)
                read(pe, ("mx", gr, HPG - 1, TT - 1))
                claim(pe, u)
                for t in range(TT):
                    last = tr(ps(u)[0:HPG, P * t:P * t + P], mx[:, gr % 2, t], ident)
                fill(last, u)

            def scores(gr, s, i):
                u = ("st", gr, s, i)
                w = gr % 2
                claim(pe, u)
                if s == 0 and i == 0:
                    pe.wait_ge(shift_in[w], 16 * HPG * (gr // 2 + 1))
                parts = (((i, 0, 0),), ((i, 1, 0), (i, 3, 384)), ((2 * i, 2, 0), (2 * i + 1, 2, 256)))[s]
                for h, c, o in parts:
                    n = SEQ - P * c
                    last = mm(ps(u)[:, o:o + n], KT[:, w, h // 2, h % 2, P * c:P * c + P], QT[:, w, h // 2, P * c:SEQ],
                              start=True, stop=True)
                fill(last, u)

            def probs_v(gr, s):
                b = gr // GPB
                pe.wait_ge(causal_done, 10 * gr + (4, 8, 10)[s])
                if s == 0 and gr:
                    pe.wait_ge(pv_free, gr)
                for c in ((0,), (1, 3), (2,))[s]:
                    o = 384 if c == 3 else 0
                    n = SEQ - P * c
                    for h in range(HPG):
                        last = mm(pv_bank[32 * h:32 * h + 32, P * c:SEQ], vp[:, b, c, HPG * (gr % GPB) + h, :],
                                  PT[s][:, h, o:o + n], start=c == 0, stop=c == 2, tile_position=(0, 32 * h))
                last.then_inc(pv_done, 1)

            def out_T(gr):
                u = ("oN", gr)
                pe.wait_ge(pv_free, gr + 1)
                claim(pe, u)
                for t in range(TT):
                    last = tr(ps(u)[:, P * t:P * t + P], oT[:, P * t:P * t + P], ident)
                fill(last, u)

            def att_T(b):
                read(pe, ("oN", GPB * b + GPB - 1))
                for c in range(DC):
                    u = ("aT", b, c)
                    claim(pe, u)
                    for t in range(TT):
                        last = tr(ps(u)[:, P * t:P * t + P], att[:, t, P * c:P * c + P], ident)
                    fill(last, u)

            def down(n, b):
                if n == 0:
                    pe.wait_ge(wout_in, 16)
                    read(pe, ("aT", b, DC - 1))
                    srcs = [(aT[:, c], wout_s[:, c]) for c in range(DC)]
                elif n == 1:
                    pe.wait_ge(wdn_in, 16)
                    pe.wait_ge(sparse_done, GB * (b + 1))
                    srcs = [(H[:, b, f], wdn_s[:, f]) for f in range(FC)]
                elif n == 2:
                    pe.wait_ge(woutp_in, 16)
                    pe.wait_ge(comb_done, KC * (b + 1))
                    srcs = [(gt[b][:, k], woutp_s[:, k]) for k in range(KC)]
                else:
                    read(pe, ("had", FC // 2 - 1))
                    read(pe, ("up", 3, b, FC - 1))
                    srcs = [(H[:, b, f], w2a[:, f]) for f in range(FC)]
                for i in range(TT // 2):
                    u = ("y", n, b, i)
                    claim(pe, u)
                    for tt in range(2):
                        t = 2 * i + tt
                        for j, (act_t, w) in enumerate(srcs):
                            last = mm(ps(u)[:, D * tt:D * tt + D], act_t[:, P * t:P * t + P], w, start=j == 0, stop=j == len(srcs) - 1)
                    fill(last, u)

            def gate_up(n, b, f):
                if f == 0:
                    pe.wait_ge(h_done, 2 * n + b + 1)
                if f % 2 == 0 and b == 0:
                    pe.wait_ge(stage_split, (1 if n == 1 else 7) + f // 2)
                hi, lo = (gua_hi, gua_lo) if f < 4 else (gub_hi, gub_lo)
                for w, nm in enumerate(("gate", "up")):
                    u = (nm, n, b, f)
                    claim(pe, u)
                    for c in range(DC):
                        last = mm3(ps(u)[:], hi[:, f % 4, w, c], lo[:, f % 4, w, c], h_hi[:, b, c], h_lo[:, b, c], c == 0, c == DC - 1)
                    fill(last, u)

            def proj(b):
                pe.wait_ge(h_done, 4 + b + 1)
                pe.wait_ge(stage_split, 6)
                for k in range(KC):
                    for w, nm in enumerate(("pj", "gt")):
                        u = (nm, b, k)
                        claim(pe, u)
                        for c in range(DC):
                            last = mm3(ps(u)[:], pj_hi[:, k, w, c], pj_lo[:, k, w, c], h_hi[:, b, c], h_lo[:, b, c], c == 0, c == DC - 1)
                        fill(last, u)

            def dt(b):
                u = ("dt", b)
                claim(pe, u)
                pe.wait_ge(chan_in, 48)
                pe.wait_ge(xc_done, KC * (b + 1))
                for k in range(KC):
                    last = mm(ps(u)[0:SH], dtw_s[:, k], xc[b][:, k], start=k == 0, stop=k == KC - 1)
                fill(last, u)

            def spread(b):
                pe.wait_ge(dts_done, b + 1)
                pe.wait_ge(sel_done, 1)
                for k in range(KC):
                    u = ("spread", b, k)
                    claim(pe, u)
                    fill(mm(ps(u)[:], sel[:, k], dts[:], start=True, stop=True), u)

            def hadamard():
                pe.wait_ge(w2_mixed, 1)
                for i in range(FC // 2):
                    u = ("had", i)
                    claim(pe, u)
                    for c in range(2):
                        last = mm(ps(u)[:, D * c:D * c + D], had, w2b[:, 2 * i + c], start=True, stop=True)
                    fill(last, u)

            run = {"ln": ln, "modT": mod_T, "gT": gates_T, "qkv": qkv, "T": heads, "mx": score_max, "maxT": max_T, "st": scores, "pv": probs_v,
                   "oN": out_T, "aT": att_T, "y": down, "gu": gate_up, "proj": proj, "dt": dt, "spread": spread, "had": hadamard}
            for s in stages:
                run[s[0]](*s[1:])


def shape_constants():
    c = np.zeros((P, C_END), np.float32)
    c[:, C_ID:C_HAD] = np.eye(P, dtype=np.float32)
    i = np.arange(P)
    par = np.array([[bin(a & b).count("1") & 1 for b in i] for a in i])
    c[:, C_HAD:C_MASK] = 1 - 2 * par
    tri = np.where(i[None, :] > i[:, None], NEG, 0.0)
    c[:, C_COS - P:C_COS] = tri
    inv = (1.0 / 10000.0 ** (np.arange(0, HD, 2, dtype=np.float32) / HD)).astype(np.float32)
    fr = np.arange(SEQ, dtype=np.float32)[:, None] * inv[None, :]
    emb = np.concatenate([fr, fr], -1)
    for o, f in ((C_COS, np.cos), (C_SIN, np.sin)):
        c[:, o:o + TT * HD] = f(emb).reshape(TT, P, HD).transpose(1, 0, 2).reshape(P, TT * HD)
    return c


def spreading():
    c = np.zeros((P, KC, P), np.float32)
    for k in range(KC):
        for m in range(P):
            h = (P * k + m) // SHD
            c[h, k, m] = c[32 + h, k, m] = 1
    return c


def kernel(**inputs):
    import concourse.bacc as _bacc
    from concourse.bass_utils import run_bass_kernel_spmd as _run

    w = {k: np.asarray(v) for k, v in inputs.items()}

    def rows(a):
        return a.reshape(-1, P, a.shape[-1]).transpose(1, 0, 2)

    def pair_up(a, b):
        both = np.stack([a, b]).reshape(2, DC, P, -1, P)
        return both.transpose(2, 3, 0, 1, 4)

    order = np.arange(HID).reshape(GB, P, 4).transpose(0, 2, 1).reshape(-1)
    chan = np.concatenate([w["L1_attn_conv_weight"]] + [w["L1_attn_" + n].reshape(INNER, 1)
                          for n in ("conv_bias", "A_log", "B", "C", "D")], axis=1)
    dtw = np.zeros((INNER, SH), np.float32)
    for h in range(SH):
        dtw[SHD * h:SHD * (h + 1), h] = w["L1_attn_dt_w"][h]
    arrays = {
        "x": w["L0_attn_x"].reshape(NB * SEQ, D),
        "wqkv": rows(w["L0_attn_w_qkv"]),
        "wout": rows(w["L0_attn_w_out"]),
        "gammas": np.tile(np.stack([w["L0_attn_q_gamma"], w["L0_attn_k_gamma"]])[None], (P, 1, 1)),
        "wgu0": pair_up(w["L0_ffn_w_gate"][:, order], w["L0_ffn_w_up"][:, order]),
        "wdn0": rows(w["L0_ffn_w_down"][order]),
        "wmod": np.stack([rows(w["L0_wmod"]), rows(w["L1_wmod"])], axis=1),
        "cT": np.stack([rows(w["L0_c"].T), rows(w["L1_c"].T)], axis=1),
        "wproj": pair_up(w["L1_attn_in_proj_w"].T, w["L1_attn_gate_proj_w"].T),
        "woutp": rows(w["L1_attn_out_proj_w"].T),
        "chan": rows(chan),
        "dtw": rows(dtw),
        "dtb": w["L1_attn_dt_b"].reshape(SH, 1),
        "wgu1": pair_up(w["L1_ffn_W1"].T, w["L1_ffn_W3"].T),
        "w2t": rows(w["L1_ffn_W2"].T),
        "consts": shape_constants(),
        "spread_sel": spreading(),
    }
    arrays = {f"in_{k}": np.ascontiguousarray(v) for k, v in arrays.items()}
    nc = _bacc.Bacc("TRN2", target_bir_lowering=False, num_devices=1)
    args = [nc.dram_tensor(k, v.shape, mybir.dt.from_np(v.dtype), kind="ExternalInput").ap() for k, v in arrays.items()]
    out = nc.dram_tensor("out_0", (NB * SEQ, D), F32, kind="ExternalOutput").ap()
    adaln_blocks(nc, *args, out)
    r = _run(nc, [arrays], core_ids=[0])
    return r.results[0]["out_0"].reshape(NB, SEQ, D)
```

```python
from contextlib import ExitStack

import numpy as np

import concourse.bass as bass
from concourse import mybir

F32 = mybir.dt.float32
R32 = mybir.dt.float32r
I32 = mybir.dt.int32
BF16 = mybir.dt.bfloat16
ALU = mybir.AluOpType
ACT = mybir.ActivationFunctionType
AX = mybir.AxisListType

P = 128
NB, SEQ, D = 2, 512, 256
TT = SEQ // P
DC = D // P
NH, HD = 16, 16
HALF = HD // 2
HID = 1024
FC = HID // P
GB = FC // 4
INNER = 512
KC = INNER // P
SH, SHD = 8, 64
TAPS = 4
SLOT = 64
SHIFT = 3 * HD
HPG = 4
NG = NB * NH // HPG
GPB = NH // HPG
EARLY = 12
RING = 7
LN_EPS, RMS_EPS = 1e-5, 1e-6
RSQRT_GUESS = float(0x5F3759DF)
LOWEST = -3.0e38
NEG = -1.0e30

C_ID = 0
C_HAD = C_ID + P
C_MASK = C_HAD + P
C_COS = C_MASK + SEQ
C_SIN = C_COS + TT * HD
C_END = C_SIN + TT * HD
S_CONV, S_BIAS, S_ALOG, S_B, S_C, S_D, S_END = 0, 4, 5, 6, 7, 8, 9


NORMS = [(0, 0), (0, 1), (1, 0), (1, 1), (2, 0), (3, 0), (2, 1), (3, 1)]
SUMS = [(0, 0, 0), (0, 0, 1), (0, 1, 0), (0, 1, 1), (1, 0, 0), (1, 0, 1), (2, 0, 0), (2, 0, 1),
        (1, 1, 0), (1, 1, 1), (3, 0, 0), (2, 1, 0), (2, 1, 1), (3, 0, 1), (3, 1, 0), (3, 1, 1)]


def maxima_steps(g, lo, hi):
    return [("mx", g, n // TT, n % TT) for n in range(lo, hi)] if g < NG else []


def attention_steps(g):
    late = maxima_steps(g + 1, EARLY, HPG * TT)
    nxt = maxima_steps(g + 2, 0, EARLY)
    heads = [("T", g + 2)] if g + 2 < NG else []
    between = {i: [] for i in range(10)}
    if g:
        between[1] += [("pv", g - 1, 1), ("pv", g - 1, 2)]
        between[5] += [("oN", g - 1)]
    between[3] += heads
    if g + 1 < NG:
        between[3] += [("maxT", g + 1)]
    if g == 0:
        between[5] += [("gT", 1)]
    if g < 2:
        between[3] += [("qkv", 1, 2 * g)]
        between[7] += [("qkv", 1, 2 * g + 1)]
    if g == GPB + 1:
        between[3] += [("y", 0, 0, i) for i in range(TT // 2)]
    if g == NG - 1:
        between[9] += [("gu", 1, 0, 4)]
    scores = [("st", g, s, i) for s, n in ((0, 4), (1, 4), (2, 2)) for i in range(n)]
    steps = []
    for i, sc in enumerate(scores):
        steps += [sc] + late[i:i + 1] + between[i]
        if i >= 6 and g != 1:
            steps += nxt[:1]
            nxt = nxt[1:]
    steps += [("pv", g, 0)] + nxt
    if g == GPB:
        steps.append(("aT", 0))
    if g == GPB + 1:
        steps.append(("ln", 1, 0))
    if g == NG - 2:
        steps += [("gu", 1, 0, f) for f in range(FC // 2)]
    return steps


def plan():
    def gu(n, b, lo, hi):
        return [("gu", n, b, f) for f in range(lo, hi)]

    def proj(b):
        return [("proj", b, k) for k in range(KC)]

    def y(n, b):
        return [("y", n, b, i) for i in range(TT // 2)]

    s = [("modT", 0, 0), ("ln", 0, 0)] + [("qkv", 0, t) for t in range(TT)]
    s += [("ln", 0, 1), ("modT", 0, 1), ("modT", 1, 0), ("modT", 1, 1), ("T", 0)]
    s += maxima_steps(0, 0, 16) + [("T", 1), ("maxT", 0), ("gT", 0)] + maxima_steps(1, 0, EARLY)
    for g in range(NG):
        s += attention_steps(g)
    s += gu(1, 0, 5, 6) + [("pv", NG - 1, 1), ("pv", NG - 1, 2)] + gu(1, 0, 6, 7) + [("oN", NG - 1)] + gu(1, 0, 7, 8)
    s += [("aT", 1)] + y(0, 1) + [("y", 1, 0, 0), ("ln", 1, 1), ("y", 1, 0, 1)]
    s += gu(1, 1, 0, 3) + [("ln", 2, 0)] + gu(1, 1, 3, 4) + proj(0) + gu(1, 1, 4, 6) + [("dt", 0)] + gu(1, 1, 6, 8)
    s += [("spread", 0)] + y(2, 0) + [("y", 1, 1, 0), ("ln", 3, 0), ("y", 1, 1, 1)]
    s += gu(3, 0, 0, 3) + [("ln", 2, 1)] + gu(3, 0, 3, 4) + proj(1) + [("had",)] + gu(3, 0, 4, 6) + [("dt", 1)] + gu(3, 0, 6, 8)
    s += [("spread", 1), ("y", 3, 0, 0)] + y(2, 1) + [("y", 3, 0, 1), ("ln", 3, 1)] + gu(3, 1, 0, 8) + y(3, 1)
    return s


def products(stage):
    k = stage[0]
    if k == "ln":
        return [("ln", stage[1], stage[2], c) for c in range(DC)]
    if k == "gT":
        return [("gT", stage[1], w) for w in range(2)]
    if k == "qkv":
        return [("qk",) + stage[1:], ("v",) + stage[1:]]
    if k == "T":
        return [(n, stage[1], j) for j in range(2) for n in ("qT", "kT")]
    if k in ("modT", "mx", "st", "maxT", "oN", "dt", "y"):
        return [stage]
    if k == "pv":
        return []
    if k == "aT":
        return [("aT", stage[1], c) for c in range(DC)]
    if k == "gu":
        return [("gate",) + stage[1:], ("up",) + stage[1:]]
    if k == "proj":
        return [(n,) + stage[1:] for n in ("pj", "gt")]
    if k == "spread":
        return [("spread", stage[1], c) for c in range(KC)]
    if k == "had":
        return [("had", i) for i in range(FC // 2)]
    raise ValueError(stage)


def adaln_blocks(nc, x, wqkv, wout, gammas, wgu0, wdn0, wmod, cT, wproj, woutp, chan, dtw, dtb, wgu1, w2t, consts, spread_sel, out):
    stages = plan()
    place = {}
    for s in stages:
        for u in products(s):
            place[u] = (len(place) % RING, len(place) // RING)

    with ExitStack() as ctx:
        cursor = [(nc.sbuf_base + 31) // 32 * 32]

        def at(name, shape, dt=F32):
            n = int(np.prod(shape[1:])) * (2 if dt == BF16 else 4)
            t = nc.alloc_sbuf_tensor_at(name, shape, dt, offset=cursor[0])
            cursor[0] += (n + 31) // 32 * 32
            return t

        cst = at("cst", [P, C_END])
        sel = at("sel", [P, KC, P], R32)
        rope_c = at("rope_c", [P, TT, 2, HD])
        rope_s = at("rope_s", [P, TT, 2, HD])
        gam = at("gam", [P, 2, HD])
        ch = at("ch", [P, KC, S_END])
        neg_a = at("neg_a", [P, KC])
        dtw_s = at("dtw_s", [P, KC, SH])
        dtb_s = at("dtb_s", [SH, 1])
        c_s = at("c_s", [P, 2, DC, NB])
        silu_c = at("silu_c", [P, 2, DC, NB])
        modT = at("modT", [P, 2, 4, DC, NB])
        gates = at("gates", [P, 2, 2, NB, D])
        stats = at("stats", [P, TT, 6])
        mv = at("mv", [P, TT, 2])
        ln_ve = at("ln_ve", [P, TT])
        ln_rs = at("ln_rs", [P, TT])
        nt = at("nt", [P, TT * 2 * NH])
        qk_ss = at("qk_ss", [P, TT, 2 * NH])
        qk_rs = at("qk_rs", [P, TT, 2 * NH])
        gateT = at("gateT", [P, 2, 2, DC, NB])
        g_tmp = at("g_tmp", [P, 3, DC, NB])
        X = at("X", [P, NB * TT, D])
        h_hi = at("h_hi", [P, NB, DC, SEQ], R32)
        h_lo = at("h_lo", [P, NB, DC, SEQ], R32)
        wout_s = at("wout_s", [P, DC, D])
        wq_at = cursor[0]
        wq_hi = at("wq_hi", [P, DC, 3 * D], R32)
        wq_lo = at("wq_lo", [P, DC, 3 * D], R32)
        stage_at = cursor[0]
        stage = at("stage", [P, 2, 2, 2, DC, P])
        gua_hi = at("gua_hi", [P, FC // 2, 2, DC, P], R32)
        gua_lo = at("gua_lo", [P, FC // 2, 2, DC, P], R32)
        xn = at("xn", [P, TT, D])
        hf = at("hf", [P, DC, SEQ])
        yt = at("yt", [P, 2, D])
        area = cursor[0]

        qkp = at("qkp", [P, TT, 2, NH, SLOT], R32)
        QT_at = cursor[0]
        QT = at("QT", [P, 3, 2, SEQ], R32)
        KT_at = cursor[0]
        KT = at("KT", [P, 3, 2, 2, SEQ], R32)
        vp_at = cursor[0]
        vp = at("vp", [P, NB, TT, NH, 32])
        rot = yt[:].rearrange("p k d -> p (k d)").rearrange("p (w h d) -> p w h d", w=2, h=NH)
        early = cursor[0]
        PTa = at("PTa", [P, HPG, SEQ])
        PTb = at("PTb", [P, HPG, SEQ])
        PTc = at("PTc", [P, HPG, SEQ // 2])
        oT = at("oT", [P, SEQ])
        junk = at("junk", [P, 2, SEQ], BF16)
        mx = at("mx", [P, 2, TT, HPG])
        negm = at("negm", [HPG, SEQ], R32)
        rc = at("rc", [P, TT, HPG])
        att_at = cursor[0]
        att = at("att", [P, TT, D])
        aT_at = cursor[0]
        aT = at("aT", [P, DC, SEQ])
        wmod_s = nc.alloc_sbuf_tensor_at("wmod_s", [P, 2, DC, 6 * D], F32, offset=early)
        g_cols = nc.alloc_sbuf_tensor_at("g_cols", [P, 2, DC, NB, P], F32, offset=att_at)
        sel_raw = nc.alloc_sbuf_tensor_at("sel_raw", [P, KC, P], F32, offset=aT_at)
        wq_raw = nc.alloc_sbuf_tensor_at("wq_raw", [P, DC, 3 * D], F32, offset=stage_at)
        cursor[0] = stage_at
        sq = at("sq", [P, TT, 2, NH, HD])
        qn = at("qn", [P, TT, 2, NH, HD])
        rr = at("rr", [P, TT, 2, NH, HD])

        cursor[0] = wq_at
        sg = at("sg", [P, 2, SEQ])
        sp_z = at("sp_z", [SH, SEQ])
        sp_e = at("sp_e", [SH, SEQ])
        sp_l = at("sp_l", [SH, SEQ])
        sp_u = at("sp_u", [SH, SEQ])
        cursor[0] = area
        gub_hi = at("gub_hi", [P, FC // 2, 2, DC, P], R32)
        gub_lo = at("gub_lo", [P, FC // 2, 2, DC, P], R32)
        H0_at = cursor[0]
        H0 = at("H0", [P, FC, SEQ])
        lean = nc.alloc_sbuf_tensor_at("lean", [P, SEQ], BF16, offset=QT_at)
        cursor[0] = QT_at + SEQ * 2
        drive = at("drive", [P, SEQ])
        state = at("state", [P, SEQ])
        dts = at("dts", [P, SEQ], R32)
        pair_hi = nc.alloc_sbuf_tensor_at("pair_hi", [P, 2, SEQ], F32, offset=QT_at + 4 * 2 * 2 * SEQ)
        cursor[0] = KT_at
        odd_wins = at("odd_wins", [P, 2, SEQ], BF16)
        both = at("both", [P, 2, SEQ], BF16)
        d_sub = at("d_sub", [P, 2, SEQ], BF16)
        d_add = at("d_add", [P, 2, SEQ], BF16)
        acc = at("acc", [P, 2, SEQ])
        skip = at("skip", [P, 2, SEQ])
        ab_at = cursor[0]
        ab = at("ab", [P, 4, SEQ])
        w2a = nc.alloc_sbuf_tensor_at("w2a", [P, FC, D], F32, offset=ab_at)
        w2b = nc.alloc_sbuf_tensor_at("w2b", [P, FC, D], F32, offset=KT_at)
        H1_at = vp_at
        H1 = nc.alloc_sbuf_tensor_at("H1", [P, FC, SEQ], F32, offset=vp_at)
        H = [H0, H1]
        xc = [nc.alloc_sbuf_tensor_at(f"xc{b}", [P, KC, SEQ], F32, offset=(H0_at, H1_at)[b]) for b in range(NB)]
        gt = [nc.alloc_sbuf_tensor_at(f"gt{b}", [P, KC, SEQ], F32, offset=(H0_at, H1_at)[b] + KC * SEQ * 4) for b in range(NB)]
        cursor[0] = early
        wdn_s = at("wdn_s", [P, FC, D])
        woutp_s = at("woutp_s", [P, KC, D])
        pj_hi = at("pj_hi", [P, KC, 2, DC, P], R32)
        pj_lo = at("pj_lo", [P, KC, 2, DC, P], R32)
        decay = at("decay", [P, 2, SEQ])

        ident = cst[:, C_ID:C_ID + P]
        had = cst[:, C_HAD:C_HAD + P]
        mask = cst[:, C_MASK:C_MASK + SEQ]
        cosv = cst[:, C_COS:C_SIN].rearrange("p (t d) -> p t d", t=TT)
        sinv = cst[:, C_SIN:C_END].rearrange("p (t d) -> p t d", t=TT)
        PT = [PTa, PTb, PTc]

        bank = [ctx.enter_context(nc.psum_tensor(f"bank{i}", [P, SEQ], F32)) for i in range(RING)]
        pv_bank = ctx.enter_context(nc.psum_tensor("pv_bank", [P, SEQ], F32))

        def sem(name):
            return ctx.enter_context(nc.semaphore(name))

        bank_full = [sem(f"bank_full{i}") for i in range(RING)]
        bank_free = [sem(f"bank_free{i}") for i in range(RING)]
        x_in = [sem(f"x_in{b}") for b in range(NB)]
        wq_in, cst_in, wout_in = sem("wq_in"), sem("cst_in"), sem("wout_in")
        ident_in = sem("ident_in")
        wmod_in = [sem(f"wmod_in{i}") for i in range(4)]
        c_in, gam_in, chan_in, sel_in = sem("c_in"), sem("gam_in"), sem("chan_in"), sem("sel_in")
        stage_in = [sem("stage_in0"), sem("stage_in1")]
        wdn_in, woutp_in, w2_in = sem("wdn_in"), sem("woutp_in"), sem("w2_in")
        shift_in = [sem("shift_in0"), sem("shift_in1")]
        out_done = sem("out_done")
        pool_consts, pool_chain, dve_chain, act_chain = sem("pool_consts"), sem("pool_chain"), sem("dve_chain"), sem("act_chain")
        silu_c_done, gateT_done, g_cols_done = sem("silu_c_done"), sem("gateT_done"), sem("g_cols_done")
        wq_split_hi, wq_split = sem("wq_split_hi"), sem("wq_split")
        stage_split = sem("stage_split")
        xn_done, h_done = sem("xn_done"), sem("h_done")
        sq_done, cos_done, roped, scaled, qk_high, qk_split = (
            sem(n) for n in ("sq_done", "cos_done", "roped", "scaled", "qk_high", "qk_split"))
        causal_done, pv_done, pv_free = (
            sem(n) for n in ("causal_done", "pv_done", "pv_free"))
        abs_done, sparse_done, x_done = sem("abs_done"), sem("sparse_done"), sem("x_done")
        conv_begun, xc_done = sem("conv_begun"), sem("xc_done")
        sp_e_done, sp_l_done, dts_done = sem("sp_e_done"), sem("sp_l_done"), sem("dts_done")
        decay_done, skip_done, y_done, comb_done = (
            sem("decay_done"), sem("skip_done"), sem("y_done"), sem("comb_done"))
        hidden_done, dts_zeroed = sem("hidden_done"), sem("dts_zeroed")
        w2_mixed = sem("w2_mixed")
        sel_done, rope_done = sem("sel_done"), sem("rope_done")

        def ps(u):
            return bank[place[u][0]]

        def claim(eng, u):
            if place[u][1]:
                eng.wait_ge(bank_free[place[u][0]], place[u][1])

        def filled(eng, u):
            eng.wait_ge(bank_full[place[u][0]], place[u][1] + 1)

        def read(eng, u):
            eng.wait_ge(bank_free[place[u][0]], place[u][1] + 1)

        def h_used(eng, n, b):
            filled(eng, (("v", b, TT - 1), ("up", 1, b, FC - 1), ("gt", b, KC - 1))[n])

        def fill(ins, u):
            ins.then_inc(bank_full[place[u][0]], 1)

        def free(ins, u):
            ins.then_inc(bank_free[place[u][0]], 1)

        block = ctx.enter_context(nc.Block())
        NCONST = 5

        @block.sync
        def _(sp):
            xv = x.rearrange("(b t p) d -> b p t d", b=NB, p=P)
            ov = out.rearrange("(b t p) d -> b p t d", b=NB, p=P)
            sp.dma_start(X[:, 0:TT, :], xv[0]).then_inc(x_in[0], 16)
            sp.dma_start(c_s[:], cT).then_inc(c_in, 16)
            sp.dma_start(cst[:, 0:P], consts[:, 0:P]).then_inc(ident_in, 16)
            def wmod_load(l, half):
                cols = slice(3 * D * half, 3 * D * (half + 1))
                sp.dma_start(wmod_s[:, l, :, cols], wmod[:, l, :, cols]).then_inc(wmod_in[2 * l + half], 16)

            wmod_load(0, 0)
            sp.dma_start(wq_raw[:], wqkv).then_inc(wq_in, 16)
            sp.dma_start(gam[:], gammas).then_inc(gam_in, 16)
            sp.dma_start(cst[:, P:], consts[:, P:]).then_inc(cst_in, 16)
            sp.dma_start(X[:, TT:2 * TT, :], xv[1]).then_inc(x_in[1], 16)
            wmod_load(0, 1)
            wmod_load(1, 0)
            wmod_load(1, 1)
            sp.dma_start(sel_raw[:], spread_sel).then_inc(sel_in, 16)
            sp.dma_start(ch[:], chan).then_inc(chan_in, 16)
            sp.dma_start(dtw_s[:], dtw).then_inc(chan_in, 16)
            sp.dma_start(dtb_s[:], dtb).then_inc(chan_in, 16)
            sp.dma_start(wout_s[:], wout).then_inc(wout_in, 16)

            def stage_load(i):
                src = wgu0[:, 2 * i:2 * i + 2] if i < 4 else wproj[:, 2 * (i - 4):2 * (i - 4) + 2] if i < 6 else wgu1[:, 2 * (i - 6):2 * (i - 6) + 2]
                if i >= 2:
                    sp.wait_ge(stage_split, i - 1)
                sp.dma_start(stage[:, i % 2], src).then_inc(stage_in[i % 2], 16)

            for g in range(NG):
                read(sp, ("maxT", g))
                for j in range(2):
                    sp.dma_start(QT[SHIFT:P:SLOT, g % 3, j, :].bitcast(F32), negm[2 * j:2 * j + 2, :].bitcast(F32)).then_inc(shift_in[g % 2], 16)
                if g == GPB - 1:
                    sp.wait_ge(qk_split, NB * TT)
                    stage_load(0)
                    stage_load(1)
                if g in (GPB + 1, GPB + 2):
                    stage_load(g - GPB + 1)
            sp.wait_ge(pv_done, 3 * NG)
            sp.dma_start(wdn_s[:], wdn0).then_inc(wdn_in, 16)
            sp.dma_start(woutp_s[:], woutp).then_inc(woutp_in, 16)
            for i in range(4, 10):
                stage_load(i)
            sp.wait_ge(sparse_done, NB * GB)
            sp.dma_start(w2a[:], w2t).then_inc(w2_in, 16)
            for b in range(NB):
                for i in range(TT // 2):
                    sp.wait_ge(x_done, SUMS.index((3, b, i)) + 1)
                    sp.dma_start(ov[b][:, 2 * i:2 * i + 2, :], X[:, TT * b + 2 * i:TT * b + 2 * i + 2, :]).then_inc(out_done, 16)
            sp.wait_ge(out_done, 16 * TT)

        @block.gpsimd
        def _(pool):
            g = nc.gpsimd
            chain = [0]

            def link(ins):
                chain[0] += 1
                ins.then_inc(pool_chain, 1)
                pool.wait_ge(pool_chain, chain[0])

            def rope(n):
                t = n % TT
                read(pool, ("qk", n // TT, t))
                if n == 0:
                    pool.wait_ge(rope_done, 1)
                else:
                    pool.wait_ge(roped, n)
                for lo, hi in ((0, HALF), (HALF, 0)):
                    tab = rope_s[:, t, :, lo:lo + HALF].unsqueeze(2).broadcast_to([P, 2, NH, HALF])
                    last = g.tensor_tensor(rot[:, :, :, lo:lo + HALF], qn[:, t, :, :, hi:hi + HALF], tab, ALU.mult)
                link(last)
                pool.wait_ge(cos_done, n + 1)
                g.tensor_tensor(rr[:, t], rr[:, t], rot, ALU.add).then_inc(roped, 1)

            def gate_columns(l):
                pool.wait_ge(gateT_done, 2 * l + 2)
                if l:
                    filled(pool, ("gT", l - 1, 1))
                g.tensor_copy(g_cols[:],
                              gateT[:, l].unsqueeze(4).broadcast_to([P, 2, DC, NB, P])).then_inc(g_cols_done, 1)

            def split_stage(i):
                half = stage[:, i % 2]
                if i < 4 or i >= 6:
                    j = i % 4 if i < 4 else i - 6
                    hi_t, lo_t = (gua_hi, gua_lo) if j < 2 else (gub_hi, gub_lo)
                    j = j % 2
                else:
                    hi_t, lo_t, j = pj_hi, pj_lo, i - 4
                pool.wait_ge(stage_in[i % 2], 16 * (i // 2 + 1))
                link(g.tensor_copy(hi_t[:, 2 * j:2 * j + 2], half))
                g.tensor_tensor(lo_t[:, 2 * j:2 * j + 2], half, hi_t[:, 2 * j:2 * j + 2].bitcast(F32), ALU.subtract).then_inc(stage_split, 1)

            def causal(gr, s, i):
                read(pool, ("st", gr, s, i))
                if s == 0:
                    v = PTa[:, i, 0:P].unsqueeze(1)
                elif s == 1:
                    v = PTb[:, i, :].rearrange("p (c k) -> p c k", k=P)[:, 0:4:3, :]
                else:
                    v = PTc[:, 2 * i:2 * i + 2, 0:P]
                g.affine_select(out=v, in_=v, compare_op=ALU.is_ge, fill=0.0, base=0,
                                pattern=[[0, v.shape[1]], [1, P]], channel_multiplier=-1).then_inc(causal_done, 1)

            def hidden(f):
                read(pool, ("gate", 1, 1, f))
                read(pool, ("up", 1, 1, f))
                g.tensor_tensor(H1[:, f], H1[:, f], sg[:, f % 2], ALU.mult).then_inc(hidden_done, 1)

            def comb(b, k):
                n = KC * b + k
                pool.wait_ge(y_done, n + 1)
                read(pool, ("gt", b, k))
                g.tensor_tensor(gt[b][:, k], xc[b][:, k], gt[b][:, k], ALU.mult).then_inc(comb_done, 1)

            g.memset(vp[:, :, :, :, HD:32], 0.0).then_inc(pool_consts, 1)
            g.memset(qkp[:, :, :, :, SHIFT:SLOT].bitcast(F32), 0.0).then_inc(pool_consts, 1)
            g.memset(KT[:].bitcast(F32), 0.0).then_inc(pool_consts, 1)
            pool.wait_ge(pool_consts, 3)
            g.memset(vp[:, :, :, :, HD:HD + 1], 1.0).then_inc(pool_consts, 1)
            g.memset(qkp[:, :, 1, :, SHIFT:SHIFT + 1].bitcast(F32), 1.0).then_inc(pool_consts, 1)
            for n in range(TT):
                rope(n)
            gate_columns(0)
            gate_columns(1)
            for gr in range(NG):
                for s, n in ((0, 4), (1, 4), (2, 2)):
                    for i in range(n):
                        causal(gr, s, i)
                    if gr == 0 and s == 2:
                        rope(TT)
                    if gr == 1:
                        rope(TT + 1 + s)
                    if gr == NG - 2 and s == 1:
                        split_stage(3)
                if gr in (GPB - 1, GPB):
                    split_stage(gr - GPB + 1)
                if gr == GPB + 1:
                    for j in range(2):
                        filled(pool, ("kT", NG - 1, j))
                    split_stage(2)
            filled(pool, ("y", 0, 1, 1))
            split_stage(4)
            split_stage(5)
            g.memset(dts[:].bitcast(F32), 0.0).then_inc(dts_zeroed, 1)
            for f in range(FC):
                hidden(f)
            for k in range(KC):
                comb(0, k)
            filled(pool, ("up", 1, 1, FC - 1))
            split_stage(6)
            split_stage(7)
            split_stage(8)
            split_stage(9)
            pool.wait_ge(w2_in, 16)
            src, dst = w2a, w2b
            for r in range(3):
                s = 1 << r
                a = src[:].rearrange("p (m two s) d -> p m two (s d)", two=2, s=s)
                z = dst[:].rearrange("p (m two s) d -> p m two (s d)", two=2, s=s)
                g.tensor_tensor(z[:, :, 0], a[:, :, 0], a[:, :, 1], ALU.add)
                last = g.tensor_tensor(z[:, :, 1], a[:, :, 0], a[:, :, 1], ALU.subtract)
                if r < 2:
                    link(last)
                else:
                    last.then_inc(w2_mixed, 1)
                src, dst = dst, src
            for k in range(KC):
                comb(1, k)

        @block.scalar
        def _(act):
            a = nc.scalar
            chain = [0]

            def link(ins):
                chain[0] += 1
                ins.then_inc(act_chain, 1)
                act.wait_ge(act_chain, chain[0])

            def ln(n, b):
                i, l, k = NORMS.index((n, b)), n // 2, 2 * (n % 2)
                read(act, ("modT", l, n % 2))
                if i:
                    act.wait_ge(h_done, i)
                if n:
                    h_used(act, n - 1, b)
                for c in range(DC):
                    u = ("ln", n, b, c)
                    filled(act, u)
                    sh, sc = modT[:, l, k, c, b:b + 1], modT[:, l, k + 1, c, b:b + 1]
                    a.activation(hf[:, c], ps(u)[:], ACT.Identity, bias=sh, scale=sc)
                    free(a.activation(h_hi[:, b, c], ps(u)[:], ACT.Identity, bias=sh, scale=sc), u)

            def qkv_in(n):
                b, t = n // TT, n % TT
                u, v = ("qk", b, t), ("v", b, t)
                filled(act, u)
                if b:
                    act.wait_ge(roped, n - TT + 1)
                a.activation(sq[:, t].rearrange("p a h d -> p (a h d)"), ps(u)[:], ACT.Square).then_inc(sq_done, 1)
                free(a.copy(qn[:, t].rearrange("p a h d -> p (a h d)"), ps(u)[:]), u)
                filled(act, v)
                if n == 0:
                    act.wait_ge(pool_consts, NCONST)
                free(a.copy(vp[:, b, t, :, 0:HD], ps(v)[:, 0:D].rearrange("p (h d) -> p h d", d=HD)), v)

            def qk_hi(n):
                t = n % TT
                act.wait_ge(scaled, n + 1)
                if n == TT:
                    filled(act, ("kT", GPB - 1, 1))
                a.copy(qkp[:, t, :, :, 0:HD], rr[:, t])
                a.copy(qkp[:, t, 0, :, 2 * HD:3 * HD], rr[:, t, 0])
                a.copy(qkp[:, t, 1, :, HD:2 * HD], rr[:, t, 1]).then_inc(qk_high, 1)

            def gates_out(l):
                for w in range(2):
                    u = ("gT", l, w)
                    filled(act, u)
                    free(a.copy(gates[:, l, w].rearrange("p b d -> p (b d)"), ps(u)[:]), u)

            def heads_out(gr):
                if gr >= 3:
                    filled(act, ("st", gr - 3, 2, 1))
                for j in range(2):
                    u, w = ("qT", gr, j), ("kT", gr, j)
                    filled(act, u)
                    free(a.copy(QT[:, gr % 3, j], ps(u)[:]), u)
                    filled(act, w)
                    a.copy(KT[0:SLOT, gr % 3, j, 0], ps(w)[0:SLOT])
                    free(a.copy(KT[SLOT:P, gr % 3, j, 1], ps(w)[SLOT:P]), w)

            def exps(gr, s):
                if gr:
                    act.wait_ge(pv_done, 3 * (gr - 1) + s + 1)
                for i in range((4, 4, 2)[s]):
                    u = ("st", gr, s, i)
                    filled(act, u)
                    if s < 2:
                        dst, src = PT[s][:, i], ps(u)[:]
                    else:
                        dst, src = PTc[:, 2 * i:2 * i + 2], ps(u)[:].rearrange("p (h q) -> p h q", h=2)
                    free(a.activation(dst, src, ACT.Exp), u)

            def aT_out(b):
                if b:
                    filled(act, ("y", 0, b - 1, 1))
                for c in range(DC):
                    u = ("aT", b, c)
                    filled(act, u)
                    free(a.copy(aT[:, c], ps(u)[:]), u)

            def hidden_used(n, b, f):
                if (n, b) == (1, 1):
                    act.wait_ge(hidden_done, f + 1)
                else:
                    read(act, ("up", n, b, f))

            def gu(n, b, f):
                u = ("gate", n, b, f)
                filled(act, u)
                if f >= 2:
                    hidden_used(n, b, f - 2)
                elif n == 1 and b:
                    hidden_used(1, 0, FC - 2 + f)
                elif n == 3:
                    hidden_used(*((3, 0) if b else (1, 1)), FC - 2 + f)
                free(a.activation(sg[:, f % 2], ps(u)[:], ACT.Silu), u)
                if (n, b) == (1, 1):
                    u = ("up", n, b, f)
                    filled(act, u)
                    free(a.copy(H1[:, f], ps(u)[:]), u)

            def absolute(b, gb):
                n = GB * b + gb
                hidden_used(1, b, 4 * gb + 3)
                if n:
                    act.wait_ge(sparse_done, n)
                a.activation(ab[:], H[b][:, 4 * gb:4 * gb + 4], ACT.Abs).then_inc(abs_done, 1)

            def conv_begin(b, k):
                n = KC * b + k
                u = ("pj", b, k)
                filled(act, u)
                if n >= 2:
                    act.wait_ge(xc_done, n - 1)
                a.activation(acc[:, k % 2], ps(u)[:], ACT.Identity, bias=ch[:, k, S_BIAS:S_BIAS + 1],
                             scale=ch[:, k, S_CONV + TAPS - 1:S_CONV + TAPS]).then_inc(conv_begun, 1)

            def proj(b):
                if b == 0:
                    act.wait_ge(chan_in, 48)
                filled(act, ("y", 1, b, 1))
                conv_begin(b, 0)
                for k in range(1, KC):
                    conv_begin(b, k)
                    if k < KC - 1:
                        conv_out(b, k - 1)
                for k in range(KC):
                    u = ("gt", b, k)
                    filled(act, u)
                    free(a.activation(gt[b][:, k], ps(u)[:], ACT.Sigmoid), u)
                conv_out(b, KC - 2)
                conv_out(b, KC - 1)

            def conv_out(b, k):
                read(act, ("pj", b, k))
                a.activation(xc[b][:, k], acc[:, k % 2], ACT.Silu).then_inc(xc_done, 1)

            def softplus(b):
                u = ("dt", b)
                filled(act, u)
                if b:
                    act.wait_ge(dts_done, b)
                a.activation(sp_z[:], ps(u)[0:SH], ACT.Identity, bias=dtb_s[:, 0:1])
                free(a.activation(sp_e[:], ps(u)[0:SH], ACT.Abs, bias=dtb_s[:, 0:1]), u)
                read(act, u)
                a.activation(sp_e[:], sp_e[:], ACT.Exp, scale=-1.0).then_inc(sp_e_done, 1)
                act.wait_ge(sp_e_done, b + 1)
                a.activation(sp_l[:], sp_e[:], ACT.Ln, bias=1.0).then_inc(sp_l_done, 1)

            def spread(b):
                if b == 0:
                    link(a.activation(neg_a[:], ch[:, :, S_ALOG], ACT.Exp))
                    link(a.mul(neg_a[:], neg_a[:], -1.0))
                for k in range(KC):
                    n = KC * b + k
                    u = ("spread", b, k)
                    filled(act, u)
                    if n >= 2:
                        act.wait_ge(y_done, n - 1)
                    a.activation(decay[:, k % 2], ps(u)[:], ACT.Exp, scale=neg_a[:, k:k + 1]).then_inc(decay_done, 1)
                    a.activation(skip[:, k % 2], xc[b][:, k], ACT.Copy, scale=ch[:, k, S_D:S_D + 1]).then_inc(skip_done, 1)

            act.wait_ge(c_in, 16)
            a.activation(silu_c[:], c_s[:], ACT.Silu).then_inc(silu_c_done, 1)
            act.wait_ge(wq_in, 16)
            a.copy(wq_hi[:], wq_raw[:]).then_inc(wq_split_hi, 1)
            ln(0, 0)
            for n in range(TT):
                qkv_in(n)
            ln(0, 1)
            qk_hi(0)
            qk_hi(1)
            qk_hi(2)
            qk_hi(3)
            heads_out(0)
            heads_out(1)
            gates_out(0)
            for gr in range(NG):
                exps(gr, 0)
                if gr + 2 < NG:
                    heads_out(gr + 2)
                if gr < 2:
                    qkv_in(TT + 2 * gr)
                exps(gr, 1)
                if gr == 0:
                    gates_out(1)
                if gr < 2:
                    qkv_in(TT + 2 * gr + 1)
                exps(gr, 2)
                if gr == 1:
                    for t in range(TT):
                        qk_hi(TT + t)
                if gr == GPB:
                    aT_out(0)
                if gr == GPB + 1:
                    ln(1, 0)
                if gr == NG - 2:
                    for f in range(FC // 2):
                        gu(1, 0, f)
                    absolute(0, 0)
            for f in range(4, FC):
                gu(1, 0, f)
            absolute(0, 1)
            aT_out(1)
            ln(1, 1)
            for f in range(3):
                gu(1, 1, f)
            ln(2, 0)
            gu(1, 1, 3)
            absolute(1, 0)
            proj(0)
            gu(1, 1, 4)
            gu(1, 1, 5)
            softplus(0)
            gu(1, 1, 6)
            gu(1, 1, 7)
            spread(0)
            absolute(1, 1)
            ln(3, 0)
            for f in range(3):
                gu(3, 0, f)
            ln(2, 1)
            gu(3, 0, 3)
            proj(1)
            for i in range(FC // 2):
                u = ("had", i)
                filled(act, u)
                free(a.mul(w2a[:, 2 * i:2 * i + 2], ps(u)[:].rearrange("p (c d) -> p c d", c=2), 1.0 / HID ** 0.5), u)
            gu(3, 0, 4)
            gu(3, 0, 5)
            softplus(1)
            gu(3, 0, 6)
            gu(3, 0, 7)
            spread(1)
            ln(3, 1)
            for f in range(FC):
                gu(3, 1, f)

        @block.vector
        def _(dve):
            v = nc.vector
            chain = [0]

            def link(ins):
                chain[0] += 1
                ins.then_inc(dve_chain, 1)
                dve.wait_ge(dve_chain, chain[0])

            def rsqrt(y, x, t):
                link(v.tensor_scalar(y.bitcast(I32), x.bitcast(I32), -0.5, RSQRT_GUESS, ALU.mult, ALU.add))
                for _ in range(3):
                    link(v.tensor_tensor(t, y, y, ALU.mult))
                    link(v.scalar_tensor_tensor(t, t, -0.5, x, ALU.mult, ALU.mult))
                    link(v.scalar_tensor_tensor(y, t, 1.5, y, ALU.add, ALU.mult))

            def ln_stats(n, b):
                i = NORMS.index((n, b))
                if n == 0:
                    dve.wait_ge(x_in[b], 16)
                if i:
                    dve.wait_ge(xn_done, i)
                for t in range(TT):
                    last = v.bn_stats(stats[:, t], X[:, TT * b + t])
                link(last)
                for t in range(TT):
                    last = v.bn_aggr(mv[:, t], stats[:, t])
                link(last)
                link(v.tensor_scalar(ln_ve[:], mv[:, :, 1], LN_EPS, None, ALU.add))
                rsqrt(ln_rs[:], ln_ve[:], nt[:, 0:TT])
                if i:
                    filled(dve, ("ln",) + NORMS[i - 1] + (DC - 1,))
                for t in range(TT):
                    last = v.tensor_scalar(xn[:, t], X[:, TT * b + t], mv[:, t, 0:1], ln_rs[:, t:t + 1], ALU.subtract, ALU.mult)
                last.then_inc(xn_done, 1)

            def ln_lo(n, b):
                read(dve, ("ln", n, b, DC - 1))
                v.tensor_tensor(h_lo[:, b], hf[:], h_hi[:, b].bitcast(F32), ALU.subtract).then_inc(h_done, 1)

            def mod_out(l, k):
                u = ("modT", l, k)
                n = 2 * l + k
                filled(dve, u)
                m = ps(u)[:, 0:12].rearrange("p (k c b) -> p k c b", k=3, c=DC)
                v.tensor_copy(modT[:, l, 2 * k], m[:, 0])
                v.tensor_scalar(modT[:, l, 2 * k + 1], m[:, 1], 1.0, None, ALU.add)
                if n:
                    dve.wait_ge(gateT_done, n)
                v.tensor_scalar(g_tmp[:, 0], m[:, 2], 0.25, None, ALU.max)
                v.tensor_scalar(g_tmp[:, 1], m[:, 2], -1.0, 0.25, ALU.mult, ALU.max)
                free(v.tensor_scalar(g_tmp[:, 2], m[:, 2], 0.0, 2.0, ALU.is_ge, ALU.mult), u)
                read(dve, u)
                link(v.tensor_tensor(g_tmp[:, 0], g_tmp[:, 0], g_tmp[:, 1], ALU.max))
                v.scalar_tensor_tensor(gateT[:, l, k], g_tmp[:, 2], -1.0, g_tmp[:, 0], ALU.add, ALU.mult).then_inc(gateT_done, 1)

            def rope_tables():
                dve.wait_ge(gam_in, 16)
                dve.wait_ge(cst_in, 16)
                for w in range(2):
                    s = HD ** -0.5 if w == 0 else 1.0
                    gm = gam[:, w].unsqueeze(1)
                    v.scalar_tensor_tensor(rope_c[:, :, w], cosv, s, gm.broadcast_to([P, TT, HD]), ALU.mult, ALU.mult)
                    for o, g0, sign in ((0, HALF, -1.0), (HALF, 0, 1.0)):
                        gs = gam[:, w, g0:g0 + HALF].unsqueeze(1).broadcast_to([P, TT, HALF])
                        last = v.scalar_tensor_tensor(rope_s[:, :, w, o:o + HALF], sinv[:, :, o:o + HALF], s * sign, gs, ALU.mult, ALU.mult)
                last.then_inc(rope_done, 1)

            def rms_cos(n):
                b, t = n // TT, n % TT
                dve.wait_ge(sq_done, n + 1)
                link(v.tensor_reduce(qk_ss[:, t], sq[:, t].rearrange("p a h d -> p (a h) d"), AX.X, ALU.add))
                read(dve, ("qk", b, t))
                if n == 0:
                    dve.wait_ge(rope_done, 1)
                tab = rope_c[:, t].unsqueeze(2).broadcast_to([P, 2, NH, HD])
                if b:
                    dve.wait_ge(qk_split, n - TT + 1)
                v.tensor_tensor(rr[:, t], qn[:, t], tab, ALU.mult).then_inc(cos_done, 1)

            def rms_scale(b, lo, hi):
                x = qk_ss[:, lo:hi].rearrange("p t h -> p (t h)")
                y = qk_rs[:, lo:hi].rearrange("p t h -> p (t h)")
                link(v.tensor_scalar(x, x, 1.0 / HD, RMS_EPS, ALU.mult, ALU.add))
                rsqrt(y, x, nt[:, 0:(hi - lo) * 2 * NH])
                for t in range(lo, hi):
                    dve.wait_ge(roped, TT * b + t + 1)
                    q = rr[:, t].rearrange("p a h d -> p (a h) d")
                    v.tensor_tensor(q, q, qk_rs[:, t].unsqueeze(2).broadcast_to([P, 2 * NH, HD]), ALU.mult).then_inc(scaled, 1)

            def qk_lo(n):
                t = n % TT
                dve.wait_ge(qk_high, n + 1)
                v.tensor_tensor(qkp[:, t, 0, :, HD:2 * HD], rr[:, t, 0], qkp[:, t, 0, :, 0:HD].bitcast(F32), ALU.subtract)
                v.tensor_tensor(qkp[:, t, 1, :, 2 * HD:3 * HD], rr[:, t, 1], qkp[:, t, 1, :, 0:HD].bitcast(F32),
                                ALU.subtract).then_inc(qk_split, 1)

            def maxima(gr, lo=0, hi=HPG * TT):
                for h in range(HPG):
                    for t in range(TT):
                        if gr >= NG or not lo <= TT * h + t < hi:
                            continue
                        u = ("mx", gr, h, t)
                        n = P * (t + 1)
                        filled(dve, u)
                        m = TT * h + t + TT * HPG * gr
                        if m >= 2:
                            read(dve, ("mx", (m - 2) // (TT * HPG), (m - 2) // TT % HPG, (m - 2) % TT))
                        free(v.tensor_tensor_reduce(out=junk[:, m % 2, 0:n], in0=ps(u)[:, 0:n], in1=mask[:, SEQ - n:SEQ], scale=1.0,
                                                    scalar=LOWEST, op0=ALU.add, op1=ALU.max,
                                                    accum_out=mx[:, gr % 2, t, h:h + 1]), u)

            def negate(gr):
                u = ("maxT", gr)
                filled(dve, u)
                if gr:
                    dve.wait_ge(shift_in[(gr - 1) % 2], 32 * ((gr - 1) // 2 + 1))
                free(v.tensor_scalar(negm[:], ps(u)[0:HPG], -1.0, None, ALU.mult), u)

            def pv_out(gr):
                dve.wait_ge(pv_done, 3 * gr + 3)
                if gr:
                    filled(dve, ("oN", gr - 1))
                v.tensor_copy(oT[:], pv_bank[:]).then_inc(pv_free, 1)

            def normalise(gr):
                u = ("oN", gr)
                gb = gr % GPB
                filled(dve, u)
                if gr == 0:
                    filled(dve, ("gT", 1, 1))
                if gr == GPB:
                    filled(dve, ("aT", 0, DC - 1))
                if gr:
                    read(dve, ("oN", gr - 1))
                m = ps(u)[:].rearrange("p (t h e) -> p t h e", t=TT, h=HPG)
                link(v.reciprocal(rc[:], m[:, :, :, HD]))
                dst = att[:, :, gb * HPG * HD:(gb + 1) * HPG * HD].rearrange("p t (h d) -> p t h d", d=HD)
                free(v.tensor_tensor(dst, m[:, :, :, 0:HD], rc[:].unsqueeze(3).broadcast_to([P, TT, HPG, HD]), ALU.mult), u)

            def residual(n, b, halves=(0, 1)):
                l, k = n // 2, n % 2
                for i in halves:
                    u = ("y", n, b, i)
                    nth = SUMS.index((n, b, i))
                    filled(dve, u)
                    if nth:
                        dve.wait_ge(x_done, nth)
                    gt_b = gates[:, l, k, b].unsqueeze(1).broadcast_to([P, 2, D])
                    free(v.tensor_tensor(yt[:], ps(u)[:].rearrange("p (t d) -> p t d", t=2), gt_b, ALU.mult), u)
                    read(dve, u)
                    xs = X[:, TT * b + 2 * i:TT * b + 2 * i + 2]
                    v.tensor_tensor(xs, xs, yt[:], ALU.add).then_inc(x_done, 1)
                    dve.wait_ge(x_done, nth + 1)

            def hidden(n, b, f):
                u = ("up", n, b, f)
                filled(dve, u)
                read(dve, ("gate", n, b, f))
                free(v.tensor_tensor(H[b][:, f], ps(u)[:], sg[:, f % 2], ALU.mult), u)

            def sparsify(b, gb, part):
                n = GB * b + gb
                ev, od = ab[:, 0:4:2], ab[:, 1:4:2]
                if part == 0:
                    dve.wait_ge(abs_done, n + 1)
                    v.tensor_tensor(pair_hi[:], ev, od, ALU.max)
                    link(v.tensor_tensor(odd_wins[:], od, ev, ALU.is_gt))
                if part == 1:
                    link(v.tensor_tensor(ev, ev, od, ALU.min))
                    v.tensor_tensor(both[:, 0], ab[:, 0], pair_hi[:, 1], ALU.is_ge)
                    link(v.tensor_tensor(both[:, 1], ab[:, 2], pair_hi[:, 0], ALU.is_gt))
                if part == 2:
                    link(v.tensor_tensor(lean[:], both[:, 0], both[:, 1], ALU.subtract))
                    ln2 = lean[:].unsqueeze(1).broadcast_to([P, 2, SEQ])
                    v.tensor_tensor(d_sub[:], ln2, odd_wins[:], ALU.subtract)
                    link(v.tensor_tensor(d_add[:], ln2, odd_wins[:], ALU.add))
                if part == 3:
                    for j, (d, thr, op) in enumerate(((d_sub[:, 0], 0.0, ALU.is_ge), (d_add[:, 0], 1.0, ALU.is_ge),
                                                      (d_add[:, 1], 0.0, ALU.is_le), (d_sub[:, 1], -1.0, ALU.is_le))):
                        hj = H[b][:, 4 * gb + j]
                        last = v.scalar_tensor_tensor(hj, d, thr, hj, op, ALU.mult)
                    last.then_inc(sparse_done, 1)

            def conv(b, k):
                n = KC * b + k
                u = ("pj", b, k)
                if n == 0:
                    dve.wait_ge(chan_in, 48)
                dve.wait_ge(conv_begun, n + 1)
                for j in range(TAPS - 2, -1, -1):
                    s = TAPS - 1 - j
                    last = v.scalar_tensor_tensor(acc[:, k % 2, s:SEQ], ps(u)[:, 0:SEQ - s], ch[:, k, S_CONV + j:S_CONV + j + 1],
                                                  acc[:, k % 2, s:SEQ], ALU.mult, ALU.add)
                    if j:
                        link(last)
                    else:
                        free(last, u)

            def softplus(b):
                dve.wait_ge(sp_e_done, b + 1)
                if b == 0:
                    dve.wait_ge(dts_zeroed, 1)
                if b:
                    dve.wait_ge(dts_done, b)
                    filled(dve, ("spread", b - 1, KC - 1))
                link(v.tensor_scalar(sp_u[:], sp_e[:], 1.0, -1.0, ALU.add, ALU.add))
                link(v.tensor_tensor(sp_u[:], sp_e[:], sp_u[:], ALU.subtract))
                dve.wait_ge(sp_l_done, b + 1)
                link(v.tensor_tensor(sp_u[:], sp_l[:], sp_u[:], ALU.add))
                link(v.scalar_tensor_tensor(sp_z[:], sp_z[:], 0.0, sp_u[:], ALU.max, ALU.add))
                link(v.tensor_copy(dts[0:SH], sp_z[:]))
                v.tensor_tensor(dts[32:32 + SH], sp_z[:], dts[0:SH].bitcast(F32), ALU.subtract).then_inc(dts_done, 1)

            def mix(b, k):
                n = KC * b + k
                u = ("spread", b, k)
                filled(dve, u)
                dve.wait_ge(decay_done, n + 1)
                dve.wait_ge(skip_done, n + 1)
                free(v.scalar_tensor_tensor(drive[:], ps(u)[:], ch[:, k, S_B:S_B + 1], xc[b][:, k], ALU.mult, ALU.mult), u)
                read(dve, u)
                if n:
                    dve.wait_ge(y_done, n)
                link(v.tensor_tensor_scan(state[:], decay[:, k % 2], drive[:], 0.0, ALU.mult, ALU.add))
                v.scalar_tensor_tensor(xc[b][:, k], state[:], ch[:, k, S_C:S_C + 1], skip[:, k % 2], ALU.mult, ALU.add).then_inc(y_done, 1)

            ln_stats(0, 0)
            mod_out(0, 0)
            dve.wait_ge(wq_split_hi, 1)
            v.tensor_tensor(wq_lo[:], wq_raw[:], wq_hi[:].bitcast(F32), ALU.subtract).then_inc(wq_split, 1)
            ln_lo(0, 0)
            rope_tables()
            ln_stats(0, 1)
            rms_cos(0)
            rms_cos(1)
            rms_cos(2)
            rms_cos(3)
            rms_scale(0, 0, TT)
            qk_lo(0)
            qk_lo(1)
            qk_lo(2)
            qk_lo(3)
            ln_lo(0, 1)
            mod_out(0, 1)
            mod_out(1, 0)
            mod_out(1, 1)
            dve.wait_ge(sel_in, 16)
            v.tensor_copy(sel[:], sel_raw[:]).then_inc(sel_done, 1)
            maxima(0)
            negate(0)
            maxima(1, 0, EARLY)
            for gr in range(NG):
                maxima(gr + 1, EARLY, 14)
                if gr:
                    pv_out(gr - 1)
                maxima(gr + 1, 14, 16)
                if gr + 1 < NG:
                    negate(gr + 1)
                if gr < 2:
                    rms_cos(TT + 2 * gr)
                if gr:
                    normalise(gr - 1)
                if gr == GPB + 1:
                    residual(0, 0)
                    ln_stats(1, 0)
                if gr < 2:
                    rms_cos(TT + 2 * gr + 1)
                if gr == 1:
                    rms_scale(1, 0, TT)
                    maxima(gr + 2, 0, 6)
                    for t in range(TT):
                        qk_lo(TT + t)
                if gr == GPB + 2:
                    for f in range(4):
                        hidden(1, 0, f)
                maxima(gr + 2, 6 if gr == 1 else 0, EARLY)
                if gr == GPB + 1:
                    ln_lo(1, 0)
            for part in range(4):
                sparsify(0, 0, part)
            hidden(1, 0, 4)
            hidden(1, 0, 5)
            pv_out(NG - 1)
            hidden(1, 0, 6)
            normalise(NG - 1)
            hidden(1, 0, 7)
            for part in range(4):
                sparsify(0, 1, part)
            residual(0, 1)
            ln_stats(1, 1)
            residual(1, 0, (0,))
            ln_lo(1, 1)
            residual(1, 0, (1,))
            ln_stats(2, 0)
            ln_lo(2, 0)
            for k in range(KC):
                conv(0, k)
            sparsify(1, 0, 0)
            sparsify(1, 0, 1)
            sparsify(1, 0, 2)
            sparsify(1, 0, 3)
            softplus(0)
            for k in range(KC):
                mix(0, k)
            for part in range(4):
                sparsify(1, 1, part)
            residual(2, 0)
            ln_stats(3, 0)
            residual(1, 1, (0,))
            ln_lo(3, 0)
            residual(1, 1, (1,))
            ln_stats(2, 1)
            for f in range(3):
                hidden(3, 0, f)
            ln_lo(2, 1)
            hidden(3, 0, 3)
            for k in range(KC):
                conv(1, k)
            hidden(3, 0, 4)
            hidden(3, 0, 5)
            softplus(1)
            hidden(3, 0, 6)
            hidden(3, 0, 7)
            for k in range(KC):
                mix(1, k)
            residual(3, 0, (0,))
            residual(2, 1)
            ln_stats(3, 1)
            residual(3, 0, (1,))
            ln_lo(3, 1)
            for f in range(FC):
                hidden(3, 1, f)
            residual(3, 1)

        @block.tensor
        def _(pe):
            mm, tr = nc.tensor.matmul, nc.tensor.transpose

            def mm3(dst, a_hi, a_lo, b_hi, b_lo, first, last):
                mm(dst, a_hi, b_hi, start=first, stop=False)
                mm(dst, a_hi, b_lo, start=False, stop=False)
                return mm(dst, a_lo, b_hi, start=False, stop=last)

            def ln(n, b):
                pe.wait_ge(xn_done, NORMS.index((n, b)) + 1)
                if n == 0 and b == 0:
                    pe.wait_ge(ident_in, 16)
                for c in range(DC):
                    u = ("ln", n, b, c)
                    claim(pe, u)
                    for t in range(TT):
                        last = tr(ps(u)[:, P * t:P * t + P], xn[:, t, P * c:P * c + P], ident)
                    fill(last, u)

            def mod_T(l, half):
                pe.wait_ge(wmod_in[2 * l + half], 16)
                pe.wait_ge(silu_c_done, 1)
                u = ("modT", l, half)
                claim(pe, u)
                for kind in range(3):
                    for c in range(DC):
                        o, w = NB * (DC * kind + c), D * (3 * half + kind) + P * c
                        for kc in range(DC):
                            last = mm(ps(u)[:, o:o + NB], wmod_s[:, l, kc, w:w + P], silu_c[:, l, kc], start=kc == 0, stop=kc == DC - 1)
                fill(last, u)

            def gates_T(l):
                pe.wait_ge(g_cols_done, l + 1)
                for w in range(2):
                    u = ("gT", l, w)
                    claim(pe, u)
                    for b in range(NB):
                        for c in range(DC):
                            o = D * b + P * c
                            last = tr(ps(u)[:, o:o + P], g_cols[:, w, c, b], ident)
                    fill(last, u)

            def qkv(b, t):
                if t == 0:
                    pe.wait_ge(h_done, b + 1)
                    pe.wait_ge(wq_split, 1)
                for u, o, n in ((("qk", b, t), 0, 2 * D), (("v", b, t), 2 * D, D)):
                    claim(pe, u)
                    for c in range(DC):
                        ts = slice(P * t, P * t + P)
                        last = mm3(ps(u)[:, 0:n], h_hi[:, b, c, ts], h_lo[:, b, c, ts],
                                   wq_hi[:, c, o:o + n], wq_lo[:, c, o:o + n], c == 0, c == DC - 1)
                    fill(last, u)

            def heads(gr):
                b, g4 = gr // GPB, gr % GPB
                pe.wait_ge(qk_split, TT * (b + 1))
                if gr == 0:
                    pe.wait_ge(pool_consts, NCONST)
                for j in range(2):
                    for w, nm in enumerate(("qT", "kT")):
                        u = (nm, gr, j)
                        claim(pe, u)
                        for t in range(TT):
                            h0 = HPG * g4 + 2 * j
                            last = tr(ps(u)[:, P * t:P * t + P], qkp[:, t, w, h0:h0 + 2, :].rearrange("p h e -> p (h e)").bitcast(F32), ident)
                        fill(last, u)

            def score_max(gr, h, t):
                u = ("mx", gr, h, t)
                claim(pe, u)
                s = gr % 3
                if h % 2 == 0 and t == 0:
                    read(pe, ("qT", gr, h // 2))
                    read(pe, ("kT", gr, h // 2))
                fill(mm(ps(u)[:, 0:P * (t + 1)], QT[:, s, h // 2, P * t:P * t + P], KT[:, s, h // 2, h % 2, 0:P * (t + 1)],
                        start=True, stop=True), u)

            def max_T(gr):
                u = ("maxT", gr)
                read(pe, ("mx", gr, HPG - 1, TT - 1))
                claim(pe, u)
                for t in range(TT):
                    last = tr(ps(u)[0:HPG, P * t:P * t + P], mx[:, gr % 2, t], ident)
                fill(last, u)

            def scores(gr, s, i):
                u = ("st", gr, s, i)
                w = gr % 3
                claim(pe, u)
                if s == 0 and i == 0:
                    pe.wait_ge(shift_in[gr % 2], 32 * (gr // 2 + 1))
                parts = (((i, 0, 0),), ((i, 1, 0), (i, 3, 384)), ((2 * i, 2, 0), (2 * i + 1, 2, 256)))[s]
                for h, c, o in parts:
                    n = SEQ - P * c
                    last = mm(ps(u)[:, o:o + n], KT[:, w, h // 2, h % 2, P * c:P * c + P], QT[:, w, h // 2, P * c:SEQ],
                              start=True, stop=True)
                fill(last, u)

            def probs_v(gr, s):
                b = gr // GPB
                pe.wait_ge(causal_done, 10 * gr + (4, 8, 10)[s])
                if s == 0 and gr:
                    pe.wait_ge(pv_free, gr)
                for c in ((0,), (1, 3), (2,))[s]:
                    o = 384 if c == 3 else 0
                    n = SEQ - P * c
                    for h in range(HPG):
                        last = mm(pv_bank[32 * h:32 * h + 32, P * c:SEQ], vp[:, b, c, HPG * (gr % GPB) + h, :],
                                  PT[s][:, h, o:o + n], start=c == 0, stop=c == 2, tile_position=(0, 32 * h))
                last.then_inc(pv_done, 1)

            def out_T(gr):
                u = ("oN", gr)
                pe.wait_ge(pv_free, gr + 1)
                claim(pe, u)
                for t in range(TT):
                    last = tr(ps(u)[:, P * t:P * t + P], oT[:, P * t:P * t + P], ident)
                fill(last, u)

            def att_T(b):
                read(pe, ("oN", GPB * b + GPB - 1))
                for c in range(DC):
                    u = ("aT", b, c)
                    claim(pe, u)
                    for t in range(TT):
                        last = tr(ps(u)[:, P * t:P * t + P], att[:, t, P * c:P * c + P], ident)
                    fill(last, u)

            def down(n, b, i):
                if n == 0:
                    pe.wait_ge(wout_in, 16)
                    read(pe, ("aT", b, DC - 1))
                    srcs = [(aT[:, c], wout_s[:, c]) for c in range(DC)]
                elif n == 1:
                    pe.wait_ge(wdn_in, 16)
                    pe.wait_ge(sparse_done, GB * (b + 1))
                    srcs = [(H[b][:, f], wdn_s[:, f]) for f in range(FC)]
                elif n == 2:
                    pe.wait_ge(woutp_in, 16)
                    pe.wait_ge(comb_done, KC * (b + 1))
                    srcs = [(gt[b][:, k], woutp_s[:, k]) for k in range(KC)]
                else:
                    read(pe, ("had", FC // 2 - 1))
                    read(pe, ("up", 3, b, FC - 1))
                    srcs = [(H[b][:, f], w2a[:, f]) for f in range(FC)]
                u = ("y", n, b, i)
                claim(pe, u)
                for tt in range(2):
                    t = 2 * i + tt
                    for j, (act_t, w) in enumerate(srcs):
                        last = mm(ps(u)[:, D * tt:D * tt + D], act_t[:, P * t:P * t + P], w, start=j == 0, stop=j == len(srcs) - 1)
                fill(last, u)

            def gate_up(n, b, f):
                if f == 0:
                    pe.wait_ge(h_done, NORMS.index((n, b)) + 1)
                if f % 2 == 0 and b == 0:
                    pe.wait_ge(stage_split, (1 if n == 1 else 7) + f // 2)
                hi, lo = (gua_hi, gua_lo) if f < 4 else (gub_hi, gub_lo)
                for w, nm in enumerate(("gate", "up")):
                    u = (nm, n, b, f)
                    claim(pe, u)
                    for c in range(DC):
                        last = mm3(ps(u)[:], hi[:, f % 4, w, c], lo[:, f % 4, w, c], h_hi[:, b, c], h_lo[:, b, c], c == 0, c == DC - 1)
                    fill(last, u)

            def proj(b, k):
                if k == 0:
                    pe.wait_ge(h_done, NORMS.index((2, b)) + 1)
                if b == 0 and k % 2 == 0:
                    pe.wait_ge(stage_split, 5 + k // 2)
                for w, nm in enumerate(("pj", "gt")):
                    u = (nm, b, k)
                    claim(pe, u)
                    for c in range(DC):
                        last = mm3(ps(u)[:], pj_hi[:, k, w, c], pj_lo[:, k, w, c], h_hi[:, b, c], h_lo[:, b, c], c == 0, c == DC - 1)
                    fill(last, u)

            def dt(b):
                u = ("dt", b)
                claim(pe, u)
                pe.wait_ge(chan_in, 48)
                pe.wait_ge(xc_done, KC * (b + 1))
                for k in range(KC):
                    last = mm(ps(u)[0:SH], dtw_s[:, k], xc[b][:, k], start=k == 0, stop=k == KC - 1)
                fill(last, u)

            def spread(b):
                pe.wait_ge(dts_done, b + 1)
                pe.wait_ge(sel_done, 1)
                for k in range(KC):
                    u = ("spread", b, k)
                    claim(pe, u)
                    fill(mm(ps(u)[:], sel[:, k], dts[:], start=True, stop=True), u)

            def hadamard():
                pe.wait_ge(w2_mixed, 1)
                for i in range(FC // 2):
                    u = ("had", i)
                    claim(pe, u)
                    for c in range(2):
                        last = mm(ps(u)[:, D * c:D * c + D], had, w2b[:, 2 * i + c], start=True, stop=True)
                    fill(last, u)

            run = {"ln": ln, "modT": mod_T, "gT": gates_T, "qkv": qkv, "T": heads, "mx": score_max, "maxT": max_T, "st": scores, "pv": probs_v,
                   "oN": out_T, "aT": att_T, "y": down, "gu": gate_up, "proj": proj, "dt": dt, "spread": spread, "had": hadamard}
            for s in stages:
                run[s[0]](*s[1:])


def shape_constants():
    c = np.zeros((P, C_END), np.float32)
    c[:, C_ID:C_HAD] = np.eye(P, dtype=np.float32)
    i = np.arange(P)
    par = np.array([[bin(a & b).count("1") & 1 for b in i] for a in i])
    c[:, C_HAD:C_MASK] = 1 - 2 * par
    tri = np.where(i[None, :] > i[:, None], NEG, 0.0)
    c[:, C_COS - P:C_COS] = tri
    inv = (1.0 / 10000.0 ** (np.arange(0, HD, 2, dtype=np.float32) / HD)).astype(np.float32)
    fr = np.arange(SEQ, dtype=np.float32)[:, None] * inv[None, :]
    emb = np.concatenate([fr, fr], -1)
    for o, f in ((C_COS, np.cos), (C_SIN, np.sin)):
        c[:, o:o + TT * HD] = f(emb).reshape(TT, P, HD).transpose(1, 0, 2).reshape(P, TT * HD)
    return c


def spreading():
    c = np.zeros((P, KC, P), np.float32)
    for k in range(KC):
        for m in range(P):
            h = (P * k + m) // SHD
            c[h, k, m] = c[32 + h, k, m] = 1
    return c


def kernel(**inputs):
    import concourse.bacc as _bacc
    from concourse.bass_utils import run_bass_kernel_spmd as _run

    w = {k: np.asarray(v) for k, v in inputs.items()}

    def rows(a):
        return a.reshape(-1, P, a.shape[-1]).transpose(1, 0, 2)

    def pair_up(a, b):
        both = np.stack([a, b]).reshape(2, DC, P, -1, P)
        return both.transpose(2, 3, 0, 1, 4)

    order = np.arange(HID).reshape(GB, P, 4).transpose(0, 2, 1).reshape(-1)
    chan = np.concatenate([w["L1_attn_conv_weight"]] + [w["L1_attn_" + n].reshape(INNER, 1)
                          for n in ("conv_bias", "A_log", "B", "C", "D")], axis=1)
    dtw = np.zeros((INNER, SH), np.float32)
    for h in range(SH):
        dtw[SHD * h:SHD * (h + 1), h] = w["L1_attn_dt_w"][h]
    arrays = {
        "x": w["L0_attn_x"].reshape(NB * SEQ, D),
        "wqkv": rows(w["L0_attn_w_qkv"]),
        "wout": rows(w["L0_attn_w_out"]),
        "gammas": np.tile(np.stack([w["L0_attn_q_gamma"], w["L0_attn_k_gamma"]])[None], (P, 1, 1)),
        "wgu0": pair_up(w["L0_ffn_w_gate"][:, order], w["L0_ffn_w_up"][:, order]),
        "wdn0": rows(w["L0_ffn_w_down"][order]),
        "wmod": np.stack([rows(w["L0_wmod"]), rows(w["L1_wmod"])], axis=1),
        "cT": np.stack([rows(w["L0_c"].T), rows(w["L1_c"].T)], axis=1),
        "wproj": pair_up(w["L1_attn_in_proj_w"].T, w["L1_attn_gate_proj_w"].T),
        "woutp": rows(w["L1_attn_out_proj_w"].T),
        "chan": rows(chan),
        "dtw": rows(dtw),
        "dtb": w["L1_attn_dt_b"].reshape(SH, 1),
        "wgu1": pair_up(w["L1_ffn_W1"].T, w["L1_ffn_W3"].T),
        "w2t": rows(w["L1_ffn_W2"].T),
        "consts": shape_constants(),
        "spread_sel": spreading(),
    }
    arrays = {f"in_{k}": np.ascontiguousarray(v) for k, v in arrays.items()}
    nc = _bacc.Bacc("TRN2", target_bir_lowering=False, num_devices=1)
    args = [nc.dram_tensor(k, v.shape, mybir.dt.from_np(v.dtype), kind="ExternalInput").ap() for k, v in arrays.items()]
    out = nc.dram_tensor("out_0", (NB * SEQ, D), F32, kind="ExternalOutput").ap()
    adaln_blocks(nc, *args, out)
    r = _run(nc, [arrays], core_ids=[0])
    return r.results[0]["out_0"].reshape(NB, SEQ, D)
```
